# Optimizing a Trainium2 kernel written in Bass

```python
import numpy as np
import jax
import jax.numpy as jnp

def _softmax(x, axis=-1):
    return jax.nn.softmax(x, axis=axis)

def _gelu(x):
    return jax.nn.gelu(x, approximate=True)

def _silu(x):
    return jax.nn.silu(x)

def _sigmoid(x):
    return jax.nn.sigmoid(x)

def _layernorm(x, axis=-1, eps=1e-05):
    m = jnp.mean(x, axis=axis, keepdims=True)
    v = jnp.var(x, axis=axis, keepdims=True)
    return (x - m) / jnp.sqrt(v + eps)

def _scatter_add(tgt, idx, src, axis=0):
    return tgt.at[idx].add(src)

def _segment_sum(src, seg, n):
    return jax.ops.segment_sum(src, seg, n)
kernel_name = 'mk_gnn_ffn_d1_gnn_r32_d0d9a0'

def setup_inputs(seed: int=0):
    np.random.seed(seed)
    _w = jnp.asarray

    def _rec_inputs():
        import jax
        import jax.numpy as jnp
        _gk = jax.random.key(seed)
        x = -0.0003713 + 1 * jax.random.normal(jax.random.fold_in(_gk, 1), (3125, 256), jnp.float32)
        _s = jax.random.randint(jax.random.fold_in(_gk, 2), (25000,), 0, 3125, jnp.int32)
        _d = jax.random.randint(jax.random.fold_in(_gk, 3), (25000,), 0, 3125, jnp.int32)
        _loop = jnp.arange(3125, dtype=jnp.int32)
        src = jnp.concatenate([_s, _d, _loop])
        dst = jnp.concatenate([_d, _s, _loop])
        _o = jnp.argsort(dst, stable=True)
        src = src[_o]
        dst = dst[_o]
        edge_weight1 = 0.000937891 + 0.999965 * jax.random.normal(jax.random.fold_in(_gk, 12), (53125, 1), jnp.float32)
        return (x, src, dst, edge_weight1)
    x, src, dst, edge_weight1 = _rec_inputs()

    def _L0_gnn_setup():
        import jax, jax.numpy as jnp
        import numpy as np
        N_NODES = 50000
        N_EDGES = 25000
        D_IN = 256
        D_OUT = 256
        key = jax.random.key(seed)
        ks = jax.random.split(key, 8)
        feat = jax.random.normal(ks[0], (N_NODES, D_IN), dtype=jnp.float32)
        weight = jax.random.normal(ks[1], (N_EDGES, 1), dtype=jnp.float32)
        src = jax.random.randint(ks[2], (N_EDGES,), 0, N_NODES, dtype=jnp.int32)
        dst = jax.random.randint(ks[3], (N_EDGES,), 0, N_NODES, dtype=jnp.int32)
        W_pool = jax.random.normal(ks[4], (D_IN, D_IN), dtype=jnp.float32) * 0.05
        b_pool = jnp.zeros((D_IN,), dtype=jnp.float32)
        W_self = jax.random.normal(ks[5], (D_OUT, D_IN), dtype=jnp.float32) * 0.05
        b_self = jnp.zeros((D_OUT,), dtype=jnp.float32)
        W_neigh = jax.random.normal(ks[6], (D_OUT, D_IN), dtype=jnp.float32) * 0.05
        b_neigh = jnp.zeros((D_OUT,), dtype=jnp.float32)
        return {'feat': feat, 'weight': weight, 'src': src, 'dst': dst, 'W_pool': W_pool, 'b_pool': b_pool, 'W_self': W_self, 'b_self': b_self, 'W_neigh': W_neigh, 'b_neigh': b_neigh}
    _L0_gnn_all = _L0_gnn_setup()
    _L0_gnn_in = {k: v for k, v in _L0_gnn_all.items() if k in ('W_pool', 'b_pool', 'W_self', 'b_self', 'W_neigh', 'b_neigh')}
    del _L0_gnn_all

    def _L0_ffn_setup():
        import jax, jax.numpy as jnp
        import numpy as np
        TOP_K = 2
        key = jax.random.key(seed)
        ks = jax.random.split(key, 4)
        B, L, D, H, E = (8, 128, 256, 1024, 8)
        s = 0.02
        return {'x': jax.random.normal(ks[0], (B, L, D), jnp.float32), 'Wg': jax.random.normal(ks[1], (D, E), jnp.float32) * s, 'bg': jnp.zeros((E,), jnp.float32), 'W1': jax.random.normal(ks[2], (E, D, H), jnp.float32) * s, 'b1': jnp.zeros((E, H), jnp.float32), 'W2': jax.random.normal(ks[3], (E, H, D), jnp.float32) * s, 'b2': jnp.zeros((E, D), jnp.float32)}
    _L0_ffn_all = _L0_ffn_setup()
    _L0_ffn_in = {k: v for k, v in _L0_ffn_all.items() if k in ('Wg', 'bg', 'W1', 'b1', 'W2', 'b2')}
    del _L0_ffn_all
    return {'x': x, 'src': src, 'dst': dst, 'edge_weight1': edge_weight1, 'L0_gnn_W_pool': _L0_gnn_in['W_pool'], 'L0_gnn_b_pool': _L0_gnn_in['b_pool'], 'L0_gnn_W_self': _L0_gnn_in['W_self'], 'L0_gnn_b_self': _L0_gnn_in['b_self'], 'L0_gnn_W_neigh': _L0_gnn_in['W_neigh'], 'L0_gnn_b_neigh': _L0_gnn_in['b_neigh'], 'L0_ffn_Wg': _L0_ffn_in['Wg'], 'L0_ffn_bg': _L0_ffn_in['bg'], 'L0_ffn_W1': _L0_ffn_in['W1'], 'L0_ffn_b1': _L0_ffn_in['b1'], 'L0_ffn_W2': _L0_ffn_in['W2'], 'L0_ffn_b2': _L0_ffn_in['b2']}

def reference(x, src, dst, edge_weight1, L0_gnn_W_pool, L0_gnn_b_pool, L0_gnn_W_self, L0_gnn_b_self, L0_gnn_W_neigh, L0_gnn_b_neigh, L0_ffn_Wg, L0_ffn_bg, L0_ffn_W1, L0_ffn_b1, L0_ffn_W2, L0_ffn_b2):
    import jax
    import jax.numpy as jnp

    def _L0_gnn_ref(feat, weight, src, dst, W_pool, b_pool, W_self, b_self, W_neigh, b_neigh):
        import jax, jax.numpy as jnp
        import numpy as np
        N_NODES = 50000
        N_EDGES = 25000
        D_IN = 256
        D_OUT = 256
        n = feat.shape[0]
        h = jax.nn.relu(feat @ W_pool.T + b_pool)
        m = h[src] * weight
        neigh = jax.ops.segment_max(m, dst, num_segments=n)
        deg = jax.ops.segment_sum(jnp.ones((src.shape[0],), feat.dtype), dst, num_segments=n)
        neigh = jnp.where((deg > 0)[:, None], neigh, jnp.zeros((), feat.dtype))
        return feat @ W_self.T + b_self + (neigh @ W_neigh.T + b_neigh)

    def _L0_ffn_ref(x, Wg, bg, W1, b1, W2, b2):
        import jax, jax.numpy as jnp
        import numpy as np
        TOP_K = 2
        B, L, D = x.shape
        E = W1.shape[0]
        xf = x.reshape(-1, D)
        gate_logits = xf @ Wg + bg
        top_w, top_i = jax.lax.top_k(gate_logits, TOP_K)
        top_w = jax.nn.softmax(top_w, axis=-1)
        w_dense = jnp.sum(jax.nn.one_hot(top_i, E, dtype=xf.dtype) * top_w[..., None], axis=1)
        out = jnp.zeros_like(xf)
        for e in range(E):
            h = jax.nn.gelu(xf @ W1[e] + b1[e], approximate=False)
            out = out + w_dense[:, e:e + 1] * (h @ W2[e] + b2[e])
        return out.reshape(B, L, D)
    x = x + _L0_gnn_ref(_layernorm(x, axis=-1), edge_weight1, src, dst, L0_gnn_W_pool, L0_gnn_b_pool, L0_gnn_W_self, L0_gnn_b_self, L0_gnn_W_neigh, L0_gnn_b_neigh)
    x = x + _L0_ffn_ref(_layernorm(x, axis=-1)[None], L0_ffn_Wg, L0_ffn_bg, L0_ffn_W1, L0_ffn_b1, L0_ffn_W2, L0_ffn_b2)[0]
    return x

_drawn_inputs = setup_inputs


def setup_inputs(seed=0):
    import zlib

    import numpy as np

    out = dict(_drawn_inputs(seed))
    spreads = {'L0_gnn_b_pool': (0.0, 0.1),
     'L0_gnn_b_self': (0.0, 0.1),
     'L0_gnn_b_neigh': (0.0, 0.1),
     'L0_ffn_bg': (0.0, 0.272),
     'L0_ffn_b1': (0.0, 0.527),
     'L0_ffn_b2': (0.0, 0.1)}
    factors = {}
    for name, (base, spread) in spreads.items():
        noise = np.random.default_rng([zlib.crc32(name.encode()), seed]).standard_normal(out[name].shape)
        drawn = base * np.exp(spread * noise) if base else spread * noise
        out[name] = jnp.asarray(drawn.astype(out[name].dtype))
    for name, factor in factors.items():
        out[name] = (out[name] * factor).astype(out[name].dtype)
    return out
```

```python
import concourse.bass as bass
from concourse import mybir
from contextlib import ExitStack

F32 = mybir.dt.float32
BF16 = mybir.dt.bfloat16
I32 = mybir.dt.int32
U32 = mybir.dt.uint32
ALU = mybir.AluOpType
ACT = mybir.ActivationFunctionType
AX = mybir.AxisListType

P = 128
N, D = 3125, 256
KD = D // P
NT = -(-N // P)
TAIL = N - (NT - 1) * P
E = 53125
COLS = 416
ETAIL = E - (P - 1) * COLS
G = 16
GROUPS = COLS // G
NEXP, HID = 8, 1024
KH = HID // P
CAP = NT * P
MOE_TILES = (2 * N + NEXP * (P - 1)) // P
TABLE = (NEXP * NT + MOE_TILES) * P
EPS = 1e-5
NEG = -3.0e38
NOWHERE = 1.0e6
PAD_DST = 8191
CREDIT = 2


def gnn_moe(nc, x, src, dst, ew, Wp, bp, Ws, bs, Wn, bn, Wg, bg, W1, b1, W2, b2, out):
    ctx = ExitStack()
    with ctx:
        def sb(name, shape, dt=F32):
            return ctx.enter_context(nc.sbuf_tensor(name, shape, dt))

        def sem(name):
            return ctx.enter_context(nc.semaphore(name))

        def sems(name, n):
            return [sem(f"{name}{i}") for i in range(n)]

        h_dram = nc.dram_tensor("h_rows", (NT * P, D), F32).ap()
        run_dram = nc.dram_tensor("running_max", (P * COLS, D), F32).ap()
        x2_dram = nc.dram_tensor("ffn_in", (NT * P, D), F32).ap()
        table = nc.dram_tensor("queues", (TABLE, 2), F32).ap()

        W1_AT, B1_AT = 0, NEXP * KD * HID
        B2_AT = B1_AT + NEXP * HID
        W2_AT = B2_AT + NEXP * D
        ARENA = W2_AT + NEXP * KH * D
        arena = sb("arena", [P, ARENA])
        at = [0]

        def carve(shape, dt=F32):
            n = 1
            for s in shape:
                n *= s
            words = n if dt != BF16 else n // 2
            v = arena[:, at[0]:at[0] + words]
            at[0] += words
            if dt != F32:
                v = v.bitcast(dt)
            if len(shape) == 2:
                v = v.rearrange("p (a b) -> p a b", b=shape[1])
            elif len(shape) == 3:
                v = v.rearrange("p (a b c) -> p a b c", b=shape[1], c=shape[2])
            return v

        gath = carve([G, D])
        run = carve([2, G, D])
        oh_lo = carve([G, P], BF16)
        oh_hi = carve([G, 32], BF16)
        src_i = carve([COLS], I32)
        dst_i = carve([COLS], I32)
        part_i = carve([COLS], I32)
        dst_f = carve([COLS])
        lo_f = carve([COLS])
        hi_f = carve([COLS])
        w_e = carve([COLS])
        flag = carve([COLS])
        w_nat = carve([3, KD, D])
        wpT = carve([KD, D])
        wsT = carve([KD, D])
        bp_b = carve([D])
        bsn_b = carve([2, D])
        hs = carve([2, D])
        hr = carve([2, D])
        idxg = carve([2, G], I32)
        firstlast = carve([2, P])
        fl_b = carve([2, P])
        newseg = carve([P])
        scanflag = carve([P])
        stT = carve([KD, P])
        carT = carve([KD, P])
        first_row = carve([COLS])
        fix_i = carve([1], I32)
        fix_f = carve([4])
        vrow = carve([D])
        vfix = carve([D])
        assert at[0] <= W2_AT

        LATE = 3
        at[0] = ARENA - LATE * KH * D
        xn = carve([2, D])
        xT = carve([2, KD, P])
        ng = carve([2, D])
        ngm = carve([2, D])
        oh1 = carve([NT, NEXP])
        oh2 = carve([NT, NEXP])
        member = carve([NT, NEXP])
        pos = carve([NT, NEXP])
        tot = carve([NEXP, NT])
        cum = carve([NEXP, NT])
        prod = carve([2, NT, NEXP])
        vals = carve([NT, 2])
        ids = carve([NT, 2])
        slot_f = carve([NT, 2])
        slot_i = carve([NT, 2], I32)
        entry = carve([NT, 2, 2])
        sl_i = carve([2, 2], I32)
        en_s = carve([2, 2, 2])
        m_cmp = carve([MOE_TILES, NEXP])
        m_mul = carve([MOE_TILES, NEXP])
        assert at[0] <= ARENA

        xs = sb("xs", [P, NT + 1, D])
        wnT = sb("wnT", [P, KD, D])
        wg_s = sb("wg_s", [P, KD, NEXP])
        bg_b = sb("bg_b", [P, NEXP])
        ident = sb("ident", [P, P])
        ones = sb("ones", [P, P])
        tri_lt = sb("tri_lt", [P, P])
        tri_le = sb("tri_le", [P, P])
        iota_r = sb("iota_r", [P, P])
        tok_f = sb("tok_f", [P, NT])
        valid = sb("valid", [P, NT])
        pcol = sb("pcol", [P, 1])
        eps = sb("eps", [P, 1])
        st = sb("st", [P, NT + 1, 6])
        mean = sb("mean", [P, NT + 1])
        var = sb("var", [P, NT + 1])
        rstd = sb("rstd", [P, NT + 1])
        tmp = sb("tmp", [P, NT + 1])
        deg = sb("deg", [P, NT])
        dmask = sb("dmask", [P, NT])
        dcum = sb("dcum", [P, NT])
        end_f = sb("end_f", [P, NT])
        end_i = sb("end_i", [P, NT], I32)
        ei = sb("ei", [P, 2], I32)
        lg = sb("lg", [P, 2, NEXP])
        mx = sb("mx", [P, 2, NEXP])
        mi = sb("mi", [P, 2, NEXP], U32)
        sent = sb("sent", [P, P])
        zrow = sb("zrow", [P, 32])
        tl = sb("tl", [1, 4, NEXP])
        tl_i = sb("tl_i", [1, NEXP], I32)
        tab_f = sb("tab_f", [1, 3, MOE_TILES])
        e_tab = sb("e_tab", [1, MOE_TILES], I32)
        r_tab = sb("r_tab", [1, MOE_TILES], I32)

        ps = ctx.enter_context(nc.psum_tensor("ps", [P, 8, 512], F32))

        s_memx, s_eps, s_prep = sem("x_tail_zeroed"), sem("eps_set"), sem("edge_pads_set")
        s_const = sem("constants_made")
        s_memc = sem("constants_filled")
        s_st = sem("statistics_taken")
        s_x = sems("x_loaded", 5)
        s_ld = sem("small_inputs_loaded")
        s_edge = sem("edges_loaded")
        s_sent = sem("queues_cleared")
        s_sentm = sem("sentinels_set")
        s_wps, s_wT = sem("weights_transposed"), sem("weights_out_of_psum")
        s_var, s_std, s_rstd = sem("variances_ready"), sem("deviations_ready"), sem("rstd_ready")
        s_xn, s_tps, s_xT = sem("xn_ready"), sem("xn_transposed"), sem("xT_ready")
        s_y, s_hs, s_hr = sem("h_product"), sem("h_biased"), sem("h_ready")
        s_hst = sems("h_stored", 2)
        s_dv = sem("vector_chain")
        dv = [0]

        def linker(eng, base=None, s=s_dv, count=dv):
            def link(ins):
                count[0] += 1
                ins.then_inc(s, 1)
                eng.wait_ge(s, count[0] if base is None else base + count[0])
            return link

        s_past = sem("waits_passed")

        def settle(eng):
            eng.sem_inc(s_past, 1)

        def turns(eng, count):
            yield 0
            with eng.Fori(1, count) as it:
                yield it

        CHUNK = NT // 5
        x_v = x[0:(NT - 1) * P, :].rearrange("(t p) d -> p t d", p=P)
        h_v = h_dram.rearrange("(t p) d -> p t d", p=P)
        x2_v = x2_dram.rearrange("(t p) d -> p t d", p=P)
        TABLE_W = TABLE * 2 // P

        def moments(dve, link, nt):
            link(dve.tensor_tensor(tmp[:, 0:nt], st[:, 0:nt, 1], st[:, 0:nt, 4], ALU.subtract))
            link(dve.tensor_tensor(mean[:, 0:nt], st[:, 0:nt, 1], st[:, 0:nt, 4], ALU.add))
            link(dve.tensor_scalar(mean[:, 0:nt], mean[:, 0:nt], 0.5, None, ALU.mult))
            link(dve.tensor_tensor(var[:, 0:nt], st[:, 0:nt, 2], st[:, 0:nt, 5], ALU.add))
            link(dve.tensor_tensor(tmp[:, 0:nt], tmp[:, 0:nt], tmp[:, 0:nt], ALU.mult))
            link(dve.tensor_scalar(tmp[:, 0:nt], tmp[:, 0:nt], 0.25, None, ALU.mult))
            dve.scalar_tensor_tensor(out=var[:, 0:nt], in0=var[:, 0:nt], scalar=1.0 / D,
                                     in1=tmp[:, 0:nt], op0=ALU.mult, op1=ALU.add).then_inc(s_var, 1)

        def col(t, n):
            return t[:, bass.ds(n, 1)]

        def tile_of(t, n):
            return t[:, bass.ds(n, 1), :].rearrange("p a d -> p (a d)")

        with nc.Block() as block:
            @block.sync
            def _(sp):
                def load(dst_ap, src_ap, s):
                    sp.dma_start(dst_ap, src_ap).then_inc(s, 16)
                for c in range(4):
                    load(xs[:, c * CHUNK:(c + 1) * CHUNK, :], x_v[:, c * CHUNK:(c + 1) * CHUNK, :], s_x[c])
                sp.wait_ge(s_memx, 1)
                load(xs[:, 4 * CHUNK:NT - 1, :], x_v[:, 4 * CHUNK:NT - 1, :], s_x[4])
                load(xs[0:TAIL, NT - 1, :], x[(NT - 1) * P:N, :], s_x[4])
                sp.wait_ge(s_prep, 3)
                for t, a in ((src_i, src.rearrange("(p c) -> p c", c=1)),
                             (dst_i, dst.rearrange("(p c) -> p c", c=1)), (w_e, ew)):
                    load(t[0:P - 1, :], a[0:(P - 1) * COLS, :].rearrange("(p c) o -> p (c o)", c=COLS), s_edge)
                    load(t[P - 1:P, 0:ETAIL], a[(P - 1) * COLS:E, :].rearrange("(p c) o -> p (c o)", c=ETAIL), s_edge)
                sp.wait_ge(s_sentm, 1)
                for c in range(TABLE_W // P):
                    load(table.rearrange("(p c) w -> p (c w)", p=P)[:, c * P:(c + 1) * P], sent[:, :], s_sent)

                def store(n, q):
                    sp.wait_ge(s_hr, n + 1 + CREDIT)
                    sp.dma_start(tile_of(h_v, n), hr[:, q, :]).then_inc(s_hst[q], 16)
                with sp.Fori(0, NT // 2) as it:
                    for q in range(2):
                        store(it * 2 + q, q)
                store(NT - 1, 0)
                sp.wait_ge(s_hst[0], 16 * (NT // 2 + 1))
                sp.wait_ge(s_hst[1], 16 * (NT // 2))
                sp.wait_ge(s_sent, 16 * (TABLE_W // P))
                sp.wait_ge(s_edge, 16 * 6)

            @block.gpsimd
            def _(pool):
                pool.memset(src_i[:, :], 0).then_inc(s_prep, 1)
                pool.memset(dst_i[:, :], PAD_DST).then_inc(s_prep, 1)
                pool.memset(w_e[:, :], 0.0).then_inc(s_prep, 1)
                pool.memset(ident[:, :], 0.0).then_inc(s_memc, 1)
                pool.memset(ones[:, :], 1.0).then_inc(s_memc, 1)
                pool.memset(tri_lt[:, :], 1.0).then_inc(s_memc, 1)
                pool.memset(tri_le[:, :], 1.0).then_inc(s_memc, 1)
                pool.memset(valid[:, :], 1.0).then_inc(s_memc, 1)
                pool.memset(sent[:, :], NOWHERE).then_inc(s_sentm, 1)
                pool.wait_ge(s_memc, 5)
                pool.affine_select(out=ident[:, :], in_=ident[:, :], compare_op=ALU.not_equal, fill=1.0,
                                   base=0, pattern=[[-1, P]], channel_multiplier=1).then_inc(s_const, 1)
                pool.affine_select(out=tri_lt[:, :], in_=tri_lt[:, :], compare_op=ALU.is_gt, fill=0.0,
                                   base=0, pattern=[[1, P]], channel_multiplier=-1).then_inc(s_const, 1)
                pool.affine_select(out=tri_le[:, :], in_=tri_le[:, :], compare_op=ALU.is_ge, fill=0.0,
                                   base=0, pattern=[[1, P]], channel_multiplier=-1).then_inc(s_const, 1)
                pool.affine_select(out=valid[:, :], in_=valid[:, :], compare_op=ALU.is_ge, fill=0.0,
                                   base=N - 1, pattern=[[-P, NT]], channel_multiplier=-1).then_inc(s_const, 1)
                pool.iota(iota_r[:, :], [[1, P]], base=0, channel_multiplier=0,
                          allow_small_or_imprecise_dtypes=True).then_inc(s_const, 1)
                pool.iota(tok_f[:, :], [[P, NT]], base=0, channel_multiplier=1,
                          allow_small_or_imprecise_dtypes=True).then_inc(s_const, 1)
                pool.iota(pcol[:, :], [[0, 1]], base=-1, channel_multiplier=COLS,
                          allow_small_or_imprecise_dtypes=True).then_inc(s_const, 1)

            @block.vector
            def _(dve):
                dve.memset(xs[:, NT - 1:NT + 1, :], 0.0).then_inc(s_memx, 1)
                dve.memset(zrow[:, :], 0.0).then_inc(s_eps, 1)
                dve.memset(eps[:, :], EPS).then_inc(s_eps, 1)
                dve.sem_inc(s_xn, CREDIT)
                dve.sem_inc(s_hs, CREDIT)
                link = linker(dve)
                for c in range(5):
                    dve.wait_ge(s_x[c], 16 if c < 4 else 32)
                    for t in range(c * CHUNK, (c + 1) * CHUNK):
                        dve.bn_stats(st[:, t, :], xs[:, t, :]).then_inc(s_st, 1)
                dve.wait_ge(s_memx, 1)
                dve.bn_stats(st[:, NT, :], xs[:, NT, :]).then_inc(s_st, 1)
                dve.wait_ge(s_st, NT + 1)
                moments(dve, link, NT + 1)
                dve.wait_ge(s_std, 1)
                dve.reciprocal(rstd[:, :], rstd[:, :]).then_inc(s_rstd, 1)
                dve.wait_ge(s_rstd, 1)

                def norm(n, q):
                    dve.wait_ge(s_tps, n - 1 + CREDIT)
                    dve.tensor_scalar(xn[:, q, :], tile_of(xs, n), col(mean, n), col(rstd, n),
                                      ALU.subtract, ALU.mult).then_inc(s_xn, 1)

                def bias(n, q):
                    dve.wait_ge(s_y, n + 1 + CREDIT)
                    dve.wait_ge(s_hr, n - 1 + CREDIT)
                    dve.tensor_tensor(hs[:, q, :], ps[:, 4 + q, 0:D], bp_b[:, :], ALU.add).then_inc(s_hs, 1)
                norm(0, 0)
                dve.wait_ge(s_ld, 16 * 8)
                with dve.Fori(0, NT // 2) as it:
                    for q in range(2):
                        norm(it * 2 + q + 1, 1 - q)
                        bias(it * 2 + q, q)
                bias(NT - 1, 0)

            @block.scalar
            def _(act):
                def load(dst_ap, src_ap):
                    act.dma_start(dst_ap, src_ap).then_inc(s_ld, 16)
                for i, w in enumerate((Wp, Ws, Wn)):
                    load(w_nat[:, i, :, :], w.rearrange("(c p) k -> p c k", p=P))
                load(bp_b[:, :], bp.partition_broadcast(P))
                load(bsn_b[:, 0, :], bs.partition_broadcast(P))
                load(bsn_b[:, 1, :], bn.partition_broadcast(P))
                load(wg_s[:, :, :], Wg.rearrange("(c p) k -> p c k", p=P))
                load(bg_b[:, :], bg.partition_broadcast(P))
                act.sem_inc(s_xT, CREDIT)
                act.sem_inc(s_hr, CREDIT)
                for i, wT in enumerate((wpT, wsT, wnT[:, :, :])):
                    act.wait_ge(s_wps, i + 1)
                    act.activation(wT.rearrange("p b o -> p (b o)"), ps[:, i, :], ACT.Copy).then_inc(s_wT, 1)
                act.wait_ge(s_var, 1)
                act.wait_ge(s_eps, 2)
                act.activation(rstd[:, :], var[:, :], ACT.Sqrt, bias=eps[:, 0:1]).then_inc(s_std, 1)

                def evac(n, q):
                    act.wait_ge(s_tps, n + 1 + CREDIT)
                    act.wait_ge(s_y, n - 1 + CREDIT)
                    act.activation(xT[:, q, :, :].rearrange("p c t -> p (c t)"), ps[:, 6 + q, 0:D],
                                   ACT.Copy).then_inc(s_xT, 1)

                def relu(it, n, q):
                    act.wait_ge(s_hs, n + 1 + CREDIT)
                    act.wait_ge(s_hst[q], 16 * it)
                    act.activation(hr[:, q, :], hs[:, q, :], ACT.Relu).then_inc(s_hr, 1)
                evac(0, 0)
                for it in turns(act, NT // 2):
                    for q in range(2):
                        evac(it * 2 + q + 1, 1 - q)
                        relu(it, it * 2 + q, q)
                relu(NT // 2, NT - 1, 0)

            @block.tensor
            def _(pe):
                pe.sem_inc(s_tps, CREDIT)
                pe.sem_inc(s_y, CREDIT)
                pe.wait_ge(s_ld, 16 * 8)
                pe.wait_ge(s_const, 7)
                for i in range(3):
                    for b in range(KD):
                        for a in range(KD):
                            last = pe.transpose(ps[:, i, b * D + a * P:b * D + (a + 1) * P],
                                                w_nat[:, i, a, b * P:(b + 1) * P], ident[:, :])
                    last.then_inc(s_wps, 1)
                pe.wait_ge(s_wT, 1)

                def turn(n, q):
                    pe.wait_ge(s_xn, n + 1 + CREDIT)
                    pe.wait_ge(s_xT, n - 1 + CREDIT)
                    for c in range(KD):
                        last = pe.transpose(ps[:, 6 + q, c * P:(c + 1) * P], xn[:, q, c * P:(c + 1) * P],
                                            ident[:, :])
                    last.then_inc(s_tps, 1)

                def product(n, q):
                    pe.wait_ge(s_xT, n + 1 + CREDIT)
                    pe.wait_ge(s_hs, n - 1 + CREDIT)
                    for c in range(KD):
                        last = pe.matmul(ps[:, 4 + q, 0:D], xT[:, q, c, :], wpT[:, c, :],
                                         start=(c == 0), stop=(c == KD - 1))
                    last.then_inc(s_y, 1)
                turn(0, 0)
                with pe.Fori(0, NT // 2) as it:
                    for q in range(2):
                        turn(it * 2 + q + 1, 1 - q)
                        product(it * 2 + q, q)
                product(NT - 1, 0)
        s_ep, s_idx = sem("edge_arrays_ready"), sem("group_indices_ready")
        s_gat = sems("rows_gathered", G)
        s_scaled = sem("row_scaled")
        s_fold = sem("running_max_ready")
        s_rst = sems("group_stored", 2)
        s_oh, s_cnt = sem("one_hots_ready"), sem("group_counted")
        s_bxn, s_btp, s_bxT, s_by, s_bx = (sem("base_xn"), sem("base_transposed"), sem("base_xT"),
                                           sem("base_product"), sem("base_ready"))
        s_q, s_q2, s_cb = sem("edges_vector_chain"), sem("base_vector_chain"), sem("counts_cleared")
        s_dg, s_flp, s_ct, s_unused, s_cs, s_cc, s_cr = (
            sem("diagonals_ready"), sem("first_last_on_rows"), sem("carries_transposed"), sem("unused_a"),
            sem("carries_scanned"), sem("carries_back"), sem("joined_rows_ready"))
        s_v, s_js, s_fixi = sem("first_ends_gathered"), sem("joined_rows_stored"), sem("first_end_index")
        s_dgr, s_dsum = sem("degrees_ready"), sem("degree_sums_ready")
        qn, qb = [0], [0]
        run_v = run_dram.rearrange("(p t) d -> p t d", t=COLS)
        IOTA_B = iota_r[:, :].unsqueeze(1).to_broadcast([P, G, P])
        IOTA_H = iota_r[:, 0:32].unsqueeze(1).to_broadcast([P, G, 32])

        with nc.Block() as block:
            @block.sync
            def _(sp):
                with sp.Fori(0, GROUPS // 2) as it:
                    for k in range(2):
                        g = it * 2 + k
                        sp.wait_ge(s_fold, g * G + 2 * G)
                        sp.dma_start(run_v[:, bass.ds(g * G, G), :], run[:, k, :, :]).then_inc(s_rst[k], 16)
                for k in range(2):
                    sp.wait_ge(s_rst[k], 16 * (GROUPS // 2))

            @block.gpsimd
            def _(pool):
                last_h, last_run = pool.to_reg(NT * P - 1), pool.to_reg(P * COLS - 1)
                with pool.Fori(0, GROUPS // 2) as it:
                    for k in range(2):
                        g = it * 2 + k
                        pool.tensor_copy(idxg[:, k, :], src_i[:, bass.ds(g * G, G)]).then_inc(s_idx, 1)
                        pool.wait_ge(s_idx, g + 1)
                        for s in range(G):
                            pool.wait_ge(s_scaled, g * G + s + 1)
                            settle(pool)
                            pool.indirect_dma_start(gath[:, s, :], None, h_dram,
                                                    bass.IndirectOffsetOnAxis(idxg[:, k, s:s + 1], 0),
                                                    bounds_check=last_h, oob_is_err=False)\
                                .then_inc(s_gat[s], 16)
                for k in range(2):
                    pool.wait_ge(s_rst[k], 16 * (GROUPS // 2))
                pool.wait_ge(s_fixi, 1)
                pool.indirect_dma_start(vrow[:, :], None, run_dram, bass.IndirectOffsetOnAxis(fix_i[:, 0:1], 0),
                                        bounds_check=last_run, oob_is_err=False).then_inc(s_v, 16)
                pool.wait_ge(s_cr, 1)
                pool.indirect_dma_start(run_dram, bass.IndirectOffsetOnAxis(fix_i[:, 0:1], 0), vfix[:, :], None,
                                        bounds_check=last_run, oob_is_err=False).then_inc(s_js, 16)
                pool.wait_ge(s_js, 16)

            @block.scalar
            def _(act):
                act.sem_inc(s_scaled, G)
                act.wait_ge(s_ep, 1)
                for it in turns(act, GROUPS // 2):
                    for k in range(2):
                        g = it * 2 + k
                        act.wait_ge(s_rst[k], it * 16)
                        act.wait_ge(s_fold, g * G + 1)
                        for s in range(G):
                            act.wait_ge(s_gat[s], g * 16 + 16)
                            act.activation(run[:, k, s, :], gath[:, s, :], ACT.Copy,
                                           scale=col(w_e, g * G + s)).then_inc(s_scaled, 1)
                            if s == G // 2:
                                act.wait_ge(s_btp, g + 1)
                                act.activation(xT[:, 0, :, :].rearrange("p c t -> p (c t)"), ps[:, 6, 0:D],
                                               ACT.Copy).then_inc(s_bxT, 1)
                act.wait_ge(s_ct, 1)
                act.activation(stT.rearrange("p c t -> p (c t)"), ps[:, 0, 0:D], ACT.Copy).then_inc(s_cc, 1)

            @block.vector
            def _(dve):
                link = linker(dve, s=s_q, count=qn)
                dve.sem_inc(s_fold, G - 1)
                dve.memset(run[:, 1, G - 1, :], 0.0).then_inc(s_fold, 1)
                link(dve.tensor_copy(dst_f[:, :], dst_i[:, :]))
                link(dve.tensor_scalar(part_i[:, :], dst_i[:, :], P - 1, None, ALU.bitwise_and))
                link(dve.tensor_copy(lo_f[:, :], part_i[:, :]))
                link(dve.tensor_scalar(part_i[:, :], dst_i[:, :], 7, None, ALU.arith_shift_right))
                link(dve.tensor_copy(hi_f[:, :], part_i[:, :]))
                link(dve.memset(flag[:, 0:1], NEG))
                link(dve.tensor_tensor(flag[:, 1:COLS], dst_f[:, 1:COLS], dst_f[:, 0:COLS - 1], ALU.not_equal))
                link(dve.tensor_scalar(flag[:, 1:COLS], flag[:, 1:COLS], NEG, None, ALU.mult))
                link(dve.tensor_scalar(first_row[:, :], dst_f[:, :], dst_f[:, 0:1], None, ALU.is_equal))
                link(dve.tensor_reduce(fix_f[:, 0:1], first_row[:, :], AX.X, ALU.add))
                link(dve.tensor_tensor(fix_f[:, 1:2], fix_f[:, 0:1], pcol[:, :], ALU.add))
                link(dve.tensor_copy(fix_i[:, :], fix_f[:, 1:2]))
                dve.tensor_scalar(firstlast[:, 0, :], ident[:, :], dst_f[:, 0:1], None, ALU.mult).then_inc(s_dg, 1)
                dve.tensor_scalar(firstlast[:, 1, :], ident[:, :], dst_f[:, COLS - 1:COLS], None, ALU.mult)\
                   .then_inc(s_dg, 1)
                link(dve.memset(oh_lo[:, 0, :], 0.0))
                dve.memset(oh_hi[:, 0, :], 0.0).then_inc(s_cb, 1)
                dve.wait_ge(s_flp, 1)
                link(dve.tensor_copy(fl_b.rearrange("p a b -> p (a b)"), ps[:, 1, 0:2 * P]))
                link(dve.memset(newseg[:, 0:1], 1.0))
                link(dve.tensor_tensor(newseg[:, 1:P], fl_b[:, 0, 1:P], fl_b[:, 1, 0:P - 1], ALU.not_equal))
                link(dve.tensor_tensor(scanflag[:, :], fl_b[:, 0, :], fl_b[:, 1, :], ALU.not_equal))
                link(dve.tensor_tensor(scanflag[:, :], scanflag[:, :], newseg[:, :], ALU.max))
                link(dve.tensor_scalar(scanflag[:, :], scanflag[:, :], NEG, None, ALU.mult))
                link(dve.tensor_scalar(newseg[:, :], newseg[:, :], NEG, None, ALU.mult))
                link(dve.tensor_tensor(bsn_b[:, 0, :], bsn_b[:, 0, :], bsn_b[:, 1, :], ALU.add))
                dve.wait_ge(s_cb, 2)
                dve.engine_nop().then_inc(s_fixi, 1)
                dve.engine_nop().then_inc(s_ep, 1)

                for it in turns(dve, GROUPS // 2):
                    for k in range(2):
                        g = it * 2 + k
                        dve.tensor_scalar(xn[:, 0, :], tile_of(xs, g), col(mean, g), col(rstd, g),
                                          ALU.subtract, ALU.mult).then_inc(s_bxn, 1)
                        dve.wait_ge(s_cnt, g)
                        lo = lo_f[:, bass.ds(g * G, G)].unsqueeze(2).to_broadcast([P, G, P])
                        hi = hi_f[:, bass.ds(g * G, G)].unsqueeze(2).to_broadcast([P, G, 32])
                        dve.tensor_tensor(oh_lo, lo, IOTA_B, ALU.is_equal).then_inc(s_oh, 1)
                        dve.tensor_tensor(oh_hi, hi, IOTA_H, ALU.is_equal).then_inc(s_oh, 1)
                        for s in range(G):
                            dve.wait_ge(s_scaled, g * G + s + 1 + G)
                            dve.wait_ge(s_fold, g * G + s + G)
                            before = run[:, k, s - 1, :] if s else run[:, 1 - k, G - 1, :]
                            dve.scalar_tensor_tensor(out=run[:, k, s, :], in0=before,
                                                     scalar=col(flag, g * G + s), in1=run[:, k, s, :],
                                                     op0=ALU.add, op1=ALU.max).then_inc(s_fold, 1)
                        dve.wait_ge(s_by, g + 1)
                        dve.tensor_tensor(tile_of(xs, g), tile_of(xs, g), ps[:, 4, 0:D], ALU.add)\
                           .then_inc(s_q2, 1)
                        dve.wait_ge(s_q2, g + 1)
                        dve.tensor_tensor(tile_of(xs, g), tile_of(xs, g), bsn_b[:, 0, :], ALU.add)\
                           .then_inc(s_bx, 1)

                dve.wait_ge(s_dgr, 1)
                link(dve.tensor_copy(deg[:, :], ps[:, 2, 0:NT]))
                dve.engine_nop().then_inc(s_dg, 1)
                link(dve.tensor_scalar(dmask[:, :], deg[:, :], 0.0, None, ALU.is_gt))
                dve.wait_ge(s_dsum, 1)
                link(dve.tensor_copy(tmp[:, 0:NT], ps[:, 3, 64:64 + NT]))
                link(dve.memset(end_f[:, :], 0.0))
                link(dve.tensor_tensor_scan(dcum[:, :], tmp[:, 0:NT], end_f[:, :], 0.0, ALU.add, ALU.add))
                link(dve.tensor_tensor(dcum[:, :], dcum[:, :], tmp[:, 0:NT], ALU.subtract))
                link(dve.tensor_tensor(end_f[:, :], dcum[:, :], ps[:, 3, 0:NT], ALU.add))
                link(dve.tensor_scalar(end_f[:, :], end_f[:, :], -1.0, 0.0, ALU.add, ALU.max))
                link(dve.tensor_copy(end_i[:, :], end_f[:, :]))
                dve.wait_ge(s_cc, 1)
                for c in range(KD):
                    link(dve.tensor_tensor_scan(carT[:, c, :], scanflag[:, :], stT[:, c, :], 0.0, ALU.add, ALU.max))
                link(dve.memset(stT[:, :, 0:1], NEG))
                for c in range(KD):
                    link(dve.tensor_tensor(stT[:, c, 1:P], carT[:, c, 0:P - 1], newseg[:, 1:P], ALU.add))
                dve.engine_nop().then_inc(s_cs, 1)
                dve.wait_ge(s_ct, 2)
                dve.wait_ge(s_v, 16)
                dve.tensor_tensor(vfix[:, :], vrow[:, :], ps[:, 1, 0:D], ALU.max).then_inc(s_cr, 1)

            @block.tensor
            def _(pe):
                pe.wait_ge(s_dg, 2)
                pe.matmul(ps[:, 1, 0:2 * P], ones[:, :], firstlast.rearrange("p a b -> p (a b)"),
                          start=True, stop=True).then_inc(s_flp, 1)
                pe.wait_ge(s_cb, 1)
                pe.matmul(ps[:, 2, 0:32], oh_lo[:, 0, :], oh_hi[:, 0, :], start=True, stop=False)\
                  .then_inc(s_cb, 1)
                with pe.Fori(0, GROUPS // 2) as it:
                    for k in range(2):
                        g = it * 2 + k
                        pe.wait_ge(s_bxn, g + 1)
                        for c in range(KD):
                            last = pe.transpose(ps[:, 6, c * P:(c + 1) * P], xn[:, 0, c * P:(c + 1) * P],
                                                ident[:, :])
                        last.then_inc(s_btp, 1)
                        pe.wait_ge(s_oh, 2 * g + 2)
                        for s in range(G):
                            last = pe.matmul(ps[:, 2, 0:32], oh_lo[:, s, :], oh_hi[:, s, :],
                                             start=False, stop=False)
                        last.then_inc(s_cnt, 1)
                        pe.wait_ge(s_bxT, g + 1)
                        for c in range(KD):
                            last = pe.matmul(ps[:, 4, 0:D], xT[:, 0, c, :], wsT[:, c, :],
                                             start=(c == 0), stop=(c == KD - 1))
                        last.then_inc(s_by, 1)
                pe.wait_ge(s_cnt, GROUPS)
                pe.wait_ge(s_bx, GROUPS)
                pe.matmul(ps[:, 2, 0:32], ones[:, :], zrow[:, :], start=False, stop=True).then_inc(s_dgr, 1)
                pe.wait_ge(s_dg, 3)
                pe.matmul(ps[:, 3, 0:NT], tri_le[:, :], deg[:, :], start=True, stop=True)
                pe.matmul(ps[:, 3, 64:64 + NT], ones[:, :], deg[:, :], start=True, stop=True).then_inc(s_dsum, 1)
                pe.wait_ge(s_fold, COLS + G)
                for c in range(KD):
                    last = pe.transpose(ps[:, 0, c * P:(c + 1) * P], run[:, 1, G - 1, c * P:(c + 1) * P],
                                        ident[:, :])
                last.then_inc(s_ct, 1)
                pe.wait_ge(s_cs, 1)
                for c in range(KD):
                    last = pe.transpose(ps[:, 1, c * P:(c + 1) * P], stT[:, c, :], ident[:, :])
                last.then_inc(s_ct, 1)
        s_ei, s_ng = sem("end_index_ready"), sems("neigh_gathered", 2)
        s_ngm, s_ntp, s_nT = sem("neigh_masked"), sem("neigh_transposed"), sem("neighT_ready")
        s_ny, s_x1, s_x1s = sem("neigh_product"), sem("x1_ready"), sem("x1_stored")
        s_var2, s_std2, s_nst = sem("variances2_ready"), sem("deviations2_ready"), sem("statistics2_taken")
        s_x2, s_x2p, s_x2T, s_x2s = sem("x2_ready"), sem("x2_transposed"), sem("x2T_ready"), sems("x2_stored", 2)
        s_gl, s_lg, s_top = sem("gate_product"), sem("logits_ready"), sem("top2_kept")
        s_r = sem("routing_vector_chain")
        s_mem, s_rk, s_sl = sem("members_ready"), sem("ranks_ready"), sem("slots_ready")
        s_dif, s_th = sem("top2_difference"), sem("tanh_ready")
        s_cp, s_sc = sem("slots_copied"), sems("entries_scattered", 4)
        s_w = sem("expert_weights_loaded")
        rn = [0]
        out_v = out[0:(NT - 1) * P, :].rearrange("(t p) d -> p t d", p=P)
        w1_s = arena[:, W1_AT:B1_AT].rearrange("p (e c h) -> p e c h", e=NEXP, c=KD)
        b1_s = arena[:, B1_AT:B2_AT].rearrange("p (e h) -> p e h", e=NEXP)
        b2_s = arena[:, B2_AT:W2_AT].rearrange("p (e d) -> p e d", e=NEXP)
        w2_s = arena[:, W2_AT:ARENA].rearrange("p (e c d) -> p e c d", e=NEXP, c=KH)
        EARLY = NEXP - LATE

        with nc.Block() as block:
            @block.sync
            def _(sp):
                def store_x1(n):
                    sp.wait_ge(s_x1, n + 1 + CREDIT)
                    sp.dma_start(tile_of(out_v, n), tile_of(xs, n)).then_inc(s_x1s, 16)

                def store_x2(n, q):
                    sp.wait_ge(s_x2, n + 1 + CREDIT)
                    sp.dma_start(tile_of(x2_v, n), xn[:, q, :]).then_inc(s_x2s[q], 16)
                with sp.Fori(0, NT - 1) as n:
                    store_x1(n)
                sp.wait_ge(s_x1, NT + CREDIT)
                sp.dma_start(out[(NT - 1) * P:N, :], xs[0:TAIL, NT - 1, :]).then_inc(s_x1s, 16)
                with sp.Fori(0, NT // 2) as it:
                    for q in range(2):
                        store_x2(it * 2 + q, q)
                store_x2(NT - 1, 0)
                sp.wait_ge(s_x1s, 16 * NT)
                sp.wait_ge(s_x2s[0], 16 * (NT // 2 + 1))
                sp.wait_ge(s_x2s[1], 16 * (NT // 2))

            @block.gpsimd
            def _(pool):
                last_row = pool.to_reg(P * COLS - 1)

                def neigh(n, q):
                    pool.wait_ge(s_ngm, n - 1 + CREDIT)
                    pool.tensor_copy(ei[:, q:q + 1], col(end_i, n)).then_inc(s_ei, 1)
                    pool.wait_ge(s_ei, n + 1)
                    settle(pool)
                    pool.indirect_dma_start(ng[:, q, :], None, run_dram,
                                            bass.IndirectOffsetOnAxis(ei[:, q:q + 1], 0),
                                            bounds_check=last_row, oob_is_err=False).then_inc(s_ng[q], 16)
                with pool.Fori(0, NT // 2) as it:
                    for q in range(2):
                        neigh(it * 2 + q, q)
                neigh(NT - 1, 0)

                last_entry = pool.to_reg(TABLE - 1)
                pool.wait_ge(s_sl, 1)

                def scatter(it, n, q):
                    for c in range(2):
                        pool.wait_ge(s_sc[2 * q + c], 16 * it)
                    pool.tensor_copy(sl_i[:, q, :], slot_i[:, bass.ds(n, 1), :].rearrange("p a b -> p (a b)"))\
                        .then_inc(s_cp, 1)
                    pool.tensor_copy(en_s[:, q, :, :].rearrange("p a b -> p (a b)"),
                                     entry[:, bass.ds(n, 1), :, :].rearrange("p a b c -> p (a b c)")).then_inc(s_cp, 1)
                    pool.wait_ge(s_cp, 2 * n + 2)
                    settle(pool)
                    for c in range(2):
                        pool.indirect_dma_start(table, bass.IndirectOffsetOnAxis(sl_i[:, q, c:c + 1], 0),
                                                en_s[:, q, c, :], None, bounds_check=last_entry, oob_is_err=False)\
                            .then_inc(s_sc[2 * q + c], 16)
                for it in turns(pool, NT // 2):
                    for q in range(2):
                        scatter(it, it * 2 + q, q)
                scatter(NT // 2, NT - 1, 0)
                for c in range(4):
                    pool.wait_ge(s_sc[c], 16 * (NT // 2 + (c < 2)))

            @block.scalar
            def _(act):
                def load(d, s):
                    act.dma_start(d, s).then_inc(s_w, 16)
                load(w1_s[:, 0:NEXP // 2], W1[0:NEXP // 2].rearrange("e (c p) h -> p e c h", p=P))
                load(w1_s[:, NEXP // 2:NEXP], W1[NEXP // 2:NEXP].rearrange("e (c p) h -> p e c h", p=P))
                load(b1_s.rearrange("p e h -> p (e h)"), b1.rearrange("e h -> (e h)").partition_broadcast(P))
                load(b2_s.rearrange("p e h -> p (e h)"), b2.rearrange("e h -> (e h)").partition_broadcast(P))
                load(w2_s[:, 0:EARLY], W2[0:EARLY].rearrange("e (c p) d -> p e c d", p=P))
                act.sem_inc(s_ngm, CREDIT)
                act.sem_inc(s_x2T, CREDIT)

                def mask(it, n, q):
                    act.wait_ge(s_ng[q], it * 16 + 16)
                    act.wait_ge(s_ntp, n - 1 + CREDIT)
                    act.activation(ngm[:, q, :], ng[:, q, :], ACT.Copy, scale=col(dmask, n)).then_inc(s_ngm, 1)
                with act.Fori(0, NT // 2) as it:
                    for q in range(2):
                        mask(it, it * 2 + q, q)
                mask(NT // 2, NT - 1, 0)
                act.wait_ge(s_var2, 1)
                act.activation(rstd[:, 0:NT], var[:, 0:NT], ACT.Sqrt, bias=eps[:, 0:1]).then_inc(s_std2, 1)

                def evac(n, q):
                    act.wait_ge(s_x2p, n + 1 + CREDIT)
                    act.wait_ge(s_gl, n - 1 + CREDIT)
                    act.activation(xT[:, q, :, :].rearrange("p c t -> p (c t)"), ps[:, 6 + q, 0:D],
                                   ACT.Copy).then_inc(s_x2T, 1)
                with act.Fori(0, NT // 2) as it:
                    for q in range(2):
                        evac(it * 2 + q, q)
                evac(NT - 1, 0)
                act.wait_ge(s_dif, 1)
                act.activation(prod[:, 0, :, 0], prod[:, 1, :, 0], ACT.Tanh, scale=0.5).then_inc(s_th, 1)
                act.wait_ge(s_w, 16 * 5)

            @block.vector
            def _(dve):
                for s in (s_nT, s_x1, s_x2, s_lg):
                    dve.sem_inc(s, CREDIT)

                def evac(n, q):
                    dve.wait_ge(s_ntp, n + 1 + CREDIT)
                    dve.wait_ge(s_ny, n - 1 + CREDIT)
                    dve.tensor_copy(xT[:, q, :, :].rearrange("p c t -> p (c t)"), ps[:, 6 + q, 0:D])\
                       .then_inc(s_nT, 1)

                def add(n, q):
                    dve.wait_ge(s_ny, n + 1 + CREDIT)
                    dve.tensor_tensor(tile_of(xs, n), tile_of(xs, n), ps[:, 4 + q, 0:D], ALU.add).then_inc(s_x1, 1)
                    dve.wait_ge(s_x1, n + 1 + CREDIT)
                    dve.bn_stats(st[:, bass.ds(n, 1), :].rearrange("p a b -> p (a b)"), tile_of(xs, n))\
                       .then_inc(s_nst, 1)
                evac(0, 0)
                with dve.Fori(0, NT // 2) as it:
                    for q in range(2):
                        evac(it * 2 + q + 1, 1 - q)
                        add(it * 2 + q, q)
                add(NT - 1, 0)
                dve.wait_ge(s_nst, NT)
                link = linker(dve, s=s_r, count=rn)
                link(dve.tensor_tensor(tmp[:, 0:NT], st[:, 0:NT, 1], st[:, 0:NT, 4], ALU.subtract))
                link(dve.tensor_tensor(mean[:, 0:NT], st[:, 0:NT, 1], st[:, 0:NT, 4], ALU.add))
                link(dve.tensor_scalar(mean[:, 0:NT], mean[:, 0:NT], 0.5, None, ALU.mult))
                link(dve.tensor_tensor(var[:, 0:NT], st[:, 0:NT, 2], st[:, 0:NT, 5], ALU.add))
                link(dve.tensor_tensor(tmp[:, 0:NT], tmp[:, 0:NT], tmp[:, 0:NT], ALU.mult))
                link(dve.tensor_scalar(tmp[:, 0:NT], tmp[:, 0:NT], 0.25, None, ALU.mult))
                dve.scalar_tensor_tensor(out=var[:, 0:NT], in0=var[:, 0:NT], scalar=1.0 / D, in1=tmp[:, 0:NT],
                                         op0=ALU.mult, op1=ALU.add).then_inc(s_var2, 1)
                dve.wait_ge(s_std2, 1)
                link(dve.reciprocal(rstd[:, 0:NT], rstd[:, 0:NT]))

                def norm(it, n, q):
                    dve.wait_ge(s_x2p, n - 1 + CREDIT)
                    dve.wait_ge(s_x2s[q], 16 * it)
                    dve.tensor_scalar(xn[:, q, :], tile_of(xs, n), col(mean, n), col(rstd, n),
                                      ALU.subtract, ALU.mult).then_inc(s_x2, 1)

                def top2(n, q):
                    dve.wait_ge(s_gl, n + 1 + CREDIT)
                    dve.tensor_tensor(lg[:, q, :], ps[:, 4 + q, 0:NEXP], bg_b[:, :], ALU.add).then_inc(s_lg, 1)
                    dve.wait_ge(s_lg, n + 1 + CREDIT)
                    settle(dve)
                    dve.max(mx[:, q, :], lg[:, q, :]).then_inc(s_top, 1)
                    dve.wait_ge(s_top, 4 * n + 1)
                    settle(dve)
                    dve.max_index(mi[:, q, :], mx[:, q, :], lg[:, q, :]).then_inc(s_top, 1)
                    dve.wait_ge(s_top, 4 * n + 2)
                    dve.tensor_copy(vals[:, bass.ds(n, 1), :].rearrange("p a b -> p (a b)"), mx[:, q, 0:2])\
                       .then_inc(s_top, 1)
                    dve.tensor_copy(ids[:, bass.ds(n, 1), :].rearrange("p a b -> p (a b)"), mi[:, q, 0:2])\
                       .then_inc(s_top, 1)
                norm(0, 0, 0)
                for it in turns(dve, NT // 2):
                    norm(it, it * 2 + 1, 1)
                    top2(it * 2, 0)
                    norm(it + 1, it * 2 + 2, 0)
                    top2(it * 2 + 1, 1)
                top2(NT - 1, 0)
                dve.wait_ge(s_top, 4 * NT)

                dve.tensor_tensor(prod[:, 1, :, 0], vals[:, :, 1], vals[:, :, 0], ALU.subtract).then_inc(s_dif, 1)
                iota_e = iota_r[:, 0:NEXP].unsqueeze(1).to_broadcast([P, NT, NEXP])
                ok = valid[:, :].unsqueeze(2).to_broadcast([P, NT, NEXP])
                for c, oh in ((0, oh1), (1, oh2)):
                    link(dve.tensor_tensor(oh, ids[:, :, c:c + 1].to_broadcast([P, NT, NEXP]), iota_e, ALU.is_equal))
                link(dve.tensor_tensor(member, oh1, oh2, ALU.add))
                dve.tensor_tensor(member, member, ok, ALU.mult).then_inc(s_mem, 1)
                dve.wait_ge(s_rk, 1)
                link(dve.tensor_copy(tot, ps[:, 3, 0:NT * NEXP].rearrange("p (t e) -> p e t", e=NEXP)))
                link(dve.memset(tmp[:, 0:NT], 0.0))
                for e in range(NEXP):
                    link(dve.tensor_tensor_scan(cum[:, e, :], tot[:, e, :], tmp[:, 0:NT], 0.0, ALU.add, ALU.add))
                link(dve.tensor_tensor(tot, cum, tot, ALU.subtract))
                link(dve.tensor_tensor(pos, tot.rearrange("p e t -> p t e"),
                                       ps[:, 2, 0:NT * NEXP].rearrange("p (t e) -> p t e", e=NEXP), ALU.add))
                link(dve.tensor_scalar(member, iota_e, float(CAP), None, ALU.mult))
                link(dve.tensor_tensor(pos, pos, member, ALU.add))
                dve.wait_ge(s_th, 1)
                link(dve.tensor_scalar(entry[:, :, 1, 1], prod[:, 0, :, 0], 0.5, 0.5, ALU.mult, ALU.add))
                link(dve.tensor_scalar(entry[:, :, 0, 1], entry[:, :, 1, 1], -1.0, 1.0, ALU.mult, ALU.add))
                for c, oh in ((0, oh1), (1, oh2)):
                    link(dve.tensor_copy(entry[:, :, c, 0], tok_f[:, :]))
                    link(dve.tensor_tensor(prod[:, c], oh, pos, ALU.mult))
                    link(dve.tensor_reduce(slot_f[:, :, c], prod[:, c], AX.X, ALU.add))
                link(dve.tensor_scalar(tmp[:, 0:NT], valid[:, :], -NOWHERE, NOWHERE, ALU.mult, ALU.add))
                for c in range(2):
                    link(dve.tensor_tensor(slot_f[:, :, c], slot_f[:, :, c], tmp[:, 0:NT], ALU.add))
                link(dve.tensor_copy(slot_i, slot_f))
                dve.engine_nop().then_inc(s_sl, 1)
                link(dve.tensor_scalar(tl[:, 0, :], cum[0:1, :, NT - 1], float(P - 1), None, ALU.add))
                link(dve.tensor_copy(tl_i[:, :], tl[:, 0, :]))
                link(dve.tensor_scalar(tl_i[:, :], tl_i[:, :], 7, None, ALU.arith_shift_right))
                link(dve.tensor_copy(tl[:, 1, :], tl_i[:, :]))
                link(dve.memset(tl[:, 3, :], 0.0))
                link(dve.tensor_tensor_scan(tl[:, 2, :], tl[:, 1, :], tl[:, 3, :], 0.0, ALU.add, ALU.add))
                shape = [1, MOE_TILES, NEXP - 1]
                link(dve.tensor_tensor(m_cmp[0:1, :, 0:NEXP - 1], tl[:, 2:3, 0:NEXP - 1].to_broadcast(shape),
                                       iota_r[0:1, 0:MOE_TILES].unsqueeze(2).to_broadcast(shape), ALU.is_le))
                link(dve.tensor_tensor(m_mul[0:1, :, 0:NEXP - 1], m_cmp[0:1, :, 0:NEXP - 1],
                                       tl[:, 1:2, 0:NEXP - 1].to_broadcast(shape), ALU.mult))
                link(dve.tensor_reduce(tab_f[:, 0, :], m_cmp[0:1, :, 0:NEXP - 1], AX.X, ALU.add))
                link(dve.tensor_reduce(tab_f[:, 1, :], m_mul[0:1, :, 0:NEXP - 1], AX.X, ALU.add))
                link(dve.tensor_tensor(tab_f[:, 1, :], iota_r[0:1, 0:MOE_TILES], tab_f[:, 1, :], ALU.subtract))
                link(dve.tensor_scalar(tab_f[:, 1, :], tab_f[:, 1, :], float(P), None, ALU.mult))
                link(dve.scalar_tensor_tensor(out=tab_f[:, 2, :], in0=tab_f[:, 0, :], scalar=float(CAP),
                                              in1=tab_f[:, 1, :], op0=ALU.mult, op1=ALU.add))
                link(dve.tensor_copy(e_tab[:, :], tab_f[:, 0, :]))
                link(dve.tensor_copy(r_tab[:, :], tab_f[:, 2, :]))

            @block.tensor
            def _(pe):
                for s in (s_ntp, s_ny, s_x2p, s_gl):
                    pe.sem_inc(s, CREDIT)

                def turn(n, q):
                    pe.wait_ge(s_ngm, n + 1 + CREDIT)
                    pe.wait_ge(s_nT, n - 1 + CREDIT)
                    for c in range(KD):
                        last = pe.transpose(ps[:, 6 + q, c * P:(c + 1) * P], ngm[:, q, c * P:(c + 1) * P],
                                            ident[:, :])
                    last.then_inc(s_ntp, 1)

                def product(n, q):
                    pe.wait_ge(s_nT, n + 1 + CREDIT)
                    pe.wait_ge(s_x1, n - 1 + CREDIT)
                    for c in range(KD):
                        last = pe.matmul(ps[:, 4 + q, 0:D], xT[:, q, c, :], wnT[:, c, :],
                                         start=(c == 0), stop=(c == KD - 1))
                    last.then_inc(s_ny, 1)
                turn(0, 0)
                with pe.Fori(0, NT // 2) as it:
                    for q in range(2):
                        turn(it * 2 + q + 1, 1 - q)
                        product(it * 2 + q, q)
                product(NT - 1, 0)

                def turn2(n, q):
                    pe.wait_ge(s_x2, n + 1 + CREDIT)
                    pe.wait_ge(s_x2T, n - 1 + CREDIT)
                    for c in range(KD):
                        last = pe.transpose(ps[:, 6 + q, c * P:(c + 1) * P], xn[:, q, c * P:(c + 1) * P],
                                            ident[:, :])
                    last.then_inc(s_x2p, 1)

                def gate(n, q):
                    pe.wait_ge(s_x2T, n + 1 + CREDIT)
                    pe.wait_ge(s_lg, n - 1 + CREDIT)
                    for c in range(KD):
                        last = pe.matmul(ps[:, 4 + q, 0:NEXP], xT[:, q, c, :], wg_s[:, c, :],
                                         start=(c == 0), stop=(c == KD - 1))
                    last.then_inc(s_gl, 1)
                pe.wait_ge(s_x1, NT + CREDIT)
                pe.wait_ge(s_nT, NT + CREDIT)
                turn2(0, 0)
                with pe.Fori(0, NT // 2) as it:
                    for q in range(2):
                        turn2(it * 2 + q + 1, 1 - q)
                        gate(it * 2 + q, q)
                gate(NT - 1, 0)
                pe.wait_ge(s_mem, 1)
                flat = member.rearrange("p t e -> p (t e)")
                pe.matmul(ps[:, 2, 0:NT * NEXP], tri_lt[:, :], flat, start=True, stop=True)
                pe.matmul(ps[:, 3, 0:NT * NEXP], ones[:, :], flat, start=True, stop=True).then_inc(s_rk, 1)
        RING = 4
        s_w2 = sem("last_w2_loaded")
        s_tab, s_tok = sems("queue_rows_loaded", RING), sem("tokens_ready")
        s_xg = sems("tokens_gathered", RING)
        s_tok0, s_xp, s_xe, s_hp = sem("token_buffers_cleared"), sem("tokens_transposed"), sem("tokensT_ready"), sem("hidden_product")
        s_pre, s_gel, s_gp = sem("hidden_biased"), sem("hidden_ready"), sem("hidden_transposed")
        s_ge, s_ge2, s_yp = sem("hiddenT_ready_scalar"), sem("hiddenT_ready_vector"), sem("out_product")
        s_yb, s_yw, s_add = sem("out_biased"), sem("out_weighted"), sems("out_added", 2)
        at_xs = [0]
        xs_flat = xs[:, :, :].rearrange("p t d -> p (t d)")

        def over_x(*shape, dt=F32):
            n = 1
            for s in shape:
                n *= s
            v = xs_flat[:, at_xs[0]:at_xs[0] + n]
            at_xs[0] += n
            if dt != F32:
                v = v.bitcast(dt)
            if len(shape) == 2:
                v = v.rearrange("p (a b) -> p a b", b=shape[1])
            elif len(shape) == 3:
                v = v.rearrange("p (a b c) -> p a b c", b=shape[1], c=shape[2])
            return v

        rows = over_x(RING, 2)
        toks = over_x(RING, 2, dt=I32)
        tg = over_x(RING, D)
        tgT = over_x(2, KD, P)
        pre = over_x(HID)
        hid = over_x(HID)
        hidT = over_x(KH, P)
        yb = over_x(2, D)
        yw = over_x(2, D)
        assert at_xs[0] <= (NT + 1) * D
        XP, HP, GP, YP = 0, 1, 3, 5

        with nc.Block() as block:
            @block.sync
            def _(sp):
                def load_rows(n, u):
                    r = sp.value_load(r_tab[0:1, bass.ds(n, 1)], min_val=0, max_val=TABLE - P)
                    sp.dma_start(rows[:, u, :], table[bass.ds(r, P), :]).then_inc(s_tab[u], 16)
                for u in range(RING):
                    load_rows(u, u)
                with sp.Fori(0, MOE_TILES // RING - 1) as it:
                    for u in range(RING):
                        sp.wait_ge(s_yw, it * RING + u + 1 + CREDIT)
                        settle(sp)
                        sp.wait_ge(s_tok, it * RING + u + 1)
                        settle(sp)
                        load_rows(it * RING + u + RING, u)

            @block.gpsimd
            def _(pool):
                last_tok = pool.to_reg(N - 1)
                pool.memset(tg[:, :, :], 0.0).then_inc(s_tok0, 1)
                pool.wait_ge(s_tok0, 1)

                def gather(it, n, u):
                    pool.wait_ge(s_tab[u], it * 16 + 16)
                    settle(pool)
                    pool.tensor_copy(toks[:, u, 0:1], rows[:, u, 0:1]).then_inc(s_tok, 1)
                    pool.wait_ge(s_xp, n + 1)
                    pool.wait_ge(s_tok, n + 1)
                    settle(pool)
                    pool.indirect_dma_start(tg[:, u, :], None, x2_dram,
                                            bass.IndirectOffsetOnAxis(toks[:, u, 0:1], 0),
                                            bounds_check=last_tok, oob_is_err=False).then_inc(s_xg[u], 16)

                def add_rows(it, n, u):
                    pool.wait_ge(s_yw, n + 1 + CREDIT)
                    pool.wait_ge(s_add[1 - u % 2], it * 32 + (u + 1) // 2 * 16)
                    settle(pool)
                    pool.indirect_dma_start(out, bass.IndirectOffsetOnAxis(toks[:, u, 0:1], 0),
                                            yw[:, u % 2, :], None, bounds_check=last_tok, oob_is_err=False,
                                            compute_op=ALU.add).then_inc(s_add[u % 2], 16)
                for u in range(RING):
                    gather(0, u, u)
                for it in turns(pool, MOE_TILES // RING - 1):
                    for u in range(RING):
                        n = it * RING + u
                        add_rows(it, n, u)
                        pool.wait_ge(s_add[u % 2], it * 32 + u // 2 * 16 + 16)
                        gather(it + 1, n + RING, u)
                for u in range(RING):
                    add_rows(MOE_TILES // RING - 1, MOE_TILES - RING + u, u)
                for q in range(2):
                    pool.wait_ge(s_add[q], MOE_TILES // 2 * 16)

            @block.scalar
            def _(act):
                act.dma_start(w2_s[:, EARLY:NEXP], W2[EARLY:NEXP].rearrange("e (c p) d -> p e c d", p=P))\
                   .then_inc(s_w2, 16)
                act.sem_inc(s_yw, CREDIT)

                def gelu(n):
                    act.wait_ge(s_pre, n + 1)
                    act.wait_ge(s_gp, n)
                    act.activation(hid[:, :], pre[:, :], ACT.Gelu).then_inc(s_gel, 1)

                def evac(n):
                    act.wait_ge(s_gp, n + 1)
                    act.wait_ge(s_yp, n)
                    act.activation(hidT[:, 0:KH // 2, :].rearrange("p c t -> p (c t)"), ps[:, GP, :],
                                   ACT.Copy).then_inc(s_ge, 1)

                def weigh(it, n, u):
                    act.wait_ge(s_yb, n + 1)
                    act.wait_ge(s_tab[u], it * 16 + 16)
                    act.wait_ge(s_add[u % 2], it * 32 + u // 2 * 16)
                    act.activation(yw[:, u % 2, :], yb[:, u % 2, :], ACT.Copy,
                                   scale=rows[:, u, 1:2]).then_inc(s_yw, 1)
                gelu(0)
                for it in turns(act, MOE_TILES // RING - 1):
                    for u in range(RING):
                        n = it * RING + u
                        evac(n)
                        gelu(n + 1)
                        weigh(it, n, u)
                for u in range(RING):
                    n = MOE_TILES - RING + u
                    evac(n)
                    if u < RING - 1:
                        gelu(n + 1)
                    weigh(MOE_TILES // RING - 1, n, u)

            @block.vector
            def _(dve):
                def expert(n):
                    return dve.value_load(e_tab[0:1, bass.ds(n, 1)], min_val=0, max_val=NEXP - 1)

                def evac_x(n, q):
                    dve.wait_ge(s_xp, n + 1 + RING)
                    dve.wait_ge(s_hp, n - 1 + CREDIT)
                    dve.tensor_copy(tgT[:, q].rearrange("p c t -> p (c t)"), ps[:, XP, 0:D]).then_inc(s_xe, 1)

                def bias_h(n):
                    e = expert(n)
                    dve.wait_ge(s_hp, n + 1 + CREDIT)
                    dve.wait_ge(s_gel, n)
                    dve.tensor_tensor(pre[:, :], ps[:, HP:HP + 2, :].rearrange("p a b -> p (a b)"),
                                      b1_s[:, bass.ds(e, 1), :].rearrange("p a h -> p (a h)"), ALU.add)\
                       .then_inc(s_pre, 1)

                def evac_h(n):
                    dve.wait_ge(s_gp, n + 1)
                    dve.wait_ge(s_yp, n)
                    dve.tensor_copy(hidT[:, KH // 2:KH, :].rearrange("p c t -> p (c t)"), ps[:, GP + 1, :])\
                       .then_inc(s_ge2, 1)

                def bias_y(n, q):
                    e = expert(n)
                    dve.wait_ge(s_yp, n + 1)
                    dve.wait_ge(s_yw, n - 1 + CREDIT)
                    dve.tensor_tensor(yb[:, q, :], ps[:, YP + q, 0:D],
                                      b2_s[:, bass.ds(e, 1), :].rearrange("p a d -> p (a d)"), ALU.add)\
                       .then_inc(s_yb, 1)
                evac_x(0, 0)
                bias_h(0)
                for it in turns(dve, MOE_TILES // RING - 1):
                    for u in range(RING):
                        n = it * RING + u
                        evac_x(n + 1, 1 - u % 2)
                        evac_h(n)
                        bias_h(n + 1)
                        bias_y(n, u % 2)
                for u in range(RING):
                    n = MOE_TILES - RING + u
                    if u < RING - 1:
                        evac_x(n + 1, 1 - u % 2)
                    evac_h(n)
                    if u < RING - 1:
                        bias_h(n + 1)
                    bias_y(n, u % 2)

            @block.tensor
            def _(pe):
                pe.sem_inc(s_xp, RING)
                pe.sem_inc(s_hp, CREDIT)

                def turn_x(it, n, u):
                    pe.wait_ge(s_xg[u], it * 16 + 16)
                    pe.wait_ge(s_xe, n)
                    for c in range(KD):
                        last = pe.transpose(ps[:, XP, c * P:(c + 1) * P], tg[:, u, c * P:(c + 1) * P], ident[:, :])
                    last.then_inc(s_xp, 1)

                def up(n, q):
                    e = pe.value_load(e_tab[0:1, bass.ds(n, 1)], min_val=0, max_val=NEXP - 1)
                    pe.wait_ge(s_xe, n + 1)
                    pe.wait_ge(s_pre, n)
                    for half in range(2):
                        for c in range(KD):
                            w = w1_s[:, bass.ds(e, 1), c, half * 512:(half + 1) * 512]
                            last = pe.matmul(ps[:, HP + half, :], tgT[:, q, c, :],
                                             w.rearrange("p a h -> p (a h)"), start=(c == 0), stop=(c == KD - 1))
                    last.then_inc(s_hp, 1)

                def turn_h(n):
                    pe.wait_ge(s_gel, n + 1)
                    for c in range(KH):
                        last = pe.transpose(ps[:, GP + c // 4, (c % 4) * P:(c % 4 + 1) * P],
                                            hid[:, c * P:(c + 1) * P], ident[:, :])
                    last.then_inc(s_gp, 1)

                def down(n, q):
                    e = pe.value_load(e_tab[0:1, bass.ds(n, 1)], min_val=0, max_val=NEXP - 1)
                    pe.wait_ge(s_ge, n + 1)
                    pe.wait_ge(s_ge2, n + 1)
                    pe.wait_ge(s_yw, n - 1 + CREDIT)
                    for c in range(KH):
                        w = w2_s[:, bass.ds(e, 1), c, :]
                        last = pe.matmul(ps[:, YP + q, 0:D], hidT[:, c, :], w.rearrange("p a d -> p (a d)"),
                                         start=(c == 0), stop=(c == KH - 1))
                    last.then_inc(s_yp, 1)
                turn_x(0, 0, 0)
                up(0, 0)
                pe.wait_ge(s_w2, 16)
                with pe.Fori(0, MOE_TILES // RING - 1) as it:
                    for u in range(RING):
                        n = it * RING + u
                        turn_x(it + (u + 1) // RING, n + 1, (u + 1) % RING)
                        turn_h(n)
                        up(n + 1, 1 - u % 2)
                        down(n, u % 2)
                for u in range(RING):
                    n = MOE_TILES - RING + u
                    if u < RING - 1:
                        turn_x(MOE_TILES // RING - 1, n + 1, u + 1)
                    turn_h(n)
                    if u < RING - 1:
                        up(n + 1, 1 - u % 2)
                    down(n, u % 2)


_INS = ['x', 'src', 'dst', 'edge_weight1', 'L0_gnn_W_pool', 'L0_gnn_b_pool', 'L0_gnn_W_self', 'L0_gnn_b_self',
        'L0_gnn_W_neigh', 'L0_gnn_b_neigh', 'L0_ffn_Wg', 'L0_ffn_bg', 'L0_ffn_W1', 'L0_ffn_b1', 'L0_ffn_W2',
        'L0_ffn_b2']


def kernel(**inputs):
    import numpy as _np
    import concourse.bacc as _bacc
    from concourse import mybir as _mybir
    from concourse.bass_utils import run_bass_kernel_spmd as _run

    nc = _bacc.Bacc("TRN2", target_bir_lowering=False, num_devices=1)
    arrays, args = {}, []
    for name in _INS:
        a = _np.ascontiguousarray(inputs[name])
        arrays[f"in_{name}_dram"] = a
        args.append(nc.dram_tensor(f"in_{name}_dram", a.shape, _mybir.dt.from_np(a.dtype), kind="ExternalInput").ap())
    args.append(nc.dram_tensor("out_dram", (N, D), F32, kind="ExternalOutput").ap())
    gnn_moe(nc, *args)
    r = _run(nc, [arrays], core_ids=[0])
    return r.results[0]["out_dram"]
```

```python
import concourse.bass as bass
from concourse import mybir
from contextlib import ExitStack

F32 = mybir.dt.float32
BF16 = mybir.dt.bfloat16
F16 = mybir.dt.float16
I32 = mybir.dt.int32
U32 = mybir.dt.uint32
ALU = mybir.AluOpType
ACT = mybir.ActivationFunctionType
AX = mybir.AxisListType

P = 128
N, D = 3125, 256
KD = D // P
NT = -(-N // P)
TAIL = N - (NT - 1) * P
E = 53125
COLS = 416
ETAIL = E - (P - 1) * COLS
G = 16
GROUPS = COLS // G
NEXP, HID = 8, 1024
KH = HID // P
CAP = NT * P
MOE_TILES = (2 * N + NEXP * (P - 1)) // P
TABLE = (NEXP * NT + MOE_TILES) * P
CH = 5
XSCALE = 1024.0
TOP = 13
EPS = 1e-5
NEG = -3.0e38
NOWHERE = 1.0e6
PAD_DST = 8191
CREDIT = 2


def gnn_moe(nc, x, src, dst, ew, Wp, bp, Ws, bs, Wn, bn, Wg, bg, W1, b1, W2, b2, out):
    ctx = ExitStack()
    with ctx:
        def sb(name, shape, dt=F32):
            return ctx.enter_context(nc.sbuf_tensor(name, shape, dt))

        def sem(name):
            return ctx.enter_context(nc.semaphore(name))

        def sems(name, n):
            return [sem(f"{name}{i}") for i in range(n)]

        h_dram = nc.dram_tensor("h_rows", (NT * P, D), F32).ap()
        run_dram = nc.dram_tensor("running_max", (P * COLS, D), F32).ap()
        x2_dram = nc.dram_tensor("ffn_in", (NT * P, D), F32).ap()
        w2_split = nc.dram_tensor("w2_parts", (NEXP, P, 2 * KH * D), F16).ap()
        table = nc.dram_tensor("queues", (TABLE, 2), F32).ap()

        W1_AT, B1_AT = 0, NEXP * KD * HID
        B2_AT = B1_AT + NEXP * HID
        W2_AT = B2_AT + NEXP * D
        ARENA = W2_AT + NEXP * KH * D
        arena = sb("arena", [P, ARENA])
        at = [B1_AT]

        def carve(shape, dt=F32):
            n = 1
            for s in shape:
                n *= s
            words = n if dt not in (BF16, F16) else n // 2
            v = arena[:, at[0]:at[0] + words]
            at[0] += words
            if dt != F32:
                v = v.bitcast(dt)
            if len(shape) == 2:
                v = v.rearrange("p (a b) -> p a b", b=shape[1])
            elif len(shape) == 3:
                v = v.rearrange("p (a b c) -> p a b c", b=shape[1], c=shape[2])
            return v

        gath = carve([G, D])
        run = carve([2, G, D])
        oh_lo = carve([G, P], BF16)
        oh_hi = carve([G, 32], BF16)
        src_i = carve([COLS], I32)
        dst_i = carve([COLS], I32)
        lo_f = carve([COLS])
        hi_f = carve([COLS])
        w_e = carve([COLS])
        flag = carve([COLS])
        wsT = carve([KD, D])
        bsn_b = carve([2, D])
        idxg = carve([2, G], I32)
        firstlast = carve([2, P])
        fl_b = carve([2, P])
        newseg = carve([P])
        scanflag = carve([P])
        stT = carve([KD, P])
        carT = carve([KD, P])
        fix_i = carve([1], I32)
        fix_f = carve([4])
        WCH = KD * HID
        wst = carve([2, WCH])
        w2st = carve([2, WCH], F16)
        end_edges = at[0]
        at[0] = B1_AT
        w_nat = carve([3, KD, D])
        wpT = carve([KD, D])
        bp_b = carve([D])
        hs = carve([2, D])
        hr = carve([2, D])
        assert at[0] <= B1_AT + G * D and KH * D == WCH
        at[0] = B1_AT
        vrow = carve([D])
        vfix = carve([D])
        at[0] = B1_AT + G * D
        part_i = carve([COLS], I32)
        dst_f = carve([COLS])
        first_row = carve([COLS])

        LATE = 2
        at[0] = ARENA - LATE * KH * D
        ng = carve([2, D])
        ngm = carve([2, D])
        lg = carve([CH, NEXP])
        mx = carve([CH, NEXP])
        mi = carve([CH, NEXP], U32)
        ids = carve([CH, 2])
        oh = carve([2, CH, NEXP])
        member = carve([CH, NEXP])
        base = carve([CH + 1, NEXP])
        pos = carve([CH, NEXP])
        prod = carve([2, CH, NEXP])
        diff = carve([CH])
        th = carve([CH])
        slot_f = carve([2, CH])
        nowhere = carve([CH])
        slot_i = carve([2, CH], I32)
        entry = carve([2, CH, 2])
        b1max = carve([NEXP])
        bnd = carve([4, NEXP])
        m_cmp = carve([MOE_TILES, NEXP])
        m_mul = carve([MOE_TILES, NEXP])
        assert max(at[0], end_edges) <= ARENA - 4 * D
        at[0] = ARENA - 4 * D
        xn = carve([2, D])
        xT = carve([2, KD, P])

        xs = sb("xs", [P, NT + 1, D])
        wnT = sb("wnT", [P, KD, D])
        wg_s = sb("wg_s", [P, KD, NEXP])
        bg_b = sb("bg_b", [P, NEXP])
        ident = sb("ident", [P, P])
        ones = sb("ones", [P, P])
        tri_lt = sb("tri_lt", [P, P])
        tri_le = sb("tri_le", [P, P])
        iota_r = sb("iota_r", [P, P])
        tok_f = sb("tok_f", [P, NT])
        valid = sb("valid", [P, NT])
        pcol = sb("pcol", [P, 1])
        eps = sb("eps", [P, 1])
        st = sb("st", [P, NT + 1, 6])
        mean = sb("mean", [P, NT + 1])
        var = sb("var", [P, NT + 1])
        rstd = sb("rstd", [P, NT + 1])
        tmp = sb("tmp", [P, NT + 1])
        deg = sb("deg", [P, NT])
        dmask = sb("dmask", [P, NT])
        dcum = sb("dcum", [P, NT])
        end_f = sb("end_f", [P, NT])
        end_i = sb("end_i", [P, NT], I32)
        ei = sb("ei", [P, 2], I32)
        wm = sb("wm", [P, 2])
        wm1 = sb("wm1", [1, 2])
        sc1 = sb("sc1", [1, 2, 2])
        wsc = sb("wsc", [P, 2, 2])
        inv1 = sb("inv1", [P, NEXP])
        inv2 = sb("inv2", [P, NEXP])
        k1 = sb("k1", [P, NEXP])
        sh = sb("sh", [P, NEXP])
        k2 = sb("k2", [P, NEXP])
        sent = sb("sent", [P, P])
        zrow = sb("zrow", [P, 32])
        tl = sb("tl", [1, 4, NEXP])
        tl_i = sb("tl_i", [1, NEXP], I32)
        tab_f = sb("tab_f", [1, 3, MOE_TILES])
        e_tab = sb("e_tab", [1, MOE_TILES], I32)
        r_tab = sb("r_tab", [1, MOE_TILES], I32)

        ps = ctx.enter_context(nc.psum_tensor("ps", [P, 8, 512], F32))

        s_memx, s_eps, s_prep = sem("x_tail_zeroed"), sem("eps_set"), sem("edge_pads_set")
        s_const = sem("constants_made")
        s_memc = sem("constants_filled")
        s_st = sem("statistics_taken")
        s_x = sems("x_loaded", 5)
        s_ld = sem("small_inputs_loaded")
        s_edge = sem("edges_loaded")
        s_sent = sem("queues_cleared")
        s_sentm = sem("sentinels_set")
        s_wps, s_wT = sem("weights_transposed"), sem("weights_out_of_psum")
        s_var, s_std, s_rstd = sem("variances_ready"), sem("deviations_ready"), sem("rstd_ready")
        s_xn, s_tps, s_xT = sem("xn_ready"), sem("xn_transposed"), sem("xT_ready")
        s_y, s_hs, s_hr = sem("h_product"), sem("h_biased"), sem("h_ready")
        s_hst = sems("h_stored", 2)
        s_dv = sem("vector_chain")
        dv = [0]

        def linker(eng, base=None, s=s_dv, count=dv):
            def link(ins):
                count[0] += 1
                ins.then_inc(s, 1)
                eng.wait_ge(s, count[0] if base is None else base + count[0])
            return link

        s_past = sem("waits_passed")

        def settle(eng):
            eng.sem_inc(s_past, 1)

        def turns(eng, count):
            yield 0
            with eng.Fori(1, count) as it:
                yield it

        CHUNK = NT // 5
        x_v = x[0:(NT - 1) * P, :].rearrange("(t p) d -> p t d", p=P)
        h_v = h_dram.rearrange("(t p) d -> p t d", p=P)
        x2_v = x2_dram.rearrange("(t p) d -> p t d", p=P)
        TABLE_W = TABLE * 2 // P

        def moments(dve, link, nt):
            link(dve.tensor_tensor(tmp[:, 0:nt], st[:, 0:nt, 1], st[:, 0:nt, 4], ALU.subtract))
            link(dve.tensor_tensor(mean[:, 0:nt], st[:, 0:nt, 1], st[:, 0:nt, 4], ALU.add))
            link(dve.tensor_scalar(mean[:, 0:nt], mean[:, 0:nt], 0.5, None, ALU.mult))
            link(dve.tensor_tensor(var[:, 0:nt], st[:, 0:nt, 2], st[:, 0:nt, 5], ALU.add))
            link(dve.tensor_tensor(tmp[:, 0:nt], tmp[:, 0:nt], tmp[:, 0:nt], ALU.mult))
            link(dve.tensor_scalar(tmp[:, 0:nt], tmp[:, 0:nt], 0.25, None, ALU.mult))
            dve.scalar_tensor_tensor(out=var[:, 0:nt], in0=var[:, 0:nt], scalar=1.0 / D,
                                     in1=tmp[:, 0:nt], op0=ALU.mult, op1=ALU.add).then_inc(s_var, 1)

        def col(t, n):
            return t[:, bass.ds(n, 1)]

        def tile_of(t, n):
            return t[:, bass.ds(n, 1), :].rearrange("p a d -> p (a d)")

        with nc.Block() as block:
            @block.sync
            def _(sp):
                def load(dst_ap, src_ap, s):
                    sp.dma_start(dst_ap, src_ap).then_inc(s, 16)
                for c in range(4):
                    load(xs[:, c * CHUNK:(c + 1) * CHUNK, :], x_v[:, c * CHUNK:(c + 1) * CHUNK, :], s_x[c])
                sp.wait_ge(s_memx, 1)
                load(xs[:, 4 * CHUNK:NT - 1, :], x_v[:, 4 * CHUNK:NT - 1, :], s_x[4])
                load(xs[0:TAIL, NT - 1, :], x[(NT - 1) * P:N, :], s_x[4])
                sp.wait_ge(s_prep, 3)
                for t, a in ((src_i, src.rearrange("(p c) -> p c", c=1)),
                             (dst_i, dst.rearrange("(p c) -> p c", c=1)), (w_e, ew)):
                    load(t[0:P - 1, :], a[0:(P - 1) * COLS, :].rearrange("(p c) o -> p (c o)", c=COLS), s_edge)
                    load(t[P - 1:P, 0:ETAIL], a[(P - 1) * COLS:E, :].rearrange("(p c) o -> p (c o)", c=ETAIL), s_edge)
                sp.wait_ge(s_sentm, 1)
                for c in range(TABLE_W // P):
                    load(table.rearrange("(p c) w -> p (c w)", p=P)[:, c * P:(c + 1) * P], sent[:, :], s_sent)

                def store(n, q):
                    sp.wait_ge(s_hr, n + 1 + CREDIT)
                    sp.dma_start(tile_of(h_v, n), hr[:, q, :]).then_inc(s_hst[q], 16)
                with sp.Fori(0, NT // 2) as it:
                    for q in range(2):
                        store(it * 2 + q, q)
                store(NT - 1, 0)
                sp.wait_ge(s_hst[0], 16 * (NT // 2 + 1))
                sp.wait_ge(s_hst[1], 16 * (NT // 2))
                sp.wait_ge(s_sent, 16 * (TABLE_W // P))
                sp.wait_ge(s_edge, 16 * 6)

            @block.gpsimd
            def _(pool):
                pool.memset(src_i[:, :], 0).then_inc(s_prep, 1)
                pool.memset(dst_i[:, :], PAD_DST).then_inc(s_prep, 1)
                pool.memset(w_e[:, :], 0.0).then_inc(s_prep, 1)
                pool.memset(ident[:, :], 0.0).then_inc(s_memc, 1)
                pool.memset(ones[:, :], 1.0).then_inc(s_memc, 1)
                pool.memset(tri_lt[:, :], 1.0).then_inc(s_memc, 1)
                pool.memset(tri_le[:, :], 1.0).then_inc(s_memc, 1)
                pool.memset(valid[:, :], 1.0).then_inc(s_memc, 1)
                pool.memset(sent[:, :], NOWHERE).then_inc(s_sentm, 1)
                pool.wait_ge(s_memc, 5)
                pool.affine_select(out=ident[:, :], in_=ident[:, :], compare_op=ALU.not_equal, fill=1.0,
                                   base=0, pattern=[[-1, P]], channel_multiplier=1).then_inc(s_const, 1)
                pool.affine_select(out=tri_lt[:, :], in_=tri_lt[:, :], compare_op=ALU.is_gt, fill=0.0,
                                   base=0, pattern=[[1, P]], channel_multiplier=-1).then_inc(s_const, 1)
                pool.affine_select(out=tri_le[:, :], in_=tri_le[:, :], compare_op=ALU.is_ge, fill=0.0,
                                   base=0, pattern=[[1, P]], channel_multiplier=-1).then_inc(s_const, 1)
                pool.affine_select(out=valid[:, :], in_=valid[:, :], compare_op=ALU.is_ge, fill=0.0,
                                   base=N - 1, pattern=[[-P, NT]], channel_multiplier=-1).then_inc(s_const, 1)
                pool.iota(iota_r[:, :], [[1, P]], base=0, channel_multiplier=0,
                          allow_small_or_imprecise_dtypes=True).then_inc(s_const, 1)
                pool.iota(tok_f[:, :], [[P, NT]], base=0, channel_multiplier=1,
                          allow_small_or_imprecise_dtypes=True).then_inc(s_const, 1)
                pool.iota(pcol[:, :], [[0, 1]], base=-1, channel_multiplier=COLS,
                          allow_small_or_imprecise_dtypes=True).then_inc(s_const, 1)

            @block.vector
            def _(dve):
                dve.memset(xs[:, NT - 1:NT + 1, :], 0.0).then_inc(s_memx, 1)
                dve.memset(zrow[:, :], 0.0).then_inc(s_eps, 1)
                dve.memset(eps[:, :], EPS).then_inc(s_eps, 1)
                dve.sem_inc(s_xn, CREDIT)
                dve.sem_inc(s_hs, CREDIT)
                link = linker(dve)
                for c in range(5):
                    dve.wait_ge(s_x[c], 16 if c < 4 else 32)
                    for t in range(c * CHUNK, (c + 1) * CHUNK):
                        dve.bn_stats(st[:, t, :], xs[:, t, :]).then_inc(s_st, 1)
                dve.wait_ge(s_memx, 1)
                dve.bn_stats(st[:, NT, :], xs[:, NT, :]).then_inc(s_st, 1)
                dve.wait_ge(s_st, NT + 1)
                moments(dve, link, NT + 1)
                dve.wait_ge(s_std, 1)
                dve.reciprocal(rstd[:, :], rstd[:, :]).then_inc(s_rstd, 1)
                dve.wait_ge(s_rstd, 1)

                def norm(n, q):
                    dve.wait_ge(s_tps, n - 1 + CREDIT)
                    dve.tensor_scalar(xn[:, q, :], tile_of(xs, n), col(mean, n), col(rstd, n),
                                      ALU.subtract, ALU.mult).then_inc(s_xn, 1)

                def bias(n, q):
                    dve.wait_ge(s_y, n + 1 + CREDIT)
                    dve.wait_ge(s_hr, n - 1 + CREDIT)
                    dve.tensor_tensor(hs[:, q, :], ps[:, 4 + q, 0:D], bp_b[:, :], ALU.add).then_inc(s_hs, 1)
                norm(0, 0)
                norm(1, 1)
                dve.wait_ge(s_ld, 16 * 8)
                with dve.Fori(0, NT // 2) as it:
                    for q in range(2):
                        norm(it * 2 + q + 2, q)
                        bias(it * 2 + q, q)
                bias(NT - 1, 0)

            @block.scalar
            def _(act):
                def load(dst_ap, src_ap):
                    act.dma_start(dst_ap, src_ap).then_inc(s_ld, 16)
                for i, w in enumerate((Wp, Ws, Wn)):
                    load(w_nat[:, i, :, :], w.rearrange("(c p) k -> p c k", p=P))
                load(bp_b[:, :], bp.partition_broadcast(P))
                load(bsn_b[:, 0, :], bs.partition_broadcast(P))
                load(bsn_b[:, 1, :], bn.partition_broadcast(P))
                load(wg_s[:, :, :], Wg.rearrange("(c p) k -> p c k", p=P))
                load(bg_b[:, :], bg.partition_broadcast(P))
                act.sem_inc(s_xT, CREDIT)
                act.sem_inc(s_hr, CREDIT)
                for i, wT in enumerate((wpT, wsT, wnT[:, :, :])):
                    act.wait_ge(s_wps, i + 1)
                    act.activation(wT.rearrange("p b o -> p (b o)"), ps[:, i, :], ACT.Copy).then_inc(s_wT, 1)
                act.wait_ge(s_var, 1)
                act.wait_ge(s_eps, 2)
                act.activation(rstd[:, :], var[:, :], ACT.Sqrt, bias=eps[:, 0:1]).then_inc(s_std, 1)

                def evac(n, q):
                    act.wait_ge(s_tps, n + 1 + CREDIT)
                    act.wait_ge(s_y, n - 1 + CREDIT)
                    act.activation(xT[:, q, :, :].rearrange("p c t -> p (c t)"), ps[:, 6 + q, 0:D],
                                   ACT.Copy).then_inc(s_xT, 1)

                def relu(it, n, q):
                    act.wait_ge(s_hs, n + 1 + CREDIT)
                    act.wait_ge(s_hst[q], 16 * it)
                    act.activation(hr[:, q, :], hs[:, q, :], ACT.Relu).then_inc(s_hr, 1)
                evac(0, 0)
                for it in turns(act, NT // 2):
                    for q in range(2):
                        evac(it * 2 + q + 1, 1 - q)
                        relu(it, it * 2 + q, q)
                relu(NT // 2, NT - 1, 0)

            @block.tensor
            def _(pe):
                pe.sem_inc(s_tps, CREDIT)
                pe.sem_inc(s_y, CREDIT)
                pe.wait_ge(s_ld, 16 * 8)
                pe.wait_ge(s_const, 7)
                for i in range(3):
                    for b in range(KD):
                        for a in range(KD):
                            last = pe.transpose(ps[:, i, b * D + a * P:b * D + (a + 1) * P],
                                                w_nat[:, i, a, b * P:(b + 1) * P], ident[:, :])
                    last.then_inc(s_wps, 1)
                pe.wait_ge(s_wT, 1)

                def turn(n, q):
                    pe.wait_ge(s_xn, n + 1 + CREDIT)
                    pe.wait_ge(s_xT, n - 1 + CREDIT)
                    for c in range(KD):
                        last = pe.transpose(ps[:, 6 + q, c * P:(c + 1) * P], xn[:, q, c * P:(c + 1) * P],
                                            ident[:, :])
                    last.then_inc(s_tps, 1)

                def product(n, q):
                    pe.wait_ge(s_xT, n + 1 + CREDIT)
                    pe.wait_ge(s_hs, n - 1 + CREDIT)
                    for c in range(KD):
                        last = pe.matmul(ps[:, 4 + q, 0:D], xT[:, q, c, :], wpT[:, c, :],
                                         start=(c == 0), stop=(c == KD - 1))
                    last.then_inc(s_y, 1)
                turn(0, 0)
                with pe.Fori(0, NT // 2) as it:
                    for q in range(2):
                        turn(it * 2 + q + 1, 1 - q)
                        product(it * 2 + q, q)
                product(NT - 1, 0)
        s_ep, s_idx = sem("edge_arrays_ready"), sem("group_indices_ready")
        s_gat = sems("rows_gathered", G)
        s_scaled = sem("row_scaled")
        s_fold = sem("running_max_ready")
        s_rst = sems("group_stored", 2)
        s_oh, s_cnt = sem("one_hots_ready"), sem("group_counted")
        s_bxn, s_btp, s_bxT, s_by, s_bx = (sem("base_xn"), sem("base_transposed"), sem("base_xT"),
                                           sem("base_product"), sem("base_ready"))
        s_q, s_q2, s_cb = sem("edges_vector_chain"), sem("base_vector_chain"), sem("counts_cleared")
        s_dg, s_flp, s_ct, s_cs, s_cc, s_cr = (
            sem("diagonals_ready"), sem("first_last_on_rows"), sem("carries_transposed"), sem("carries_scanned"), sem("carries_back"), sem("joined_rows_ready"))
        s_v, s_js, s_fixi = sem("first_ends_gathered"), sem("joined_rows_stored"), sem("first_end_index")
        s_dgr, s_dsum = sem("degrees_ready"), sem("degree_sums_ready")
        qn = [0]
        s_wld, s_wmx, s_wmt, s_wm1, s_wsb, s_wsc, s_whi, s_wlo = (
            sems("weights_loaded", 2), sem("row_maxima"), sem("row_maxima_turned"), sem("chunk_scale"),
            sem("chunk_scale_on_all"), sem("scale_kept"), sems("high_parts_made", 2), sems("low_parts_made", 2))
        s_wsk = sem("inverse_kept")
        EXPONENT = 0xFF << 23
        s_w2s, s_wq = sem("w2_parts_stored"), sem("scale_vector_chain")
        w1_p = arena[:, W1_AT:B1_AT].bitcast(F16).rearrange("p (e a k) -> p e a k", e=NEXP, a=2)
        run_v = run_dram.rearrange("(p t) d -> p t d", t=COLS)
        IOTA_B = iota_r[:, :].unsqueeze(1).to_broadcast([P, G, P])
        IOTA_H = iota_r[:, 0:32].unsqueeze(1).to_broadcast([P, G, 32])

        def groups(eng, body):
            for it in turns(eng, NEXP):
                body(it, True)
            with eng.Fori(NEXP, GROUPS // 2) as it:
                body(it, False)

        with nc.Block() as block:
            @block.sync
            def _(sp):
                def body(it, weights):
                    for k in range(2):
                        g = it * 2 + k
                        if weights:
                            sp.wait_ge(s_wlo[k], it)
                            w = (W1, W2)[k][bass.ds(it, 1)].rearrange("e (c p) h -> p (e c) h", p=P)
                            sp.dma_start(wst[:, k, :].rearrange("p (c h) -> p c h", c=(KD, KH)[k]), w)\
                              .then_inc(s_wld[k], 16)
                        sp.wait_ge(s_fold, g * G + 2 * G)
                        sp.dma_start(run_v[:, bass.ds(g * G, G), :], run[:, k, :, :]).then_inc(s_rst[k], 16)
                        if weights and k == 1:
                            sp.wait_ge(s_wlo[1], it + 1)
                            sp.dma_start(w2_split[bass.ds(it, 1)].rearrange("e p k -> p (e k)"),
                                         w2st.rearrange("p a k -> p (a k)")).then_inc(s_w2s, 16)
                groups(sp, body)
                for k in range(2):
                    sp.wait_ge(s_rst[k], 16 * (GROUPS // 2))
                sp.wait_ge(s_w2s, 16 * NEXP)

            @block.gpsimd
            def _(pool):
                last_h, last_run = pool.to_reg(NT * P - 1), pool.to_reg(P * COLS - 1)
                with pool.Fori(0, GROUPS // 2) as it:
                    for k in range(2):
                        g = it * 2 + k
                        pool.tensor_copy(idxg[:, k, :], src_i[:, bass.ds(g * G, G)]).then_inc(s_idx, 1)
                        pool.wait_ge(s_idx, g + 1)
                        for s in range(G):
                            pool.wait_ge(s_scaled, g * G + s + 1)
                            settle(pool)
                            pool.indirect_dma_start(gath[:, s, :], None, h_dram,
                                                    bass.IndirectOffsetOnAxis(idxg[:, k, s:s + 1], 0),
                                                    bounds_check=last_h, oob_is_err=False)\
                                .then_inc(s_gat[s], 16)
                for k in range(2):
                    pool.wait_ge(s_rst[k], 16 * (GROUPS // 2))
                pool.wait_ge(s_fixi, 1)
                pool.indirect_dma_start(vrow[:, :], None, run_dram, bass.IndirectOffsetOnAxis(fix_i[:, 0:1], 0),
                                        bounds_check=last_run, oob_is_err=False).then_inc(s_v, 16)
                pool.wait_ge(s_cr, 1)
                pool.indirect_dma_start(run_dram, bass.IndirectOffsetOnAxis(fix_i[:, 0:1], 0), vfix[:, :], None,
                                        bounds_check=last_run, oob_is_err=False).then_inc(s_js, 16)
                pool.wait_ge(s_js, 16)

            @block.scalar
            def _(act):
                act.sem_inc(s_scaled, G)
                act.wait_ge(s_ep, 1)

                def body(it, weights):
                    for k in range(2):
                        g = it * 2 + k
                        act.wait_ge(s_rst[k], it * 16)
                        act.wait_ge(s_fold, g * G + 1)
                        for s in range(G):
                            act.wait_ge(s_gat[s], g * 16 + 16)
                            act.activation(run[:, k, s, :], gath[:, s, :], ACT.Copy,
                                           scale=col(w_e, g * G + s)).then_inc(s_scaled, 1)
                            if s == G // 2:
                                act.wait_ge(s_btp, g + 1)
                                act.activation(xT[:, 0, :, :].rearrange("p c t -> p (c t)"), ps[:, 6, 0:D],
                                               ACT.Copy).then_inc(s_bxT, 1)
                        if weights:
                            act.wait_ge(s_wsc, g + 1)
                            if k == 1:
                                act.wait_ge(s_w2s, it * 16)
                            high = w2st[:, 0, :] if k else w1_p[:, bass.ds(it, 1), 0, :].rearrange("p e k -> p (e k)")
                            act.activation(high, wst[:, k, :], ACT.Copy, scale=wsc[:, k, 0:1]).then_inc(s_whi[k], 1)
                groups(act, body)
                act.wait_ge(s_ct, 1)
                act.activation(stT.rearrange("p c t -> p (c t)"), ps[:, 0, 0:D], ACT.Copy).then_inc(s_cc, 1)

            @block.vector
            def _(dve):
                link = linker(dve, s=s_q, count=qn)
                dve.sem_inc(s_fold, G - 1)
                dve.memset(run[:, 1, G - 1, :], 0.0).then_inc(s_fold, 1)
                link(dve.tensor_copy(dst_f[:, :], dst_i[:, :]))
                link(dve.tensor_scalar(part_i[:, :], dst_i[:, :], P - 1, None, ALU.bitwise_and))
                link(dve.tensor_copy(lo_f[:, :], part_i[:, :]))
                link(dve.tensor_scalar(part_i[:, :], dst_i[:, :], 7, None, ALU.arith_shift_right))
                link(dve.tensor_copy(hi_f[:, :], part_i[:, :]))
                link(dve.memset(flag[:, 0:1], NEG))
                link(dve.tensor_tensor(flag[:, 1:COLS], dst_f[:, 1:COLS], dst_f[:, 0:COLS - 1], ALU.not_equal))
                link(dve.tensor_scalar(flag[:, 1:COLS], flag[:, 1:COLS], NEG, None, ALU.mult))
                link(dve.tensor_scalar(first_row[:, :], dst_f[:, :], dst_f[:, 0:1], None, ALU.is_equal))
                link(dve.tensor_reduce(fix_f[:, 0:1], first_row[:, :], AX.X, ALU.add))
                link(dve.tensor_tensor(fix_f[:, 1:2], fix_f[:, 0:1], pcol[:, :], ALU.add))
                link(dve.tensor_copy(fix_i[:, :], fix_f[:, 1:2]))
                dve.tensor_scalar(firstlast[:, 0, :], ident[:, :], dst_f[:, 0:1], None, ALU.mult).then_inc(s_dg, 1)
                dve.tensor_scalar(firstlast[:, 1, :], ident[:, :], dst_f[:, COLS - 1:COLS], None, ALU.mult)\
                   .then_inc(s_dg, 1)
                link(dve.memset(oh_lo[:, 0, :], 0.0))
                dve.memset(oh_hi[:, 0, :], 0.0).then_inc(s_cb, 1)
                dve.wait_ge(s_flp, 1)
                link(dve.tensor_copy(fl_b.rearrange("p a b -> p (a b)"), ps[:, 1, 0:2 * P]))
                link(dve.memset(newseg[:, 0:1], 1.0))
                link(dve.tensor_tensor(newseg[:, 1:P], fl_b[:, 0, 1:P], fl_b[:, 1, 0:P - 1], ALU.not_equal))
                link(dve.tensor_tensor(scanflag[:, :], fl_b[:, 0, :], fl_b[:, 1, :], ALU.not_equal))
                link(dve.tensor_tensor(scanflag[:, :], scanflag[:, :], newseg[:, :], ALU.max))
                link(dve.tensor_scalar(scanflag[:, :], scanflag[:, :], NEG, None, ALU.mult))
                link(dve.tensor_scalar(newseg[:, :], newseg[:, :], NEG, None, ALU.mult))
                link(dve.tensor_tensor(bsn_b[:, 0, :], bsn_b[:, 0, :], bsn_b[:, 1, :], ALU.add))
                dve.wait_ge(s_cb, 2)
                dve.engine_nop().then_inc(s_fixi, 1)
                dve.engine_nop().then_inc(s_ep, 1)

                def chunk_max(it, k):
                    dve.wait_ge(s_wld[k], it * 16 + 16)
                    dve.tensor_reduce(wm[:, k:k + 1], wst[:, k, :], AX.X, ALU.max,
                                      apply_absolute_value=True).then_inc(s_wmx, 1)

                def chunk_scale(it, k):
                    g = it * 2 + k
                    dve.wait_ge(s_wmt, g + 1)
                    dve.tensor_reduce(wm1[:, 0:1], ps[0:1, 5, 0:P], AX.X, ALU.max).then_inc(s_wq, 1)
                    dve.wait_ge(s_wq, g * 3 + 1)
                    dve.tensor_scalar(wm1[:, 1:2], wm1[:, 0:1], 2.0 ** -60, None, ALU.max).then_inc(s_wq, 1)
                    dve.wait_ge(s_wq, g * 3 + 2)
                    dve.tensor_scalar(wm1[:, 0:1].bitcast(I32), wm1[:, 1:2].bitcast(I32), EXPONENT, None,
                                      ALU.bitwise_and).then_inc(s_wq, 1)
                    dve.wait_ge(s_wq, g * 3 + 3)
                    dve.tensor_scalar(sc1[:, k, 0:1].bitcast(I32), wm1[:, 0:1].bitcast(I32), -1.0,
                                      float((2 * 127 + TOP) << 23), ALU.mult, ALU.add).then_inc(s_wm1, 1)
                    dve.tensor_scalar(sc1[:, k, 1:2].bitcast(I32), wm1[:, 0:1].bitcast(I32), -float(TOP << 23),
                                      None, ALU.add).then_inc(s_wm1, 1)

                def chunk_keep(it, k):
                    dve.wait_ge(s_wsb, it * 2 + k + 1)
                    dve.tensor_copy(wsc[:, k, :], ps[:, 7, 0:2]).then_inc(s_wsc, 1)
                    dve.tensor_copy(col((inv1, inv2)[k], it), ps[:, 7, 1:2]).then_inc(s_wsk, 1)

                def chunk_low(it, k):
                    dve.wait_ge(s_whi[k], it + 1)
                    part = [w2st[:, a, :] if k else w1_p[:, bass.ds(it, 1), a, :].rearrange("p e k -> p (e k)")
                            for a in range(2)]
                    dve.scalar_tensor_tensor(out=part[1], in0=wst[:, k, :], scalar=wsc[:, k, 0:1], in1=part[0],
                                             op0=ALU.mult, op1=ALU.subtract).then_inc(s_wlo[k], 1)

                def body(it, weights):
                    for k in range(2):
                        g = it * 2 + k
                        dve.tensor_scalar(xn[:, 0, :], tile_of(xs, g), col(mean, g), col(rstd, g),
                                          ALU.subtract, ALU.mult).then_inc(s_bxn, 1)
                        dve.wait_ge(s_cnt, g)
                        lo = lo_f[:, bass.ds(g * G, G)].unsqueeze(2).to_broadcast([P, G, P])
                        hi = hi_f[:, bass.ds(g * G, G)].unsqueeze(2).to_broadcast([P, G, 32])
                        dve.tensor_tensor(oh_lo, lo, IOTA_B, ALU.is_equal).then_inc(s_oh, 1)
                        dve.tensor_tensor(oh_hi, hi, IOTA_H, ALU.is_equal).then_inc(s_oh, 1)
                        for s in range(G):
                            dve.wait_ge(s_scaled, g * G + s + 1 + G)
                            dve.wait_ge(s_fold, g * G + s + G)
                            before = run[:, k, s - 1, :] if s else run[:, 1 - k, G - 1, :]
                            dve.scalar_tensor_tensor(out=run[:, k, s, :], in0=before,
                                                     scalar=col(flag, g * G + s), in1=run[:, k, s, :],
                                                     op0=ALU.add, op1=ALU.max).then_inc(s_fold, 1)
                            if weights and s == G // 2:
                                chunk_max(it, k)
                            if weights and s == G // 2 + 3:
                                chunk_scale(it, k)
                            if weights and s == G // 2 + 5:
                                chunk_keep(it, k)
                        dve.wait_ge(s_by, g + 1)
                        dve.tensor_tensor(tile_of(xs, g), tile_of(xs, g), ps[:, 4, 0:D], ALU.add)\
                           .then_inc(s_q2, 1)
                        dve.wait_ge(s_q2, g + 1)
                        dve.tensor_tensor(tile_of(xs, g), tile_of(xs, g), bsn_b[:, 0, :], ALU.add)\
                           .then_inc(s_bx, 1)
                        if weights:
                            chunk_low(it, k)
                groups(dve, body)

                dve.wait_ge(s_dgr, 1)
                link(dve.tensor_copy(deg[:, :], ps[:, 2, 0:NT]))
                dve.engine_nop().then_inc(s_dg, 1)
                link(dve.tensor_scalar(dmask[:, :], deg[:, :], 0.0, None, ALU.is_gt))
                dve.wait_ge(s_dsum, 1)
                link(dve.tensor_copy(tmp[:, 0:NT], ps[:, 3, 64:64 + NT]))
                link(dve.memset(end_f[:, :], 0.0))
                link(dve.tensor_tensor_scan(dcum[:, :], tmp[:, 0:NT], end_f[:, :], 0.0, ALU.add, ALU.add))
                link(dve.tensor_tensor(dcum[:, :], dcum[:, :], tmp[:, 0:NT], ALU.subtract))
                link(dve.tensor_tensor(end_f[:, :], dcum[:, :], ps[:, 3, 0:NT], ALU.add))
                link(dve.tensor_scalar(end_f[:, :], end_f[:, :], -1.0, 0.0, ALU.add, ALU.max))
                link(dve.tensor_copy(end_i[:, :], end_f[:, :]))
                dve.wait_ge(s_cc, 1)
                for c in range(KD):
                    link(dve.tensor_tensor_scan(carT[:, c, :], scanflag[:, :], stT[:, c, :], 0.0, ALU.add, ALU.max))
                link(dve.memset(stT[:, :, 0:1], NEG))
                for c in range(KD):
                    link(dve.tensor_tensor(stT[:, c, 1:P], carT[:, c, 0:P - 1], newseg[:, 1:P], ALU.add))
                dve.engine_nop().then_inc(s_cs, 1)
                dve.wait_ge(s_ct, 2)
                dve.wait_ge(s_v, 16)
                dve.tensor_tensor(vfix[:, :], vrow[:, :], ps[:, 1, 0:D], ALU.max).then_inc(s_cr, 1)

            @block.tensor
            def _(pe):
                pe.wait_ge(s_dg, 2)
                pe.matmul(ps[:, 1, 0:2 * P], ones[:, :], firstlast.rearrange("p a b -> p (a b)"),
                          start=True, stop=True).then_inc(s_flp, 1)
                pe.wait_ge(s_cb, 1)
                pe.matmul(ps[:, 2, 0:32], oh_lo[:, 0, :], oh_hi[:, 0, :], start=True, stop=False)\
                  .then_inc(s_cb, 1)

                def body(it, weights):
                    for k in range(2):
                        g = it * 2 + k
                        pe.wait_ge(s_bxn, g + 1)
                        for c in range(KD):
                            last = pe.transpose(ps[:, 6, c * P:(c + 1) * P], xn[:, 0, c * P:(c + 1) * P],
                                                ident[:, :])
                        last.then_inc(s_btp, 1)
                        pe.wait_ge(s_oh, 2 * g + 2)
                        for s in range(G):
                            last = pe.matmul(ps[:, 2, 0:32], oh_lo[:, s, :], oh_hi[:, s, :],
                                             start=False, stop=False)
                        last.then_inc(s_cnt, 1)
                        pe.wait_ge(s_bxT, g + 1)
                        for c in range(KD):
                            last = pe.matmul(ps[:, 4, 0:D], xT[:, 0, c, :], wsT[:, c, :],
                                             start=(c == 0), stop=(c == KD - 1))
                        last.then_inc(s_by, 1)
                        if weights:
                            pe.wait_ge(s_wmx, g + 1)
                            pe.matmul(ps[0:1, 5, 0:P], wm[:, k:k + 1], ident[:, :], start=True, stop=True)\
                              .then_inc(s_wmt, 1)
                            pe.wait_ge(s_wm1, g * 2 + 2)
                            pe.matmul(ps[:, 7, 0:2], ones[0:1, :], sc1[:, k, :], start=True, stop=True)\
                              .then_inc(s_wsb, 1)
                groups(pe, body)
                pe.wait_ge(s_cnt, GROUPS)
                pe.wait_ge(s_bx, GROUPS)
                pe.matmul(ps[:, 2, 0:32], ones[:, :], zrow[:, :], start=False, stop=True).then_inc(s_dgr, 1)
                pe.wait_ge(s_dg, 3)
                pe.matmul(ps[:, 3, 0:NT], tri_le[:, :], deg[:, :], start=True, stop=True)
                pe.matmul(ps[:, 3, 64:64 + NT], ones[:, :], deg[:, :], start=True, stop=True).then_inc(s_dsum, 1)
                pe.wait_ge(s_fold, COLS + G)
                for c in range(KD):
                    last = pe.transpose(ps[:, 0, c * P:(c + 1) * P], run[:, 1, G - 1, c * P:(c + 1) * P],
                                        ident[:, :])
                last.then_inc(s_ct, 1)
                pe.wait_ge(s_cs, 1)
                for c in range(KD):
                    last = pe.transpose(ps[:, 1, c * P:(c + 1) * P], stT[:, c, :], ident[:, :])
                last.then_inc(s_ct, 1)
        s_ei, s_ng = sem("end_index_ready"), sems("neigh_gathered", 2)
        s_ngm, s_ntp, s_nT = sem("neigh_masked"), sem("neigh_transposed"), sem("neighT_ready")
        s_ny, s_x1, s_x1s = sem("neigh_product"), sem("x1_ready"), sem("x1_stored")
        s_var2, s_std2, s_nst = sem("variances2_ready"), sem("deviations2_ready"), sem("statistics2_taken")
        s_x2, s_x2p, s_x2T, s_x2s = sem("x2_ready"), sem("x2_transposed"), sem("x2T_ready"), sems("x2_stored", 2)
        s_gu = sem("gate_product")
        s_gl, s_lg = sem("gate_products"), sem("gate_products_read")
        s_r = sem("routing_vector_chain")
        s_mem, s_rk, s_sl = sem("members_ready"), sem("ranks_ready"), sem("slots_ready")
        s_dif, s_th = sem("top2_difference"), sem("tanh_ready")
        s_sc = sem("entries_scattered")
        s_w, s_b1 = sem("w2_parts_loaded"), sem("expert_biases_loaded")
        s_rc = sem("routing_chain")
        rn, qr = [0], [0]
        ROUTE = 20
        out_v = out[0:(NT - 1) * P, :].rearrange("(t p) d -> p t d", p=P)
        b1_s = arena[:, B1_AT:B2_AT].rearrange("p (e h) -> p e h", e=NEXP)
        b2_s = arena[:, B2_AT:W2_AT].rearrange("p (e d) -> p e d", e=NEXP)
        w2_p = arena[:, W2_AT:ARENA].bitcast(F16).rearrange("p (e k) -> p e k", e=NEXP)
        EARLY = NEXP - LATE

        with nc.Block() as block:
            @block.sync
            def _(sp):
                def store_x1(n):
                    sp.wait_ge(s_x1, n + 1 + CREDIT)
                    sp.dma_start(tile_of(out_v, n), tile_of(xs, n)).then_inc(s_x1s, 16)

                def store_x2(n, q):
                    sp.wait_ge(s_x2, n + 1 + CREDIT)
                    sp.dma_start(tile_of(x2_v, n), xn[:, q, :]).then_inc(s_x2s[q], 16)
                with sp.Fori(0, NT - 1) as n:
                    store_x1(n)
                sp.wait_ge(s_x1, NT + CREDIT)
                sp.dma_start(out[(NT - 1) * P:N, :], xs[0:TAIL, NT - 1, :]).then_inc(s_x1s, 16)
                def load(d, a, s):
                    sp.dma_start(d, a).then_inc(s, 16)
                load(b1_s.rearrange("p e h -> p (e h)"), b1.rearrange("e h -> (e h)").partition_broadcast(P), s_b1)
                load(b2_s.rearrange("p e h -> p (e h)"), b2.rearrange("e h -> (e h)").partition_broadcast(P), s_b1)
                load(w2_p[:, 0:EARLY], w2_split[0:EARLY].rearrange("e p k -> p e k"), s_w)
                with sp.Fori(0, NT // 2) as it:
                    for q in range(2):
                        store_x2(it * 2 + q, q)
                store_x2(NT - 1, 0)
                sp.wait_ge(s_x1s, 16 * NT)
                sp.wait_ge(s_w, 16)
                sp.wait_ge(s_x2s[0], 16 * (NT // 2 + 1))
                sp.wait_ge(s_x2s[1], 16 * (NT // 2))

            @block.gpsimd
            def _(pool):
                last_row = pool.to_reg(P * COLS - 1)

                def neigh(n, q):
                    pool.wait_ge(s_ngm, n - 1 + CREDIT)
                    pool.tensor_copy(ei[:, q:q + 1], col(end_i, n)).then_inc(s_ei, 1)
                    pool.wait_ge(s_ei, n + 1)
                    settle(pool)
                    pool.indirect_dma_start(ng[:, q, :], None, run_dram,
                                            bass.IndirectOffsetOnAxis(ei[:, q:q + 1], 0),
                                            bounds_check=last_row, oob_is_err=False).then_inc(s_ng[q], 16)
                with pool.Fori(0, NT // 2) as it:
                    for q in range(2):
                        neigh(it * 2 + q, q)
                neigh(NT - 1, 0)

                last_entry = pool.to_reg(TABLE - 1)
                with pool.Fori(1, NT // CH + 1) as chunk:
                    pool.wait_ge(s_sl, chunk)
                    settle(pool)
                    for t in range(CH):
                        for c in range(2):
                            pool.indirect_dma_start(table, bass.IndirectOffsetOnAxis(slot_i[:, c, t:t + 1], 0),
                                                    entry[:, c, t, :], None, bounds_check=last_entry,
                                                    oob_is_err=False).then_inc(s_sc, 16)
                pool.wait_ge(s_sc, 16 * 2 * NT)

            @block.scalar
            def _(act):
                act.sem_inc(s_ngm, CREDIT)
                act.sem_inc(s_x2T, CREDIT)

                def mask(it, n, q):
                    act.wait_ge(s_ng[q], it * 16 + 16)
                    act.wait_ge(s_ntp, n - 1 + CREDIT)
                    act.activation(ngm[:, q, :], ng[:, q, :], ACT.Copy, scale=col(dmask, n)).then_inc(s_ngm, 1)
                with act.Fori(0, NT // 2) as it:
                    for q in range(2):
                        mask(it, it * 2 + q, q)
                mask(NT // 2, NT - 1, 0)
                act.wait_ge(s_var2, 1)
                act.activation(rstd[:, 0:NT], var[:, 0:NT], ACT.Sqrt, bias=eps[:, 0:1]).then_inc(s_std2, 1)

                def evac(n, q):
                    act.wait_ge(s_x2p, n + 1 + CREDIT)
                    act.wait_ge(s_gu, n - 1 + CREDIT)
                    act.activation(xT[:, q, :, :].rearrange("p c t -> p (c t)"), ps[:, 6 + q, 0:D],
                                   ACT.Copy).then_inc(s_x2T, 1)

                def chunk_of(chunk, par):
                    for t in range(CH):
                        evac(chunk * CH + t, (par + t) % 2)
                    act.wait_ge(s_dif, chunk + 1)
                    act.activation(th, diff, ACT.Tanh, scale=0.5).then_inc(s_th, 1)
                with act.Fori(0, NT // CH // 2) as it:
                    for par in range(2):
                        chunk_of(it * 2 + par, par)
                chunk_of(NT // CH - 1, 0)

            @block.vector
            def _(dve):
                for s in (s_nT, s_x1, s_x2):
                    dve.sem_inc(s, CREDIT)

                def evac(n, q):
                    dve.wait_ge(s_ntp, n + 1 + CREDIT)
                    dve.wait_ge(s_ny, n - 1 + CREDIT)
                    dve.tensor_copy(xT[:, q, :, :].rearrange("p c t -> p (c t)"), ps[:, 6 + q, 0:D])\
                       .then_inc(s_nT, 1)

                def add(n, q):
                    dve.wait_ge(s_ny, n + 1 + CREDIT)
                    dve.tensor_tensor(tile_of(xs, n), tile_of(xs, n), ps[:, 4 + q, 0:D], ALU.add).then_inc(s_x1, 1)
                    dve.wait_ge(s_x1, n + 1 + CREDIT)
                    dve.bn_stats(st[:, bass.ds(n, 1), :].rearrange("p a b -> p (a b)"), tile_of(xs, n))\
                       .then_inc(s_nst, 1)
                evac(0, 0)
                with dve.Fori(0, NT // 2) as it:
                    for q in range(2):
                        evac(it * 2 + q + 1, 1 - q)
                        add(it * 2 + q, q)
                add(NT - 1, 0)
                dve.wait_ge(s_nst, NT)
                link = linker(dve, s=s_r, count=qr)
                link(dve.tensor_tensor(tmp[:, 0:NT], st[:, 0:NT, 1], st[:, 0:NT, 4], ALU.subtract))
                link(dve.tensor_tensor(mean[:, 0:NT], st[:, 0:NT, 1], st[:, 0:NT, 4], ALU.add))
                link(dve.tensor_scalar(mean[:, 0:NT], mean[:, 0:NT], 0.5, None, ALU.mult))
                link(dve.tensor_tensor(var[:, 0:NT], st[:, 0:NT, 2], st[:, 0:NT, 5], ALU.add))
                link(dve.tensor_tensor(tmp[:, 0:NT], tmp[:, 0:NT], tmp[:, 0:NT], ALU.mult))
                link(dve.tensor_scalar(tmp[:, 0:NT], tmp[:, 0:NT], 0.25, None, ALU.mult))
                dve.scalar_tensor_tensor(out=var[:, 0:NT], in0=var[:, 0:NT], scalar=1.0 / D, in1=tmp[:, 0:NT],
                                         op0=ALU.mult, op1=ALU.add).then_inc(s_var2, 1)
                dve.wait_ge(s_std2, 1)
                link(dve.reciprocal(rstd[:, 0:NT], rstd[:, 0:NT]))

                def norm(it, n, q):
                    dve.wait_ge(s_x2p, n - 1 + CREDIT)
                    dve.wait_ge(s_x2s[q], 16 * it)
                    dve.tensor_scalar(xn[:, q, :], tile_of(xs, n), col(mean, n), col(rstd, n),
                                      ALU.subtract, ALU.mult).then_inc(s_x2, 1)

                iota_e = iota_r[:, 0:NEXP].unsqueeze(1).to_broadcast([P, CH, NEXP])

                def route(chunk):
                    def link(ins):
                        rn[0] += 1
                        ins.then_inc(s_rc, 1)
                        dve.wait_ge(s_rc, chunk * ROUTE + rn[0])
                        settle(dve)
                    rn[0] = 0
                    dve.wait_ge(s_gl, chunk + 1)
                    link(dve.tensor_tensor(lg, ps[:, 4, 0:CH * NEXP].rearrange("p (t e) -> p t e", e=NEXP),
                                           bg_b[:, :].unsqueeze(1).to_broadcast([P, CH, NEXP]), ALU.add))
                    dve.engine_nop().then_inc(s_lg, 1)
                    for t in range(CH):
                        last = dve.max(mx[:, t, :], lg[:, t, :])
                    link(last)
                    for t in range(CH):
                        last = dve.max_index(mi[:, t, :], mx[:, t, :], lg[:, t, :])
                    link(last)
                    dve.tensor_tensor(diff, mx[:, :, 1], mx[:, :, 0], ALU.subtract).then_inc(s_dif, 1)
                    link(dve.tensor_copy(ids, mi[:, :, 0:2]))
                    for c in range(2):
                        last = dve.tensor_tensor(oh[:, c], ids[:, :, c:c + 1].to_broadcast([P, CH, NEXP]), iota_e,
                                                 ALU.is_equal)
                    link(last)
                    link(dve.tensor_tensor(member, oh[:, 0], oh[:, 1], ALU.add))
                    ok = valid[:, bass.ds(chunk * CH, CH)]
                    dve.tensor_tensor(member, member, ok.unsqueeze(2).to_broadcast([P, CH, NEXP]), ALU.mult)\
                       .then_inc(s_mem, 1)
                    link(dve.tensor_scalar(nowhere, ok, -NOWHERE, NOWHERE, ALU.mult, ALU.add))
                    dve.wait_ge(s_rk, chunk + 1)
                    for t in range(CH):
                        link(dve.tensor_tensor(base[:, t + 1, :], base[:, t, :],
                                               ps[:, 3, t * NEXP:(t + 1) * NEXP], ALU.add))
                    link(dve.tensor_tensor(pos, base[:, 0:CH, :],
                                           ps[:, 2, 0:CH * NEXP].rearrange("p (t e) -> p t e", e=NEXP), ALU.add))
                    link(dve.tensor_copy(base[:, 0, :], base[:, CH, :]))
                    for c in range(2):
                        last = dve.tensor_tensor(prod[:, c], oh[:, c], pos, ALU.mult)
                    link(last)
                    for c in range(2):
                        last = dve.tensor_reduce(slot_f[:, c, :], prod[:, c], AX.X, ALU.add)
                    link(last)
                    for c in range(2):
                        last = dve.tensor_tensor(slot_f[:, c, :], slot_f[:, c, :], nowhere, ALU.add)
                    link(last)
                    dve.wait_ge(s_th, chunk + 1)
                    dve.wait_ge(s_sc, chunk * (16 * 2 * CH))
                    link(dve.tensor_copy(slot_i, slot_f))
                    for c in range(2):
                        last = dve.tensor_copy(entry[:, c, :, 0], tok_f[:, bass.ds(chunk * CH, CH)])
                    link(last)
                    link(dve.tensor_scalar(entry[:, 1, :, 1], th, 0.5, 0.5, ALU.mult, ALU.add))
                    dve.tensor_scalar(entry[:, 0, :, 1], entry[:, 1, :, 1], -1.0, 1.0, ALU.mult, ALU.add)\
                       .then_inc(s_sl, 1)
                    assert rn[0] == ROUTE

                link(dve.tensor_scalar(base[:, 0, :], iota_r[:, 0:NEXP], float(CAP), None, ALU.mult))
                norm(0, 0, 0)
                for pair in turns(dve, NT // CH // 2):
                    for par in range(2):
                        for t in range(CH):
                            n = par * CH + t + 1
                            norm(pair * CH + n // 2, pair * (2 * CH) + n, n % 2)
                        route(pair * 2 + par)
                for t in range(CH - 1):
                    norm(NT // 2 - 2 + (t + 1) // 2, NT - CH + t + 1, (t + 1) % 2)
                route(NT // CH - 1)
                dve.wait_ge(s_rc, ROUTE * (NT // CH))
                link(dve.scalar_tensor_tensor(out=tl[:, 0, :], in0=iota_r[0:1, 0:NEXP], scalar=-float(CAP),
                                              in1=base[0:1, 0, :], op0=ALU.mult, op1=ALU.add))
                link(dve.tensor_scalar(tl[:, 0, :], tl[:, 0, :], float(P - 1), None, ALU.add))
                link(dve.tensor_copy(tl_i[:, :], tl[:, 0, :]))
                link(dve.tensor_scalar(tl_i[:, :], tl_i[:, :], 7, None, ALU.arith_shift_right))
                link(dve.tensor_copy(tl[:, 1, :], tl_i[:, :]))
                link(dve.memset(tl[:, 3, :], 0.0))
                link(dve.tensor_tensor_scan(tl[:, 2, :], tl[:, 1, :], tl[:, 3, :], 0.0, ALU.add, ALU.add))
                shape = [1, MOE_TILES, NEXP - 1]
                link(dve.tensor_tensor(m_cmp[0:1, :, 0:NEXP - 1], tl[:, 2:3, 0:NEXP - 1].to_broadcast(shape),
                                       iota_r[0:1, 0:MOE_TILES].unsqueeze(2).to_broadcast(shape), ALU.is_le))
                link(dve.tensor_tensor(m_mul[0:1, :, 0:NEXP - 1], m_cmp[0:1, :, 0:NEXP - 1],
                                       tl[:, 1:2, 0:NEXP - 1].to_broadcast(shape), ALU.mult))
                link(dve.tensor_reduce(tab_f[:, 0, :], m_cmp[0:1, :, 0:NEXP - 1], AX.X, ALU.add))
                link(dve.tensor_reduce(tab_f[:, 1, :], m_mul[0:1, :, 0:NEXP - 1], AX.X, ALU.add))
                link(dve.tensor_tensor(tab_f[:, 1, :], iota_r[0:1, 0:MOE_TILES], tab_f[:, 1, :], ALU.subtract))
                link(dve.tensor_scalar(tab_f[:, 1, :], tab_f[:, 1, :], float(P), None, ALU.mult))
                link(dve.scalar_tensor_tensor(out=tab_f[:, 2, :], in0=tab_f[:, 0, :], scalar=float(CAP),
                                              in1=tab_f[:, 1, :], op0=ALU.mult, op1=ALU.add))
                link(dve.tensor_copy(e_tab[:, :], tab_f[:, 0, :]))
                link(dve.tensor_copy(r_tab[:, :], tab_f[:, 2, :]))
                dve.wait_ge(s_b1, 32)
                link(dve.tensor_reduce(b1max, b1_s, AX.X, ALU.max, apply_absolute_value=True))
                link(dve.scalar_tensor_tensor(out=bnd[:, 0, :], in0=inv1[:, :], scalar=float(D) * 2.0 ** (TOP + 1),
                                              in1=b1max, op0=ALU.mult, op1=ALU.add))
                link(dve.tensor_scalar(bnd[:, 1, :], bnd[:, 0, :], 2.0 ** -60, None, ALU.max))
                link(dve.tensor_scalar(bnd[:, 2, :].bitcast(I32), bnd[:, 1, :].bitcast(I32), EXPONENT, None,
                                       ALU.bitwise_and))
                link(dve.tensor_scalar(sh[:, :].bitcast(I32), bnd[:, 2, :].bitcast(I32), -1.0,
                                       float((2 * 127 + TOP) << 23), ALU.mult, ALU.add))
                link(dve.tensor_scalar(bnd[:, 3, :].bitcast(I32), bnd[:, 2, :].bitcast(I32), -float(TOP << 23), None,
                                       ALU.add))
                link(dve.tensor_scalar(k1[:, :], inv1[:, :], 1.0 / XSCALE, None, ALU.mult))
                link(dve.tensor_tensor(k2[:, :], inv2[:, :], bnd[:, 3, :], ALU.mult))

            @block.tensor
            def _(pe):
                for s in (s_ntp, s_ny, s_x2p, s_gu):
                    pe.sem_inc(s, CREDIT)

                def turn(n, q):
                    pe.wait_ge(s_ngm, n + 1 + CREDIT)
                    pe.wait_ge(s_nT, n - 1 + CREDIT)
                    for c in range(KD):
                        last = pe.transpose(ps[:, 6 + q, c * P:(c + 1) * P], ngm[:, q, c * P:(c + 1) * P],
                                            ident[:, :])
                    last.then_inc(s_ntp, 1)

                def product(n, q):
                    pe.wait_ge(s_nT, n + 1 + CREDIT)
                    pe.wait_ge(s_x1, n - 1 + CREDIT)
                    for c in range(KD):
                        last = pe.matmul(ps[:, 4 + q, 0:D], xT[:, q, c, :], wnT[:, c, :],
                                         start=(c == 0), stop=(c == KD - 1))
                    last.then_inc(s_ny, 1)
                turn(0, 0)
                with pe.Fori(0, NT // 2) as it:
                    for q in range(2):
                        turn(it * 2 + q + 1, 1 - q)
                        product(it * 2 + q, q)
                product(NT - 1, 0)

                def turn2(n, q):
                    pe.wait_ge(s_x2, n + 1 + CREDIT)
                    pe.wait_ge(s_x2T, n - 1 + CREDIT)
                    for c in range(KD):
                        last = pe.transpose(ps[:, 6 + q, c * P:(c + 1) * P], xn[:, q, c * P:(c + 1) * P],
                                            ident[:, :])
                    last.then_inc(s_x2p, 1)

                def gate(n, q, t):
                    pe.wait_ge(s_x2T, n + 1 + CREDIT)
                    for c in range(KD):
                        last = pe.matmul(ps[:, 4, t * NEXP:(t + 1) * NEXP], xT[:, q, c, :], wg_s[:, c, :],
                                         start=(c == 0), stop=(c == KD - 1))
                    last.then_inc(s_gu, 1)

                def chunk_of(chunk, par, final=False):
                    pe.wait_ge(s_lg, chunk + 1)
                    for t in range(CH):
                        n = chunk * CH + t
                        if not (final and t == CH - 1):
                            turn2(n + 1, (par + t + 1) % 2)
                        gate(n, (par + t) % 2, t)
                    pe.wait_ge(s_gu, chunk * CH + CH + CREDIT)
                    pe.sem_inc(s_gl, 1)
                    pe.wait_ge(s_mem, chunk + 1)
                    flat = member.rearrange("p t e -> p (t e)")
                    pe.matmul(ps[:, 2, 0:CH * NEXP], tri_lt[:, :], flat, start=True, stop=True)
                    pe.matmul(ps[:, 3, 0:CH * NEXP], ones[:, :], flat, start=True, stop=True).then_inc(s_rk, 1)
                pe.sem_inc(s_lg, 1)
                pe.wait_ge(s_x1, NT + CREDIT)
                pe.wait_ge(s_nT, NT + CREDIT)
                turn2(0, 0)
                with pe.Fori(0, NT // CH // 2) as it:
                    for par in range(2):
                        chunk_of(it * 2 + par, par)
                chunk_of(NT // CH - 1, 0, True)

        RING = 4
        s_w2 = sem("last_w2_loaded")
        s_tab, s_tok = sems("queue_rows_loaded", RING), sem("tokens_ready")
        s_xg = sems("tokens_gathered", RING)
        s_tok0, s_xp, s_xe, s_hp = sem("token_buffers_cleared"), sem("tokens_transposed"), sem("tokensT_ready"), sem("hidden_product")
        s_pre, s_gel, s_gp = sem("hidden_biased"), sem("hidden_ready"), sem("hidden_transposed")
        s_xh, s_hh, s_hl = sem("tokensT_high"), sem("hiddenT_high"), sem("hiddenT_ready")
        s_yp = sem("out_product")
        s_yb, s_yw, s_add = sem("out_biased"), sem("out_weighted"), sems("out_added", 2)
        at_xs = [0]
        xs_flat = xs[:, :, :].rearrange("p t d -> p (t d)")

        def over_x(*shape, dt=F32):
            n = 1
            for s in shape:
                n *= s
            v = xs_flat[:, at_xs[0]:at_xs[0] + n]
            at_xs[0] += n
            if dt != F32:
                v = v.bitcast(dt)
            if len(shape) == 2:
                v = v.rearrange("p (a b) -> p a b", b=shape[1])
            elif len(shape) == 3:
                v = v.rearrange("p (a b c) -> p a b c", b=shape[1], c=shape[2])
            return v

        rows = over_x(RING, 2)
        toks = over_x(RING, 2, dt=I32)
        tg = over_x(RING, D)
        tgT = over_x(2 * KD * P, dt=F16)\
            .rearrange("p (q a c t) -> p q a c t", q=2, a=2, c=KD)
        pre = over_x(HID)
        hid = over_x(HID)
        hidT = over_x(KH * P, dt=F16).rearrange("p (a c t) -> p a c t", a=2, c=KH)
        yb = over_x(2, D)
        yw = over_x(2, D)
        assert at_xs[0] <= (NT + 1) * D
        XP, HP, GP, YP = 0, 1, 3, 5

        with nc.Block() as block:
            @block.sync
            def _(sp):
                def load_rows(n, u):
                    r = sp.value_load(r_tab[0:1, bass.ds(n, 1)], min_val=0, max_val=TABLE - P)
                    sp.dma_start(rows[:, u, :], table[bass.ds(r, P), :]).then_inc(s_tab[u], 16)
                for u in range(RING):
                    load_rows(u, u)
                with sp.Fori(0, MOE_TILES // RING - 1) as it:
                    for u in range(RING):
                        sp.wait_ge(s_yw, it * RING + u + 1 + CREDIT)
                        settle(sp)
                        sp.wait_ge(s_tok, it * RING + u + 1)
                        settle(sp)
                        load_rows(it * RING + u + RING, u)

            @block.gpsimd
            def _(pool):
                last_tok = pool.to_reg(N - 1)
                pool.memset(tg[:, :, :], 0.0).then_inc(s_tok0, 1)
                pool.wait_ge(s_tok0, 1)

                def gather(it, n, u):
                    pool.wait_ge(s_tab[u], it * 16 + 16)
                    settle(pool)
                    pool.tensor_copy(toks[:, u, 0:1], rows[:, u, 0:1]).then_inc(s_tok, 1)
                    pool.wait_ge(s_xp, n + 1)
                    pool.wait_ge(s_tok, n + 1)
                    settle(pool)
                    pool.indirect_dma_start(tg[:, u, :], None, x2_dram,
                                            bass.IndirectOffsetOnAxis(toks[:, u, 0:1], 0),
                                            bounds_check=last_tok, oob_is_err=False).then_inc(s_xg[u], 16)

                def add_rows(it, n, u):
                    pool.wait_ge(s_yw, n + 1 + CREDIT)
                    pool.wait_ge(s_add[1 - u % 2], it * 32 + (u + 1) // 2 * 16)
                    settle(pool)
                    pool.indirect_dma_start(out, bass.IndirectOffsetOnAxis(toks[:, u, 0:1], 0),
                                            yw[:, u % 2, :], None, bounds_check=last_tok, oob_is_err=False,
                                            compute_op=ALU.add).then_inc(s_add[u % 2], 16)
                for u in range(RING):
                    gather(0, u, u)
                for it in turns(pool, MOE_TILES // RING - 1):
                    for u in range(RING):
                        n = it * RING + u
                        add_rows(it, n, u)
                        pool.wait_ge(s_add[u % 2], it * 32 + u // 2 * 16 + 16)
                        gather(it + 1, n + RING, u)
                for u in range(RING):
                    add_rows(MOE_TILES // RING - 1, MOE_TILES - RING + u, u)
                for q in range(2):
                    pool.wait_ge(s_add[q], MOE_TILES // 2 * 16)

            @block.scalar
            def _(act):
                act.dma_start(w2_p[:, EARLY:NEXP], w2_split[EARLY:NEXP].rearrange("e p k -> p e k"))\
                   .then_inc(s_w2, 16)
                act.sem_inc(s_yw, CREDIT)

                def high_x(n, q):
                    act.wait_ge(s_xp, n + 1 + RING)
                    act.wait_ge(s_hp, 2 * (n - 1 + CREDIT))
                    act.activation(tgT[:, q, 0].rearrange("p c t -> p (c t)"), ps[:, XP, 0:D], ACT.Copy,
                                   scale=XSCALE).then_inc(s_xh, 1)

                def gelu(n):
                    for half in range(2):
                        act.wait_ge(s_pre, 2 * n + half + 1)
                        if half == 0:
                            act.wait_ge(s_gp, 2 * n)
                        act.activation(hid[:, half * 512:(half + 1) * 512], pre[:, half * 512:(half + 1) * 512],
                                       ACT.Gelu).then_inc(s_gel, 1)

                def high_h(n):
                    e = act.value_load(e_tab[0:1, bass.ds(n, 1)], min_val=0, max_val=NEXP - 1)
                    for half in range(2):
                        act.wait_ge(s_gp, 2 * n + half + 1)
                        if half == 0:
                            act.wait_ge(s_yp, n)
                        settle(act)
                        act.activation(hidT[:, 0, half * 4:half * 4 + 4, :].rearrange("p c t -> p (c t)"),
                                       ps[:, GP + half, :], ACT.Copy, scale=col(sh, e)).then_inc(s_hh, 1)

                def weigh(it, n, u):
                    act.wait_ge(s_yb, n + 1)
                    act.wait_ge(s_tab[u], it * 16 + 16)
                    act.wait_ge(s_add[u % 2], it * 32 + u // 2 * 16)
                    act.activation(yw[:, u % 2, :], yb[:, u % 2, :], ACT.Copy,
                                   scale=rows[:, u, 1:2]).then_inc(s_yw, 1)
                high_x(0, 0)
                gelu(0)
                for it in turns(act, MOE_TILES // RING - 1):
                    for u in range(RING):
                        n = it * RING + u
                        high_x(n + 1, 1 - u % 2)
                        high_h(n)
                        gelu(n + 1)
                        weigh(it, n, u)
                for u in range(RING):
                    n = MOE_TILES - RING + u
                    if u < RING - 1:
                        high_x(n + 1, 1 - u % 2)
                    high_h(n)
                    if u < RING - 1:
                        gelu(n + 1)
                    weigh(MOE_TILES // RING - 1, n, u)

            @block.vector
            def _(dve):
                def expert(n):
                    return dve.value_load(e_tab[0:1, bass.ds(n, 1)], min_val=0, max_val=NEXP - 1)

                def low_x(n, q):
                    dve.wait_ge(s_xh, n + 1)
                    dve.scalar_tensor_tensor(out=tgT[:, q, 1].rearrange("p c t -> p (c t)"), in0=ps[:, XP, 0:D],
                                             scalar=XSCALE, in1=tgT[:, q, 0].rearrange("p c t -> p (c t)"),
                                             op0=ALU.mult, op1=ALU.subtract).then_inc(s_xe, 1)

                def bias_h(n, e):
                    for half in range(2):
                        dve.wait_ge(s_hp, 2 * (n + CREDIT) + half + 1)
                        dve.wait_ge(s_gel, 2 * n)
                        b = b1_s[:, bass.ds(e, 1), half * 512:(half + 1) * 512].rearrange("p a h -> p (a h)")
                        dve.scalar_tensor_tensor(out=pre[:, half * 512:(half + 1) * 512], in0=ps[:, HP + half, :],
                                                 scalar=col(k1, e), in1=b, op0=ALU.mult, op1=ALU.add)\
                           .then_inc(s_pre, 1)

                def low_h(n, e):
                    for half in range(2):
                        dve.wait_ge(s_hh, 2 * n + half + 1)
                        part = [hidT[:, a, half * 4:half * 4 + 4, :].rearrange("p c t -> p (c t)") for a in range(2)]
                        dve.scalar_tensor_tensor(out=part[1], in0=ps[:, GP + half, :], scalar=col(sh, e),
                                                 in1=part[0], op0=ALU.mult, op1=ALU.subtract).then_inc(s_hl, 1)

                def bias_y(n, q, e):
                    dve.wait_ge(s_yp, n + 1)
                    dve.wait_ge(s_yw, n - 1 + CREDIT)
                    dve.scalar_tensor_tensor(out=yb[:, q, :], in0=ps[:, YP + q, 0:D], scalar=col(k2, e),
                                             in1=b2_s[:, bass.ds(e, 1), :].rearrange("p a d -> p (a d)"),
                                             op0=ALU.mult, op1=ALU.add).then_inc(s_yb, 1)
                low_x(0, 0)
                bias_h(0, expert(0))
                for it in turns(dve, MOE_TILES // RING - 1):
                    for u in range(RING):
                        n = it * RING + u
                        low_x(n + 1, 1 - u % 2)
                        e, e_next = expert(n), expert(n + 1)
                        low_h(n, e)
                        bias_h(n + 1, e_next)
                        bias_y(n, u % 2, e)
                for u in range(RING):
                    n = MOE_TILES - RING + u
                    if u < RING - 1:
                        low_x(n + 1, 1 - u % 2)
                    e = expert(n)
                    low_h(n, e)
                    if u < RING - 1:
                        bias_h(n + 1, expert(n + 1))
                    bias_y(n, u % 2, e)

            @block.tensor
            def _(pe):
                pe.sem_inc(s_xp, RING)
                pe.sem_inc(s_hp, 2 * CREDIT)

                def turn_x(it, n, u):
                    pe.wait_ge(s_xg[u], it * 16 + 16)
                    pe.wait_ge(s_xe, n)
                    for c in range(KD):
                        last = pe.transpose(ps[:, XP, c * P:(c + 1) * P], tg[:, u, c * P:(c + 1) * P], ident[:, :])
                    last.then_inc(s_xp, 1)

                PASSES = ((0, 0), (0, 1), (1, 0))

                def up(n, q):
                    e = pe.value_load(e_tab[0:1, bass.ds(n, 1)], min_val=0, max_val=NEXP - 1)
                    pe.wait_ge(s_xe, n + 1)
                    pe.wait_ge(s_pre, 2 * n)
                    for half in range(2):
                        for c in range(KD):
                            for a, b in PASSES:
                                w = w1_p[:, bass.ds(e, 1), b, c * HID + half * 512:c * HID + (half + 1) * 512]
                                last = pe.matmul(ps[:, HP + half, :], tgT[:, q, a, c, :],
                                                 w.rearrange("p a h -> p (a h)"), start=(c + a + b == 0),
                                                 stop=(c == KD - 1 and (a, b) == PASSES[-1]))
                        last.then_inc(s_hp, 1)

                def turn_h(n):
                    for half in range(2):
                        pe.wait_ge(s_gel, 2 * n + half + 1)
                        for c in range(4):
                            at = half * 4 + c
                            last = pe.transpose(ps[:, GP + half, c * P:(c + 1) * P], hid[:, at * P:(at + 1) * P],
                                                ident[:, :])
                        last.then_inc(s_gp, 1)

                def down(n, q):
                    e = pe.value_load(e_tab[0:1, bass.ds(n, 1)], min_val=0, max_val=NEXP - 1)
                    pe.wait_ge(s_yw, n - 1 + CREDIT)
                    for c in range(KH):
                        if c % 4 == 0:
                            pe.wait_ge(s_hl, 2 * n + c // 4 + 1)
                        for a, b in PASSES:
                            w = w2_p[:, bass.ds(e, 1), b * WCH + c * D:b * WCH + (c + 1) * D]
                            last = pe.matmul(ps[:, YP + q, 0:D], hidT[:, a, c, :], w.rearrange("p a d -> p (a d)"),
                                             start=(c + a + b == 0), stop=(c == KH - 1 and (a, b) == PASSES[-1]))
                    last.then_inc(s_yp, 1)
                turn_x(0, 0, 0)
                up(0, 0)
                pe.wait_ge(s_w2, 16)
                with pe.Fori(0, MOE_TILES // RING - 1) as it:
                    for u in range(RING):
                        n = it * RING + u
                        turn_x(it + (u + 1) // RING, n + 1, (u + 1) % RING)
                        turn_h(n)
                        up(n + 1, 1 - u % 2)
                        down(n, u % 2)
                for u in range(RING):
                    n = MOE_TILES - RING + u
                    if u < RING - 1:
                        turn_x(MOE_TILES // RING - 1, n + 1, u + 1)
                    turn_h(n)
                    if u < RING - 1:
                        up(n + 1, 1 - u % 2)
                    down(n, u % 2)


_INS = ['x', 'src', 'dst', 'edge_weight1', 'L0_gnn_W_pool', 'L0_gnn_b_pool', 'L0_gnn_W_self', 'L0_gnn_b_self',
        'L0_gnn_W_neigh', 'L0_gnn_b_neigh', 'L0_ffn_Wg', 'L0_ffn_bg', 'L0_ffn_W1', 'L0_ffn_b1', 'L0_ffn_W2',
        'L0_ffn_b2']


def kernel(**inputs):
    import numpy as _np
    import concourse.bacc as _bacc
    from concourse import mybir as _mybir
    from concourse.bass_utils import run_bass_kernel_spmd as _run

    nc = _bacc.Bacc("TRN2", target_bir_lowering=False, num_devices=1)
    arrays, args = {}, []
    for name in _INS:
        a = _np.ascontiguousarray(inputs[name])
        arrays[f"in_{name}_dram"] = a
        args.append(nc.dram_tensor(f"in_{name}_dram", a.shape, _mybir.dt.from_np(a.dtype), kind="ExternalInput").ap())
    args.append(nc.dram_tensor("out_dram", (N, D), F32, kind="ExternalOutput").ap())
    gnn_moe(nc, *args)
    r = _run(nc, [arrays], core_ids=[0])
    return r.results[0]["out_dram"]
```

```python
import concourse.bass as bass
from concourse import mybir
from contextlib import ExitStack

F32 = mybir.dt.float32
BF16 = mybir.dt.bfloat16
F16 = mybir.dt.float16
I32 = mybir.dt.int32
U32 = mybir.dt.uint32
ALU = mybir.AluOpType
ACT = mybir.ActivationFunctionType
AX = mybir.AxisListType

P = 128
N, D = 3125, 256
KD = D // P
NT = -(-N // P)
TAIL = N - (NT - 1) * P
E = 53125
COLS = 416
ETAIL = E - (P - 1) * COLS
G = 16
GROUPS = COLS // G
NEXP, HID = 8, 1024
KH = HID // P
CAP = NT * P
MOE_TILES = (2 * N + NEXP * (P - 1)) // P
QCOLS = NEXP * NT
XW = D + NEXP
SIGN = 2000
XSCALE = 1024.0
TOP = 13
EPS = 1e-5
NEG = -3.0e38
NOWHERE = 1.0e6
PAD_DST = 8191
NG = 4
PIECES = 4
RING = 4
TURNS = MOE_TILES // RING
CREDIT = 2


def gnn_moe(nc, x, src, dst, ew, Wp, bp, Ws, bs, Wn, bn, Wg, bg, W1, b1, W2, b2, out):
    ctx = ExitStack()
    with ctx:
        def sb(name, shape, dt=F32):
            return ctx.enter_context(nc.sbuf_tensor(name, shape, dt))

        def sem(name):
            return ctx.enter_context(nc.semaphore(name))

        def sems(name, n):
            return [sem(f"{name}{i}") for i in range(n)]

        h_dram = nc.dram_tensor("h_rows", (NT * P, D), F32).ap()
        run_dram = nc.dram_tensor("running_max", (P * COLS, D), F32).ap()
        x2_dram = nc.dram_tensor("ffn_in", (NT * P, XW), F32).ap()
        w2_split = nc.dram_tensor("w2_parts", (NEXP, P, 2 * KH * D), F16).ap()

        W1_AT, B1_AT = 0, NEXP * KD * HID
        B2_AT = B1_AT + NEXP * HID
        W2_AT = B2_AT + NEXP * D
        ARENA = W2_AT + NEXP * KH * D
        arena = sb("arena", [P, ARENA])
        at = [B1_AT]

        def carve(shape, dt=F32):
            n = 1
            for s in shape:
                n *= s
            words = n if dt not in (BF16, F16) else n // 2
            v = arena[:, at[0]:at[0] + words]
            at[0] += words
            if dt != F32:
                v = v.bitcast(dt)
            if len(shape) == 2:
                v = v.rearrange("p (a b) -> p a b", b=shape[1])
            elif len(shape) == 3:
                v = v.rearrange("p (a b c) -> p a b c", b=shape[1], c=shape[2])
            return v

        gath = carve([G, D])
        run = carve([2, G, D])
        iota_b = carve([P], BF16)
        oh_lo = carve([G, P], BF16)
        oh_hi = carve([G, 32], BF16)
        src_i = carve([COLS + G], I32)
        dst_i = carve([COLS], I32)
        lo_f = carve([COLS])
        hi_f = carve([COLS], BF16)
        w_e = carve([COLS])
        flag = carve([COLS])
        wsT = carve([KD, D])
        bsn_b = carve([2, D])
        idxg = carve([2, G], I32)
        firstlast = carve([2, P])
        fl_b = carve([2, P])
        newseg = carve([P])
        scanflag = carve([P])
        stT = carve([KD, P])
        carT = carve([KD, P])
        fix_i = carve([1], I32)
        fix_f = carve([4])
        WCH = KD * HID
        wst = carve([2, WCH])
        w2st = carve([2, WCH], F16)
        end_edges = at[0]
        at[0] = B1_AT
        w_nat = carve([3, KD, D])
        wpT = carve([KD, D])
        bp_b = carve([D])
        hs = carve([2, D])
        hr = carve([2, D])
        assert at[0] <= B1_AT + G * D and KH * D == WCH
        at[0] = B1_AT
        vrow = carve([D])
        vfix = carve([D])
        at[0] = B1_AT + G * D
        part_i = carve([COLS], I32)
        dst_f = carve([COLS])
        first_row = carve([COLS])

        MIDDLE, LATE = 2, 1
        at[0] = ARENA - (MIDDLE + LATE) * KH * D
        ng = carve([NG, D])
        x2_ring = ng
        ngm = carve([2, D])
        lg = carve([NT, NEXP])
        mx = carve([NT, NEXP])
        mi = carve([NT, NEXP], U32)
        ids = carve([NT, 2])
        oh = carve([2, NT, NEXP])
        member = carve([NT, NEXP])
        pos = carve([NT, NEXP])
        prod = carve([2, NT, NEXP])
        diff = carve([NT])
        th = carve([NT])
        slot_f = carve([2, NT])
        nowhere = carve([NT])
        slot_i = carve([2, NT], I32)
        half_i = carve([2, 2, NT], I32)
        w12 = carve([2, NT])
        assert at[0] <= ARENA - LATE * KH * D
        at[0] = ARENA - LATE * KH * D
        iota_q = carve([QCOLS], F16)
        zeros_q = carve([QCOLS], F16)
        cum = carve([NEXP, NT])
        half_f = carve([2, 2, NT])
        m_cmp = carve([MOE_TILES, NEXP - 1])
        m_mul = carve([MOE_TILES, NEXP - 1])
        oh_row = carve([4, P], F16)
        oh_col = carve([4, QCOLS], F16)
        end_late = at[0]
        at[0] = ARENA - LATE * KH * D + 5 * NT * 4
        found = carve([QCOLS])
        negative = carve([QCOLS])
        empty = carve([QCOLS])
        assert end_late <= ARENA and at[0] <= end_late - 2 * (P + QCOLS)

        assert end_edges <= ARENA - 4 * D
        at[0] = ARENA - 4 * D
        xn = carve([2, D])
        xT = carve([2, KD, P])

        xs = sb("xs", [P, NT + 1, XW])
        wnT = sb("wnT", [P, KD, D])
        wg_s = sb("wg_s", [P, KD, NEXP])
        bg_b = sb("bg_b", [P, NEXP])
        ident = sb("ident", [P, P])
        ones = sb("ones", [P, P])
        b1_n = sb("b1_n", [NEXP * KH, P])
        b1_row = sb("b1_row", [NEXP * KH, 1])
        b1_diag = sb("b1_diag", [NEXP * KH, NEXP * KH])
        b1max = sb("b1max", [P, NEXP])
        tri_lt = sb("tri_lt", [P, P])
        tri_le = sb("tri_le", [P, P])
        iota_r = sb("iota_r", [P, P])
        tok_f = sb("tok_f", [P, NT])
        valid = sb("valid", [P, NT])
        pcol = sb("pcol", [P, 1])
        eps = sb("eps", [P, 1])
        st = sb("st", [P, NT + 1, 6])
        mean = sb("mean", [P, NT + 1])
        var = sb("var", [P, NT + 1])
        rstd = sb("rstd", [P, NT + 1])
        tmp = sb("tmp", [P, NT + 1])
        deg = sb("deg", [P, NT])
        dmask = sb("dmask", [P, NT])
        dcum = sb("dcum", [P, NT])
        end_f = sb("end_f", [P, NT])
        end_i = sb("end_i", [P, NT], I32)
        ei = sb("ei", [P, 2 * NG], I32)
        wm_p = sb("wm_p", [P, PIECES])
        wm = sb("wm", [P, 2])
        wm1 = sb("wm1", [1, 2])
        sc1 = sb("sc1", [1, 2, 2])
        wsc = sb("wsc", [P, 2, 2])
        inv1 = sb("inv1", [P, NEXP])
        inv2 = sb("inv2", [P, NEXP])
        k1 = sb("k1", [P, NEXP])
        sh = sb("sh", [P, NEXP])
        k2 = sb("k2", [P, NEXP])
        code = sb("code", [P, NT])
        code_2 = sb("code_2", [P, 2, NT])
        distance = sb("distance", [P, 2, P], F16)
        bnd = sb("bnd", [P, 4, NEXP])
        q_tok = sb("q_tok", [P, QCOLS + MOE_TILES], I32)
        zrow = sb("zrow", [P, 32])
        tl = sb("tl", [1, 4, NEXP])
        tl_i = sb("tl_i", [1, NEXP], I32)
        tab_f = sb("tab_f", [1, 2, MOE_TILES])
        tab_e = sb("tab_e", [1, MOE_TILES + RING])
        pack_f = sb("pack_f", [1, TURNS])
        packs = sb("packs", [1, TURNS], I32)
        c_tab = sb("c_tab", [1, MOE_TILES], I32)

        ps = ctx.enter_context(nc.psum_tensor("ps", [P, 8, 512], F32))

        s_memx, s_eps, s_prep = sem("x_tail_zeroed"), sem("eps_set"), sem("edge_pads_set")
        s_const = sem("constants_made")
        s_memc = sem("constants_filled")
        s_st = sem("statistics_taken")
        s_x = sems("x_loaded", 5)
        s_wp, s_ld = sem("pool_weights_loaded"), sem("small_inputs_loaded")
        s_edge = sem("edges_loaded")
        s_wps, s_wT = sem("weights_transposed"), sem("weights_out_of_psum")
        s_var, s_std, s_rstd = sem("variances_ready"), sem("deviations_ready"), sem("rstd_ready")
        s_xn, s_tps, s_xT = sem("xn_ready"), sem("xn_transposed"), sem("xT_ready")
        s_y, s_hs, s_hr = sem("h_product"), sem("h_biased"), sem("h_ready")
        s_hst = sems("h_stored", 2)
        s_dv = sem("vector_chain")
        dv = [0]

        def linker(eng, base=None, s=s_dv, count=dv):
            def link(ins):
                count[0] += 1
                ins.then_inc(s, 1)
                eng.wait_ge(s, count[0] if base is None else base + count[0])
            return link

        s_past = sem("waits_passed")

        def settle(eng):
            eng.sem_inc(s_past, 1)

        def turns(eng, count):
            yield 0
            with eng.Fori(1, count) as it:
                yield it

        CHUNK = NT // 5
        FIRSTS = 2 * CHUNK
        assert 2 * (FIRSTS - 2) == NT + 1 - FIRSTS
        x_v = x[0:(NT - 1) * P, :].rearrange("(t p) d -> p t d", p=P)
        h_v = h_dram.rearrange("(t p) d -> p t d", p=P)
        x2_v = x2_dram.rearrange("(t p) d -> p t d", p=P)

        def moments(dve, link, a, b, ready):
            t, m, v, p = tmp[:, a:b], mean[:, a:b], var[:, a:b], st[:, a:b]
            link(dve.tensor_tensor(t, p[:, :, 1], p[:, :, 4], ALU.subtract))
            link(dve.tensor_tensor(m, p[:, :, 1], p[:, :, 4], ALU.add))
            link(dve.tensor_scalar(m, m, 0.5, None, ALU.mult))
            link(dve.tensor_tensor(v, p[:, :, 2], p[:, :, 5], ALU.add))
            link(dve.tensor_tensor(t, t, t, ALU.mult))
            link(dve.tensor_scalar(t, t, 0.25, None, ALU.mult))
            dve.scalar_tensor_tensor(out=v, in0=v, scalar=1.0 / D, in1=t, op0=ALU.mult, op1=ALU.add)\
               .then_inc(ready, 1)

        def flat(t):
            return t.rearrange("p t e -> p (t e)")

        def col(t, n):
            return t[:, bass.ds(n, 1)]

        def tile_of(t, n):
            return t[:, bass.ds(n, 1), :].rearrange("p a d -> p (a d)")

        def x_tile(n):
            return xs[:, bass.ds(n, 1), 0:D].rearrange("p a d -> p (a d)")

        with nc.Block() as block:
            @block.sync
            def _(sp):
                def load(dst_ap, src_ap, s):
                    sp.dma_start(dst_ap, src_ap).then_inc(s, 16)
                for c in range(4):
                    load(xs[:, c * CHUNK:(c + 1) * CHUNK, 0:D], x_v[:, c * CHUNK:(c + 1) * CHUNK, :], s_x[c])
                sp.wait_ge(s_memx, 1)
                load(xs[:, 4 * CHUNK:NT - 1, 0:D], x_v[:, 4 * CHUNK:NT - 1, :], s_x[4])
                load(xs[0:TAIL, NT - 1, 0:D], x[(NT - 1) * P:N, :], s_x[4])
                sp.wait_ge(s_prep, 3)
                for t, a in ((src_i[:, 0:COLS], src.rearrange("(p c) -> p c", c=1)),
                             (dst_i, dst.rearrange("(p c) -> p c", c=1)), (w_e, ew)):
                    load(t[0:P - 1, :], a[0:(P - 1) * COLS, :].rearrange("(p c) o -> p (c o)", c=COLS), s_edge)
                    load(t[P - 1:P, 0:ETAIL], a[(P - 1) * COLS:E, :].rearrange("(p c) o -> p (c o)", c=ETAIL), s_edge)

                def store(n, q):
                    sp.wait_ge(s_hr, n + 1 + CREDIT)
                    sp.dma_start(tile_of(h_v, n), hr[:, q, :]).then_inc(s_hst[q], 16)
                with sp.Fori(0, NT // 2) as it:
                    for q in range(2):
                        store(it * 2 + q, q)
                store(NT - 1, 0)
                sp.wait_ge(s_hst[0], 16 * (NT // 2 + 1))
                sp.wait_ge(s_hst[1], 16 * (NT // 2))
                sp.wait_ge(s_edge, 16 * 6)

            @block.gpsimd
            def _(pool):
                pool.memset(src_i[:, :], 0).then_inc(s_prep, 1)
                pool.memset(dst_i[:, :], PAD_DST).then_inc(s_prep, 1)
                pool.memset(w_e[:, :], 0.0).then_inc(s_prep, 1)
                pool.memset(ident[:, :], 0.0).then_inc(s_memc, 1)
                pool.memset(ones[:, :], 1.0).then_inc(s_memc, 1)
                pool.memset(tri_lt[:, :], 1.0).then_inc(s_memc, 1)
                pool.memset(tri_le[:, :], 1.0).then_inc(s_memc, 1)
                pool.memset(valid[:, :], 1.0).then_inc(s_memc, 1)
                pool.wait_ge(s_memc, 5)
                pool.affine_select(out=ident[:, :], in_=ident[:, :], compare_op=ALU.not_equal, fill=1.0,
                                   base=0, pattern=[[-1, P]], channel_multiplier=1).then_inc(s_const, 1)
                pool.affine_select(out=tri_lt[:, :], in_=tri_lt[:, :], compare_op=ALU.is_gt, fill=0.0,
                                   base=0, pattern=[[1, P]], channel_multiplier=-1).then_inc(s_const, 1)
                pool.affine_select(out=tri_le[:, :], in_=tri_le[:, :], compare_op=ALU.is_ge, fill=0.0,
                                   base=0, pattern=[[1, P]], channel_multiplier=-1).then_inc(s_const, 1)
                pool.affine_select(out=valid[:, :], in_=valid[:, :], compare_op=ALU.is_ge, fill=0.0,
                                   base=N - 1, pattern=[[-P, NT]], channel_multiplier=-1).then_inc(s_const, 1)
                pool.iota(iota_r[:, :], [[1, P]], base=0, channel_multiplier=0,
                          allow_small_or_imprecise_dtypes=True).then_inc(s_const, 1)
                pool.iota(tok_f[:, :], [[P, NT]], base=0, channel_multiplier=1,
                          allow_small_or_imprecise_dtypes=True).then_inc(s_const, 1)
                pool.iota(pcol[:, :], [[0, 1]], base=-1, channel_multiplier=COLS,
                          allow_small_or_imprecise_dtypes=True).then_inc(s_const, 1)

            @block.vector
            def _(dve):
                dve.memset(xs[:, NT - 1:NT + 1, :], 0.0).then_inc(s_memx, 1)
                dve.memset(zrow[:, :], 0.0).then_inc(s_eps, 1)
                dve.memset(eps[:, :], EPS).then_inc(s_eps, 1)
                dve.sem_inc(s_xn, CREDIT)
                dve.sem_inc(s_hs, CREDIT)
                link = linker(dve)

                def stats(n):
                    dve.bn_stats(st[:, bass.ds(n, 1), :].rearrange("p a b -> p (a b)"), x_tile(n)).then_inc(s_st, 1)

                def statistics(a, b, turn):
                    dve.wait_ge(s_st, b)
                    moments(dve, link, a, b, s_var)
                    dve.wait_ge(s_std, turn)
                    dve.reciprocal(rstd[:, a:b], rstd[:, a:b]).then_inc(s_rstd, 1)
                    dve.wait_ge(s_rstd, turn)
                for c in range(2):
                    dve.wait_ge(s_x[c], 16)
                    for t in range(c * CHUNK, (c + 1) * CHUNK):
                        stats(t)
                statistics(0, FIRSTS, 1)

                def norm(n, q):
                    dve.wait_ge(s_tps, n - 1 + CREDIT)
                    dve.tensor_scalar(xn[:, q, :], x_tile(n), col(mean, n), col(rstd, n),
                                      ALU.subtract, ALU.mult).then_inc(s_xn, 1)

                def bias(n, q):
                    dve.wait_ge(s_y, n + 1 + CREDIT)
                    dve.wait_ge(s_hr, n - 1 + CREDIT)
                    dve.tensor_tensor(hs[:, q, :], ps[:, 4 + q, 0:D], bp_b[:, :], ALU.add).then_inc(s_hs, 1)
                norm(0, 0)
                norm(1, 1)
                dve.wait_ge(s_wp, 32)
                for c in range(2, 5):
                    dve.wait_ge(s_x[c], 16 if c < 4 else 32)
                dve.wait_ge(s_memx, 1)
                with dve.Fori(0, FIRSTS // 2 - 1) as it:
                    for q in range(2):
                        norm(it * 2 + q + 2, q)
                        bias(it * 2 + q, q)
                        stats(it * 4 + 2 * q + FIRSTS)
                        stats(it * 4 + 2 * q + 1 + FIRSTS)
                statistics(FIRSTS, NT + 1, 2)
                with dve.Fori(FIRSTS // 2 - 1, NT // 2) as it:
                    for q in range(2):
                        norm(it * 2 + q + 2, q)
                        bias(it * 2 + q, q)
                bias(NT - 1, 0)

            @block.scalar
            def _(act):
                def load(dst_ap, src_ap):
                    act.dma_start(dst_ap, src_ap).then_inc(s_ld, 16)
                act.dma_start(w_nat[:, 0, :, :], Wp.rearrange("(c p) k -> p c k", p=P)).then_inc(s_wp, 16)
                act.dma_start(bp_b[:, :], bp.partition_broadcast(P)).then_inc(s_wp, 16)
                for i, w in ((1, Ws), (2, Wn)):
                    load(w_nat[:, i, :, :], w.rearrange("(c p) k -> p c k", p=P))
                load(bsn_b[:, 0, :], bs.partition_broadcast(P))
                load(bsn_b[:, 1, :], bn.partition_broadcast(P))
                load(wg_s[:, :, :], Wg.rearrange("(c p) k -> p c k", p=P))
                load(bg_b[:, :], bg.partition_broadcast(P))
                load(b1_n[:, :], b1.rearrange("e (c p) -> (e c) p", p=P))
                act.sem_inc(s_xT, CREDIT)
                act.sem_inc(s_hr, CREDIT)

                def evac_weight(i):
                    act.wait_ge(s_wps, i + 1)
                    wT = (wpT, wsT, wnT[:, :, :])[i]
                    act.activation(wT.rearrange("p b o -> p (b o)"), ps[:, i, :], ACT.Copy).then_inc(s_wT, 1)

                def deviations(a, b, turn):
                    act.wait_ge(s_var, turn)
                    act.activation(rstd[:, a:b], var[:, a:b], ACT.Sqrt, bias=eps[:, 0:1]).then_inc(s_std, 1)
                act.wait_ge(s_eps, 2)
                act.activation(wm[:, 0:1], eps[:, 0:1], ACT.Sqrt)
                evac_weight(0)
                deviations(0, FIRSTS, 1)

                def evac(n, q):
                    act.wait_ge(s_tps, n + 1 + CREDIT)
                    act.wait_ge(s_y, n - 1 + CREDIT)
                    act.activation(xT[:, q, :, :].rearrange("p c t -> p (c t)"), ps[:, 6 + q, 0:D],
                                   ACT.Copy).then_inc(s_xT, 1)

                def relu(it, n, q):
                    act.wait_ge(s_hs, n + 1 + CREDIT)
                    act.wait_ge(s_hst[q], 16 * it)
                    act.activation(hr[:, q, :], hs[:, q, :], ACT.Relu).then_inc(s_hr, 1)
                evac(0, 0)
                for it in turns(act, FIRSTS // 2 - 1):
                    for q in range(2):
                        evac(it * 2 + q + 1, 1 - q)
                        relu(it, it * 2 + q, q)
                deviations(FIRSTS, NT + 1, 2)
                evac_weight(1)
                evac_weight(2)
                with act.Fori(FIRSTS // 2 - 1, NT // 2) as it:
                    for q in range(2):
                        evac(it * 2 + q + 1, 1 - q)
                        relu(it, it * 2 + q, q)
                relu(NT // 2, NT - 1, 0)

            @block.tensor
            def _(pe):
                pe.sem_inc(s_tps, CREDIT)
                pe.sem_inc(s_y, CREDIT)
                def turn_weight(i):
                    for b in range(KD):
                        for a in range(KD):
                            last = pe.transpose(ps[:, i, b * D + a * P:b * D + (a + 1) * P],
                                                w_nat[:, i, a, b * P:(b + 1) * P], ident[:, :])
                    last.then_inc(s_wps, 1)
                pe.wait_ge(s_const, 7)
                pe.wait_ge(s_wp, 32)
                turn_weight(0)
                pe.wait_ge(s_wT, 1)

                def turn(n, q):
                    pe.wait_ge(s_xn, n + 1 + CREDIT)
                    pe.wait_ge(s_xT, n - 1 + CREDIT)
                    for c in range(KD):
                        last = pe.transpose(ps[:, 6 + q, c * P:(c + 1) * P], xn[:, q, c * P:(c + 1) * P],
                                            ident[:, :])
                    last.then_inc(s_tps, 1)

                def product(n, q):
                    pe.wait_ge(s_xT, n + 1 + CREDIT)
                    pe.wait_ge(s_hs, n - 1 + CREDIT)
                    for c in range(KD):
                        last = pe.matmul(ps[:, 4 + q, 0:D], xT[:, q, c, :], wpT[:, c, :],
                                         start=(c == 0), stop=(c == KD - 1))
                    last.then_inc(s_y, 1)
                turn(0, 0)
                with pe.Fori(0, FIRSTS // 2 - 1) as it:
                    for q in range(2):
                        turn(it * 2 + q + 1, 1 - q)
                        product(it * 2 + q, q)
                pe.wait_ge(s_ld, 16 * 7)
                turn_weight(1)
                turn_weight(2)
                with pe.Fori(FIRSTS // 2 - 1, NT // 2) as it:
                    for q in range(2):
                        turn(it * 2 + q + 1, 1 - q)
                        product(it * 2 + q, q)
                product(NT - 1, 0)

        s_ep, s_idx = sem("edge_arrays_ready"), sem("group_indices_ready")
        s_gat = sems("rows_gathered", G)
        s_scaled = sem("row_scaled")
        s_fold = sem("running_max_ready")
        s_rst = sems("group_stored", 2)
        s_oh, s_cnt = sem("one_hots_ready"), sem("group_counted")
        s_bxn, s_btp, s_bxT, s_by, s_bx = (sem("base_xn"), sem("base_transposed"), sem("base_xT"),
                                           sem("base_product"), sem("base_ready"))
        s_q, s_cb = sem("edges_vector_chain"), sem("counts_cleared")
        s_dg, s_flp, s_ct, s_cs, s_cc, s_cr = (
            sem("diagonals_ready"), sem("first_last_on_rows"), sem("carries_transposed"),
            sem("carries_scanned"), sem("carries_back"), sem("joined_rows_ready"))
        s_bd, s_bm = sem("b1_maxima_ready"), sem("b1_maxima_on_all")
        s_v, s_js, s_fixi = sem("first_ends_gathered"), sem("joined_rows_stored"), sem("first_end_index")
        s_dgr, s_dsum = sem("degrees_ready"), sem("degree_sums_ready")
        qn = [0]
        s_wld, s_wmx, s_wmt, s_wm1, s_wsb, s_wsc, s_whi, s_wlo = (
            sems("weights_loaded", 2), sem("row_maxima"), sem("row_maxima_turned"), sem("chunk_scale"),
            sem("chunk_scale_on_all"), sem("scale_kept"), sems("high_parts_made", 2), sems("low_parts_made", 2))
        s_wsk = sem("inverse_kept")
        PIECE = WCH // PIECES
        INDEX_AT, MAX_AT, HIGH_AT, BASE_AT = 1, 7, 8, 11
        PARTS = 4
        STEPS = G // PARTS
        WLINKS = 4
        EXPONENT = 0xFF << 23
        s_w2s, s_wq = sem("w2_parts_stored"), sem("scale_vector_chain")
        w1_p = arena[:, W1_AT:B1_AT].bitcast(F16).rearrange("p (e a k) -> p e a k", e=NEXP, a=2)
        run_v = run_dram.rearrange("(p t) d -> p t d", t=COLS)
        IOTA_H = iota_b[:, 0:32].unsqueeze(1).to_broadcast([P, G, 32])

        FIRST, LAST = 0, NEXP - 1
        BOTH, REST, NONE = 2, 1, 0

        def groups(eng, body):
            for it in turns(eng, NEXP):
                body(it, BOTH)
            body(NEXP, REST)
            with eng.Fori(NEXP + 1, GROUPS // 2) as it:
                body(it, NONE)

        def chunk_in_work(it, k, weights):
            if weights == BOTH:
                return not (it is FIRST and k == 0)
            return weights == REST and k == 0

        with nc.Block() as block:
            @block.sync
            def _(sp):
                def store_w2(it):
                    sp.wait_ge(s_wlo[1], it)
                    sp.dma_start(w2_split[bass.ds(it - 1, 1)].rearrange("e p k -> p (e k)"),
                                 w2st.rearrange("p a k -> p (a k)")).then_inc(s_w2s, 16)

                def load_weights(it, k):
                    sp.wait_ge(s_wlo[k], it)
                    w = (W1, W2)[k][bass.ds(it, 1)].rearrange("e (c p) h -> p (e c) h", p=P)
                    sp.dma_start(wst[:, k, :].rearrange("p (c h) -> p c h", c=(KD, KH)[k]), w)\
                      .then_inc(s_wld[k], 16)

                def body(it, weights):
                    for k in range(2):
                        g = it * 2 + k
                        for part in range(PARTS):
                            sp.wait_ge(s_fold, g * G + G + (part + 1) * STEPS)
                            settle(sp)
                            if part == PARTS - 1 and weights == BOTH and (k == 0 or it is not LAST):
                                load_weights(it + k, 1 - k)
                            sp.dma_start(run_v[:, bass.ds(g * G + part * STEPS, STEPS), :],
                                         run[:, k, part * STEPS:(part + 1) * STEPS, :]).then_inc(s_rst[k], 16)
                        if weights and k == 0 and it is not FIRST:
                            store_w2(it)
                load_weights(0, 0)
                for it in turns(sp, LAST):
                    body(it, BOTH)
                body(LAST, BOTH)
                body(NEXP, REST)
                with sp.Fori(NEXP + 1, GROUPS // 2) as it:
                    body(it, NONE)
                for k in range(2):
                    sp.wait_ge(s_rst[k], 16 * PARTS * (GROUPS // 2))
                sp.wait_ge(s_w2s, 16 * NEXP)

            @block.gpsimd
            def _(pool):
                last_h, last_run = pool.to_reg(NT * P - 1), pool.to_reg(P * COLS - 1)
                pool.tensor_copy(idxg[:, 0, :], src_i[:, 0:G]).then_inc(s_idx, 1)
                with pool.Fori(0, GROUPS // 2) as it:
                    for k in range(2):
                        g = it * 2 + k
                        pool.wait_ge(s_idx, g + 1)
                        for s in range(G):
                            pool.wait_ge(s_scaled, g * G + s + 1)
                            settle(pool)
                            pool.indirect_dma_start(gath[:, s, :], None, h_dram,
                                                    bass.IndirectOffsetOnAxis(idxg[:, k, s:s + 1], 0),
                                                    bounds_check=last_h, oob_is_err=False)\
                                .then_inc(s_gat[s], 16)
                for k in range(2):
                    pool.wait_ge(s_rst[k], 16 * PARTS * (GROUPS // 2))
                pool.wait_ge(s_fixi, 1)
                pool.indirect_dma_start(vrow[:, :], None, run_dram, bass.IndirectOffsetOnAxis(fix_i[:, 0:1], 0),
                                        bounds_check=last_run, oob_is_err=False).then_inc(s_v, 16)
                pool.wait_ge(s_cr, 1)
                pool.indirect_dma_start(run_dram, bass.IndirectOffsetOnAxis(fix_i[:, 0:1], 0), vfix[:, :], None,
                                        bounds_check=last_run, oob_is_err=False).then_inc(s_js, 16)
                pool.wait_ge(s_js, 16)

            @block.scalar
            def _(act):
                act.sem_inc(s_scaled, G)
                act.wait_ge(s_ep, 1)

                def high(e, k):
                    act.wait_ge(s_wsc, e * 2 + k + 1)
                    if k == 1:
                        act.wait_ge(s_w2s, e * 16)
                    part = w2st[:, 0, :] if k else w1_p[:, bass.ds(e, 1), 0, :].rearrange("p e k -> p (e k)")
                    act.activation(part, wst[:, k, :], ACT.Copy, scale=wsc[:, k, 0:1]).then_inc(s_whi[k], 1)

                def body(it, weights):
                    for k in range(2):
                        g = it * 2 + k
                        act.wait_ge(s_rst[k], it * (16 * PARTS))
                        act.wait_ge(s_fold, g * G + 1)
                        for s in range(G):
                            act.wait_ge(s_gat[s], g * 16 + 16)
                            act.activation(run[:, k, s, :], gath[:, s, :], ACT.Copy,
                                           scale=col(w_e, g * G + s)).then_inc(s_scaled, 1)
                            if s == 2:
                                act.wait_ge(s_btp, g + 1)
                                act.activation(xT[:, 0, :, :].rearrange("p c t -> p (c t)"), ps[:, 6, 0:D],
                                               ACT.Copy).then_inc(s_bxT, 1)
                            if s == HIGH_AT and chunk_in_work(it, k, weights):
                                high(it - 1 + k, 1 - k)
                groups(act, body)
                act.wait_ge(s_ct, 1)
                act.activation(stT.rearrange("p c t -> p (c t)"), ps[:, 0, 0:D], ACT.Copy).then_inc(s_cc, 1)

            @block.vector
            def _(dve):
                link = linker(dve, s=s_q, count=qn)
                dve.sem_inc(s_fold, G - 1)
                dve.memset(run[:, 1, G - 1, :], 0.0).then_inc(s_fold, 1)
                link(dve.tensor_copy(dst_f[:, :], dst_i[:, :]))
                link(dve.tensor_copy(iota_b[:, :], iota_r[:, :]))
                link(dve.tensor_reduce(b1_row[:, :], b1_n[:, :], AX.X, ALU.max, apply_absolute_value=True))
                dve.tensor_scalar(b1_diag[:, :], ident[0:NEXP * KH, 0:NEXP * KH], b1_row[:, 0:1], None, ALU.mult)\
                   .then_inc(s_bd, 1)
                link(dve.tensor_scalar(part_i[:, :], dst_i[:, :], P - 1, None, ALU.bitwise_and))
                link(dve.tensor_copy(lo_f[:, :], part_i[:, :]))
                link(dve.tensor_scalar(part_i[:, :], dst_i[:, :], 7, None, ALU.arith_shift_right))
                link(dve.tensor_copy(hi_f[:, :], part_i[:, :]))
                link(dve.memset(flag[:, 0:1], NEG))
                link(dve.tensor_tensor(flag[:, 1:COLS], dst_f[:, 1:COLS], dst_f[:, 0:COLS - 1], ALU.not_equal))
                link(dve.tensor_scalar(flag[:, 1:COLS], flag[:, 1:COLS], NEG, None, ALU.mult))
                link(dve.tensor_scalar(first_row[:, :], dst_f[:, :], dst_f[:, 0:1], None, ALU.is_equal))
                link(dve.tensor_reduce(fix_f[:, 0:1], first_row[:, :], AX.X, ALU.add))
                link(dve.tensor_tensor(fix_f[:, 1:2], fix_f[:, 0:1], pcol[:, :], ALU.add))
                link(dve.tensor_copy(fix_i[:, :], fix_f[:, 1:2]))
                dve.tensor_scalar(firstlast[:, 0, :], ident[:, :], dst_f[:, 0:1], None, ALU.mult).then_inc(s_dg, 1)
                dve.tensor_scalar(firstlast[:, 1, :], ident[:, :], dst_f[:, COLS - 1:COLS], None, ALU.mult)\
                   .then_inc(s_dg, 1)
                link(dve.memset(oh_lo[:, 0, :], 0.0))
                dve.memset(oh_hi[:, 0, :], 0.0).then_inc(s_cb, 1)
                dve.wait_ge(s_flp, 1)
                link(dve.tensor_copy(fl_b.rearrange("p a b -> p (a b)"), ps[:, 1, 0:2 * P]))
                link(dve.memset(newseg[:, 0:1], 1.0))
                link(dve.tensor_tensor(newseg[:, 1:P], fl_b[:, 0, 1:P], fl_b[:, 1, 0:P - 1], ALU.not_equal))
                link(dve.tensor_tensor(scanflag[:, :], fl_b[:, 0, :], fl_b[:, 1, :], ALU.not_equal))
                link(dve.tensor_tensor(scanflag[:, :], scanflag[:, :], newseg[:, :], ALU.max))
                link(dve.tensor_scalar(scanflag[:, :], scanflag[:, :], NEG, None, ALU.mult))
                link(dve.tensor_scalar(newseg[:, :], newseg[:, :], NEG, None, ALU.mult))
                link(dve.tensor_tensor(bsn_b[:, 0, :], bsn_b[:, 0, :], bsn_b[:, 1, :], ALU.add))
                dve.wait_ge(s_bm, 1)
                link(dve.tensor_reduce(b1max[:, :], ps[:, 3, 0:NEXP * KH].rearrange("p (e c) -> p e c", c=KH), AX.X,
                                       ALU.max))
                dve.wait_ge(s_cb, 2)
                dve.engine_nop().then_inc(s_fixi, 1)
                dve.engine_nop().then_inc(s_ep, 1)

                def chunk_max(it, k, i):
                    if i == 0:
                        dve.wait_ge(s_wld[k], it * 16 + 16)
                    last = dve.tensor_reduce(wm_p[:, i:i + 1], wst[:, k, i * PIECE:(i + 1) * PIECE], AX.X, ALU.max,
                                             apply_absolute_value=True)
                    if i == PIECES - 1:
                        last.then_inc(s_wq, 1)

                def chunk_rows(it, k):
                    dve.wait_ge(s_wq, (it * 2 + k) * WLINKS + 1)
                    dve.tensor_reduce(wm[:, k:k + 1], wm_p[:, :], AX.X, ALU.max).then_inc(s_wmx, 1)

                def chunk_top(it, k):
                    dve.wait_ge(s_wmt, it * 2 + k + 1)
                    dve.tensor_reduce(wm1[:, 0:1], ps[0:1, 5, 0:P], AX.X, ALU.max).then_inc(s_wq, 1)

                def chunk_floor(it, k):
                    dve.wait_ge(s_wq, (it * 2 + k) * WLINKS + 2)
                    dve.tensor_scalar(wm1[:, 1:2], wm1[:, 0:1], 2.0 ** -60, None, ALU.max).then_inc(s_wq, 1)

                def chunk_exponent(it, k):
                    dve.wait_ge(s_wq, (it * 2 + k) * WLINKS + 3)
                    dve.tensor_scalar(wm1[:, 0:1].bitcast(I32), wm1[:, 1:2].bitcast(I32), EXPONENT, None,
                                      ALU.bitwise_and).then_inc(s_wq, 1)

                def chunk_scale(it, k):
                    dve.wait_ge(s_wq, (it * 2 + k) * WLINKS + 4)
                    dve.tensor_scalar(sc1[:, k, 0:1].bitcast(I32), wm1[:, 0:1].bitcast(I32), -1.0,
                                      float((2 * 127 + TOP) << 23), ALU.mult, ALU.add).then_inc(s_wm1, 1)
                    dve.tensor_scalar(sc1[:, k, 1:2].bitcast(I32), wm1[:, 0:1].bitcast(I32), -float(TOP << 23),
                                      None, ALU.add).then_inc(s_wm1, 1)

                def chunk_keep(it, k):
                    dve.wait_ge(s_wsb, it * 2 + k + 1)
                    dve.tensor_copy(wsc[:, k, :], ps[:, 7, 0:2]).then_inc(s_wsc, 1)
                    dve.tensor_copy(col((inv1, inv2)[k], it), ps[:, 7, 1:2]).then_inc(s_wsk, 1)

                def chunk_low(it, k, i):
                    if i == 0:
                        dve.wait_ge(s_whi[k], it + 1)
                    at = slice(i * PIECE, (i + 1) * PIECE)
                    part = [w2st[:, a, at] if k else w1_p[:, bass.ds(it, 1), a, at].rearrange("p e k -> p (e k)")
                            for a in range(2)]
                    last = dve.scalar_tensor_tensor(out=part[1], in0=wst[:, k, at], scalar=wsc[:, k, 0:1],
                                                    in1=part[0], op0=ALU.mult, op1=ALU.subtract)
                    if i == PIECES - 1:
                        last.then_inc(s_wlo[k], 1)

                def this_chunk(it, k, s):
                    if MAX_AT <= s < MAX_AT + PIECES:
                        chunk_max(it, k, s - MAX_AT)
                    elif s == G - 3:
                        chunk_rows(it, k)
                    elif s == G - 1:
                        chunk_top(it, k)

                def chunk_before(it, k, s):
                    if s in (0, 1, 2, 5):
                        {0: chunk_floor, 1: chunk_exponent, 2: chunk_scale, 5: chunk_keep}[s](it, k)
                    elif s >= G - PIECES:
                        chunk_low(it, k, s - (G - PIECES))

                def body(it, weights):
                    for k in range(2):
                        g = it * 2 + k
                        dve.tensor_scalar(xn[:, 0, :], x_tile(g), col(mean, g), col(rstd, g),
                                          ALU.subtract, ALU.mult).then_inc(s_bxn, 1)
                        for s in range(G):
                            dve.wait_ge(s_scaled, g * G + s + 1 + G)
                            dve.wait_ge(s_fold, g * G + s + G)
                            before = run[:, k, s - 1, :] if s else run[:, 1 - k, G - 1, :]
                            dve.scalar_tensor_tensor(out=run[:, k, s, :], in0=before,
                                                     scalar=col(flag, g * G + s), in1=run[:, k, s, :],
                                                     op0=ALU.add, op1=ALU.max).then_inc(s_fold, 1)
                            if s == INDEX_AT:
                                dve.tensor_copy(idxg[:, 1 - k, :], src_i[:, bass.ds(g * G + G, G)])\
                                   .then_inc(s_idx, 1)
                            if s == 0:
                                dve.wait_ge(s_cnt, g)
                                hi = hi_f[:, bass.ds(g * G, G)].unsqueeze(2).to_broadcast([P, G, 32])
                                dve.tensor_tensor(oh_hi, hi, IOTA_H, ALU.is_equal)
                            last = dve.tensor_scalar(oh_lo[:, s, :], iota_b[:, :], col(lo_f, g * G + s), None,
                                                     ALU.is_equal)
                            if s == G - 1:
                                last.then_inc(s_oh, 1)
                            if weights == BOTH:
                                this_chunk(it, k, s)
                            if chunk_in_work(it, k, weights):
                                chunk_before(it - 1 + k, 1 - k, s)
                            if s == BASE_AT:
                                dve.wait_ge(s_by, g + 1)
                                dve.tensor_tensor(x_tile(g), x_tile(g), ps[:, 4, 0:D], ALU.add)\
                                   .then_inc(s_bx, 1)

                groups(dve, body)

                dve.wait_ge(s_cc, 1)
                for c in range(KD):
                    link(dve.tensor_tensor_scan(carT[:, c, :], scanflag[:, :], stT[:, c, :], 0.0, ALU.add, ALU.max))
                link(dve.memset(stT[:, :, 0:1], NEG))
                for c in range(KD):
                    link(dve.tensor_tensor(stT[:, c, 1:P], carT[:, c, 0:P - 1], newseg[:, 1:P], ALU.add))
                dve.engine_nop().then_inc(s_cs, 1)
                dve.wait_ge(s_dgr, 1)
                link(dve.tensor_copy(deg[:, :], ps[:, 2, 0:NT]))
                dve.engine_nop().then_inc(s_dg, 1)
                link(dve.tensor_scalar(dmask[:, :], deg[:, :], 0.0, None, ALU.is_gt))
                dve.wait_ge(s_dsum, 1)
                link(dve.tensor_copy(tmp[:, 0:NT], ps[:, 3, 64:64 + NT]))
                link(dve.memset(end_f[:, :], 0.0))
                link(dve.tensor_tensor_scan(dcum[:, :], tmp[:, 0:NT], end_f[:, :], 0.0, ALU.add, ALU.add))
                link(dve.tensor_tensor(dcum[:, :], dcum[:, :], tmp[:, 0:NT], ALU.subtract))
                link(dve.tensor_tensor(end_f[:, :], dcum[:, :], ps[:, 3, 0:NT], ALU.add))
                link(dve.tensor_scalar(end_f[:, :], end_f[:, :], -1.0, 0.0, ALU.add, ALU.max))
                link(dve.tensor_copy(end_i[:, :], end_f[:, :]))
                dve.wait_ge(s_ct, 2)
                dve.wait_ge(s_v, 16)
                dve.tensor_tensor(vfix[:, :], vrow[:, :], ps[:, 1, 0:D], ALU.max).then_inc(s_cr, 1)
                link(dve.scalar_tensor_tensor(out=bnd[:, 0, :], in0=inv1[:, :], scalar=float(D) * 2.0 ** (TOP + 1),
                                              in1=b1max[:, :], op0=ALU.mult, op1=ALU.add))
                link(dve.tensor_scalar(bnd[:, 1, :], bnd[:, 0, :], 2.0 ** -60, None, ALU.max))
                link(dve.tensor_scalar(bnd[:, 2, :].bitcast(I32), bnd[:, 1, :].bitcast(I32), EXPONENT, None,
                                       ALU.bitwise_and))
                link(dve.tensor_scalar(sh[:, :].bitcast(I32), bnd[:, 2, :].bitcast(I32), -1.0,
                                       float((2 * 127 + TOP) << 23), ALU.mult, ALU.add))
                link(dve.tensor_scalar(bnd[:, 3, :].bitcast(I32), bnd[:, 2, :].bitcast(I32), -float(TOP << 23), None,
                                       ALU.add))
                link(dve.tensor_scalar(k1[:, :], inv1[:, :], 1.0 / XSCALE, None, ALU.mult))
                link(dve.tensor_tensor(k2[:, :], inv2[:, :], bnd[:, 3, :], ALU.mult))
                link(dve.tensor_scalar(code[:, :], tok_f[:, :], 1.0, None, ALU.add))
                link(dve.tensor_scalar(code_2[:, 0], code[:, :], float(SIGN), None, ALU.is_gt))
                link(dve.tensor_scalar(code_2[:, 1], code[:, :], -2.0, float(SIGN), ALU.mult, ALU.add))
                link(dve.tensor_tensor(code_2[:, 0], code_2[:, 0], code_2[:, 1], ALU.mult))
                link(dve.tensor_tensor(code[:, :], code[:, :], code_2[:, 0], ALU.add))

            @block.tensor
            def _(pe):
                pe.wait_ge(s_bd, 1)
                pe.matmul(ps[:, 3, 0:NEXP * KH], ones[0:NEXP * KH, :], b1_diag[:, :], start=True, stop=True)\
                  .then_inc(s_bm, 1)
                pe.wait_ge(s_dg, 2)
                pe.matmul(ps[:, 1, 0:2 * P], ones[:, :], firstlast.rearrange("p a b -> p (a b)"),
                          start=True, stop=True).then_inc(s_flp, 1)
                pe.wait_ge(s_cb, 1)
                pe.matmul(ps[:, 2, 0:32], oh_lo[:, 0, :], oh_hi[:, 0, :], start=True, stop=False)\
                  .then_inc(s_cb, 1)

                def spread(e, k):
                    pe.wait_ge(s_wm1, (e * 2 + k) * 2 + 2)
                    pe.matmul(ps[:, 7, 0:2], ones[0:1, :], sc1[:, k, :], start=True, stop=True).then_inc(s_wsb, 1)

                def body(it, weights):
                    for k in range(2):
                        g = it * 2 + k
                        pe.wait_ge(s_bxn, g + 1)
                        for c in range(KD):
                            last = pe.transpose(ps[:, 6, c * P:(c + 1) * P], xn[:, 0, c * P:(c + 1) * P],
                                                ident[:, :])
                        last.then_inc(s_btp, 1)
                        pe.wait_ge(s_bxT, g + 1)
                        for c in range(KD):
                            pe.matmul(ps[:, 4, 0:D], xT[:, 0, c, :], wsT[:, c, :], start=(c == 0), stop=False)
                        pe.matmul(ps[:, 4, 0:D], ones[0:1, :], bsn_b[0:1, 0, :], start=False, stop=True)\
                          .then_inc(s_by, 1)
                        if chunk_in_work(it, k, weights):
                            spread(it - 1 + k, 1 - k)
                        if weights == BOTH:
                            pe.wait_ge(s_wmx, g + 1)
                            pe.matmul(ps[0:1, 5, 0:P], wm[:, k:k + 1], ident[:, :], start=True, stop=True)\
                              .then_inc(s_wmt, 1)
                        pe.wait_ge(s_oh, g + 1)
                        for s in range(G):
                            last = pe.matmul(ps[:, 2, 0:32], oh_lo[:, s, :], oh_hi[:, s, :],
                                             start=False, stop=False)
                        last.then_inc(s_cnt, 1)
                groups(pe, body)
                pe.wait_ge(s_fold, COLS + G)
                for c in range(KD):
                    last = pe.transpose(ps[:, 0, c * P:(c + 1) * P], run[:, 1, G - 1, c * P:(c + 1) * P],
                                        ident[:, :])
                last.then_inc(s_ct, 1)
                pe.wait_ge(s_cs, 1)
                for c in range(KD):
                    last = pe.transpose(ps[:, 1, c * P:(c + 1) * P], stT[:, c, :], ident[:, :])
                last.then_inc(s_ct, 1)
                pe.wait_ge(s_cnt, GROUPS)
                pe.wait_ge(s_bx, GROUPS)
                pe.matmul(ps[:, 2, 0:32], ones[:, :], zrow[:, :], start=False, stop=True).then_inc(s_dgr, 1)
                pe.wait_ge(s_dg, 3)
                pe.matmul(ps[:, 3, 0:NT], tri_le[:, :], deg[:, :], start=True, stop=True)
                pe.matmul(ps[:, 3, 64:64 + NT], ones[:, :], deg[:, :], start=True, stop=True).then_inc(s_dsum, 1)
        s_ei, s_ng = sem("end_index_ready"), sems("neigh_gathered", NG)
        s_ngm, s_ntp, s_nT = sem("neigh_masked"), sem("neigh_transposed"), sem("neighT_ready")
        s_ny, s_x1, s_x1s = sem("neigh_product"), sem("x1_ready"), sem("x1_stored")
        s_nst, s_var2, s_std2 = sem("statistics2_taken"), sem("variances2_ready"), sem("deviations2_ready")
        s_x2, s_x2k = sem("x2_ready"), sem("x2_kept")
        s_x2p, s_x2T, s_x2s = sem("x2_transposed"), sem("x2T_ready"), sem("x2_stored")
        s_gu = sem("gate_product")
        s_r = sem("routing_vector_chain")
        s_dif, s_th, s_wd = sem("top2_difference"), sem("tanh_ready"), sem("dense_weights_ready")
        s_mem, s_rk = sem("members_ready"), sem("ranks_ready")
        s_hf, s_ds, s_or = sem("slot_halves_ready"), sem("distances_ready"), sem("row_one_hots_ready")
        s_z, s_oq, s_qm, s_qd = (sem("queue_constants_ready"), sem("queue_one_hots_ready"), sem("queue_product"),
                                 sem("queues_complete"))
        s_w = sem("expert_inputs_loaded")
        qr = [0]
        out_v = out[0:(NT - 1) * P, :].rearrange("(t p) d -> p t d", p=P)
        b1_s = arena[:, B1_AT:B2_AT].rearrange("p (e h) -> p e h", e=NEXP)
        b2_s = arena[:, B2_AT:W2_AT].rearrange("p (e d) -> p e d", e=NEXP)
        w2_p = arena[:, W2_AT:ARENA].bitcast(F16).rearrange("p (e k) -> p e k", e=NEXP)
        EARLY = NEXP - MIDDLE - LATE
        TG, TR, TT, TQ = 2, 3, 1, 0

        with nc.Block() as block:
            @block.sync
            def _(sp):
                def store_x1(n):
                    sp.wait_ge(s_x1, n + 1 + CREDIT)
                    sp.dma_start(tile_of(out_v, n), x_tile(n)).then_inc(s_x1s, 16)

                def load(d, a, s):
                    sp.dma_start(d, a).then_inc(s, 16)
                with sp.Fori(0, NT - 1) as n:
                    store_x1(n)
                sp.wait_ge(s_x1, NT + CREDIT)
                sp.dma_start(out[(NT - 1) * P:N, :], xs[0:TAIL, NT - 1, 0:D]).then_inc(s_x1s, 16)
                load(b1_s.rearrange("p e h -> p (e h)"), b1.rearrange("e h -> (e h)").partition_broadcast(P), s_w)
                load(b2_s.rearrange("p e h -> p (e h)"), b2.rearrange("e h -> (e h)").partition_broadcast(P), s_w)
                load(w2_p[:, 0:EARLY], w2_split[0:EARLY].rearrange("e p k -> p e k"), s_w)
                sp.wait_ge(s_x2k, NT + NG)
                sp.wait_ge(s_wd, 1)
                sp.dma_start(x2_v, xs[:, 0:NT, :]).then_inc(s_x2s, 16)
                sp.wait_ge(s_hf, 1)
                load(w2_p[:, EARLY:NEXP - LATE], w2_split[EARLY:NEXP - LATE].rearrange("e p k -> p e k"), s_w)
                sp.wait_ge(s_w, 64)
                sp.wait_ge(s_x2s, 16)

            @block.gpsimd
            def _(pool):
                last_row = pool.to_reg(P * COLS - 1)
                pool.memset(zeros_q, 0.0).then_inc(s_z, 1)

                def indices(n, half, count):
                    pool.wait_ge(s_ngm, n + 1)
                    settle(pool)
                    pool.tensor_copy(ei[:, half * NG:half * NG + count], end_i[:, bass.ds(n, count)])\
                        .then_inc(s_ei, 1)

                def neigh(n, u):
                    pool.wait_ge(s_ngm, n + 1)
                    settle(pool)
                    pool.indirect_dma_start(ng[:, u % NG, :], None, run_dram,
                                            bass.IndirectOffsetOnAxis(ei[:, u:u + 1], 0),
                                            bounds_check=last_row, oob_is_err=False).then_inc(s_ng[u % NG], 16)
                with pool.Fori(0, NT // (2 * NG)) as it:
                    for half in range(2):
                        n = it * 2 * NG + half * NG
                        indices(n, half, NG)
                        pool.wait_ge(s_ei, it * 2 + half + 1)
                        settle(pool)
                        for u in range(NG):
                            neigh(n + u, half * NG + u)
                indices(NT - 1, 0, 1)
                pool.wait_ge(s_ei, NT // NG + 1)
                neigh(NT - 1, 0)
                pool.iota(iota_q, [[1, QCOLS]], base=0, channel_multiplier=0,
                          allow_small_or_imprecise_dtypes=True).then_inc(s_z, 1)

            @block.scalar
            def _(act):
                act.sem_inc(s_ngm, NG)
                act.sem_inc(s_nT, CREDIT)
                act.sem_inc(s_x2T, NG)
                act.sem_inc(s_x2k, NG)

                def mask(it, n, u):
                    act.wait_ge(s_ng[u], it * 16 + 16)
                    act.wait_ge(s_ntp, n - 1 + CREDIT)
                    act.activation(ngm[:, u % 2, :], ng[:, u, :], ACT.Copy, scale=col(dmask, n)).then_inc(s_ngm, 1)

                def evac_n(n, q):
                    act.wait_ge(s_ntp, n + 1 + CREDIT)
                    act.wait_ge(s_ny, n - 1 + CREDIT)
                    act.activation(xT[:, q, :, :].rearrange("p c t -> p (c t)"), ps[:, 6 + q, 0:D],
                                   ACT.Copy).then_inc(s_nT, 1)
                mask(0, 0, 0)
                with act.Fori(0, NT // NG) as it:
                    for u in range(NG):
                        n = it * NG + u
                        mask(it + (u + 1) // NG, n + 1, (u + 1) % NG)
                        evac_n(n, u % 2)
                evac_n(NT - 1, 0)
                act.wait_ge(s_var2, 1)
                act.activation(rstd[:, 0:NT], var[:, 0:NT], ACT.Sqrt, bias=eps[:, 0:1]).then_inc(s_std2, 1)

                def evac_x2(n, u):
                    act.wait_ge(s_x2p, n + 1)
                    act.wait_ge(s_gu, n - 1 + CREDIT)
                    act.activation(xT[:, u % 2, :, :].rearrange("p c t -> p (c t)"), ps[:, 4 + u, 0:D],
                                   ACT.Copy).then_inc(s_x2T, 1)
                    act.activation(x_tile(n), x2_ring[:, u, :], ACT.Copy).then_inc(s_x2k, 1)
                act.wait_ge(s_x1s, 16 * NT)
                with act.Fori(0, NT // NG) as it:
                    for u in range(NG):
                        evac_x2(it * NG + u, u)
                evac_x2(NT - 1, 0)
                act.wait_ge(s_dif, 1)
                act.activation(th, diff, ACT.Tanh, scale=0.5).then_inc(s_th, 1)

                def row_one_hot(n, turn):
                    act.activation(distance[:, turn, :], iota_q[:, 0:P], ACT.Abs, scale=-1.0,
                                   bias=col(half_f[:, 0, 1], n)).then_inc(s_ds, 1)
                    act.wait_ge(s_ds, n + 1)
                    act.activation(oh_row[:, turn * 2 + 1, :], distance[:, turn, :], ACT.Relu, scale=-1.0,
                                   bias=ones[:, 0:1]).then_inc(s_or, 1)
                act.wait_ge(s_hf, 1)
                act.wait_ge(s_z, 2)
                for it in turns(act, NT // 2):
                    for q in range(2):
                        if it is not FIRST:
                            act.wait_ge(s_qm, it * 2 + q - 1)
                        settle(act)
                        row_one_hot(it * 2 + q, q)
                act.wait_ge(s_qm, NT - 2)
                row_one_hot(NT - 1, 0)

            @block.vector
            def _(dve):
                dve.sem_inc(s_x1, CREDIT)

                def add(n, q):
                    dve.wait_ge(s_ny, n + 1 + CREDIT)
                    dve.tensor_tensor(x_tile(n), x_tile(n), ps[:, 4 + q, 0:D], ALU.add).then_inc(s_x1, 1)
                    dve.wait_ge(s_x1, n + 1 + CREDIT)
                    dve.bn_stats(st[:, bass.ds(n, 1), :].rearrange("p a b -> p (a b)"), x_tile(n))\
                       .then_inc(s_nst, 1)
                with dve.Fori(0, NT // 2) as it:
                    for q in range(2):
                        add(it * 2 + q, q)
                add(NT - 1, 0)
                dve.wait_ge(s_nst, NT)
                link = linker(dve, s=s_r, count=qr)
                moments(dve, link, 0, NT, s_var2)
                dve.wait_ge(s_std2, 1)
                link(dve.reciprocal(rstd[:, 0:NT], rstd[:, 0:NT]))

                def norm(n, u):
                    dve.wait_ge(s_x2k, n + 1)
                    dve.tensor_scalar(x2_ring[:, u, :], x_tile(n), col(mean, n), col(rstd, n),
                                      ALU.subtract, ALU.mult).then_inc(s_x2, 1)
                dve.wait_ge(s_ngm, NT + NG)
                with dve.Fori(0, NT // NG) as it:
                    for u in range(NG):
                        norm(it * NG + u, u)
                norm(NT - 1, 0)
                ok = valid[:, 0:NT]
                link(dve.tensor_scalar(nowhere, ok, -NOWHERE, NOWHERE, ALU.mult, ALU.add))

                def by_tile(t):
                    return t.rearrange("p (t e) -> p t e", e=NEXP)
                each = [P, NT, NEXP]
                dve.wait_ge(s_gu, NT + CREDIT)
                link(dve.tensor_tensor(lg, by_tile(ps[:, TG, 0:QCOLS]), bg_b[:, :].unsqueeze(1).to_broadcast(each),
                                       ALU.add))
                for t in range(NT):
                    last = dve.max(mx[:, t, :], lg[:, t, :])
                link(last)
                for t in range(NT):
                    last = dve.max_index(mi[:, t, :], mx[:, t, :], lg[:, t, :])
                link(last)
                dve.tensor_tensor(diff, mx[:, :, 1], mx[:, :, 0], ALU.subtract).then_inc(s_dif, 1)
                link(dve.tensor_copy(ids, mi[:, :, 0:2]))
                iota_e = iota_r[:, 0:NEXP].unsqueeze(1).to_broadcast(each)
                for c in range(2):
                    last = dve.tensor_tensor(oh[:, c], ids[:, :, c:c + 1].to_broadcast(each), iota_e, ALU.is_equal)
                link(last)
                link(dve.tensor_tensor(member, oh[:, 0], oh[:, 1], ALU.add))
                dve.tensor_tensor(member, member, ok.unsqueeze(2).to_broadcast(each), ALU.mult).then_inc(s_mem, 1)
                dve.wait_ge(s_th, 1)
                link(dve.tensor_scalar(w12[:, 1, :], th, 0.5, 0.5, ALU.mult, ALU.add))
                link(dve.tensor_scalar(w12[:, 0, :], w12[:, 1, :], -1.0, 1.0, ALU.mult, ALU.add))
                for c in range(2):
                    last = dve.tensor_tensor(prod[:, c], oh[:, c], w12[:, c, :].unsqueeze(2).to_broadcast(each),
                                             ALU.mult)
                link(last)
                dve.tensor_tensor(xs[:, 0:NT, D:XW], prod[:, 0], prod[:, 1], ALU.add).then_inc(s_wd, 1)
                dve.wait_ge(s_wd, 1)
                dve.wait_ge(s_rk, 1)
                totals = ps[:, TT, 0:QCOLS].rearrange("p (t e) -> p e t", e=NEXP)
                link(dve.memset(pos[:, 0:4, :], 0.0))
                zeros = pos[:, 0:4, :].rearrange("p t e -> p (t e)")[:, 0:NT]
                for e in range(NEXP):
                    last = dve.tensor_tensor_scan(cum[:, e, :], totals[:, e, :], zeros, 0.0, ALU.add, ALU.add)
                link(last)
                link(dve.tensor_tensor(pos, cum.rearrange("p e t -> p t e"), by_tile(ps[:, TT, 0:QCOLS]),
                                       ALU.subtract))
                link(dve.tensor_tensor(pos, pos, by_tile(ps[:, TR, 0:QCOLS]), ALU.add))
                link(dve.scalar_tensor_tensor(out=pos, in0=iota_e, scalar=float(CAP), in1=pos, op0=ALU.mult,
                                              op1=ALU.add))
                for c in range(2):
                    last = dve.tensor_tensor(prod[:, c], oh[:, c], pos, ALU.mult)
                link(last)
                for c in range(2):
                    last = dve.tensor_reduce(slot_f[:, c, :], prod[:, c], AX.X, ALU.add)
                link(last)
                link(dve.tensor_tensor(slot_f, slot_f, nowhere.unsqueeze(1).to_broadcast([P, 2, NT]), ALU.add))
                link(dve.tensor_copy(slot_i, slot_f))
                dve.tensor_scalar(half_i[:, 0], slot_i, P - 1, None, ALU.bitwise_and)
                link(dve.tensor_scalar(half_i[:, 1], slot_i, 7, None, ALU.arith_shift_right))
                dve.tensor_copy(half_f, half_i).then_inc(s_hf, 1)
                dve.wait_ge(s_hf, 1)
                dve.wait_ge(s_z, 2)

                def one_hots(n, turn):
                    dve.tensor_scalar(oh_row[:, turn * 2, :], iota_q[:, 0:P], col(half_f[:, 0, 0], n), None,
                                      ALU.is_equal)
                    for c in range(2):
                        dve.tensor_scalar(oh_col[:, turn * 2 + c, :], iota_q[:, :], col(half_f[:, 1, c], n),
                                          col(code, n), ALU.is_equal, ALU.mult).then_inc(s_oq, 1)
                for it in turns(dve, NT // 2):
                    for q in range(2):
                        if it is not FIRST:
                            dve.wait_ge(s_qm, it * 2 + q - 1)
                        one_hots(it * 2 + q, q)
                dve.wait_ge(s_qm, NT - 2)
                one_hots(NT - 1, 0)
                link(dve.tensor_scalar(tl[:, 0, :], cum[0:1, :, NT - 1], float(P - 1), None, ALU.add))
                link(dve.tensor_copy(tl_i[:, :], tl[:, 0, :]))
                link(dve.tensor_scalar(tl_i[:, :], tl_i[:, :], 7, None, ALU.arith_shift_right))
                link(dve.tensor_copy(tl[:, 1, :], tl_i[:, :]))
                link(dve.memset(tl[:, 3, :], 0.0))
                link(dve.tensor_tensor_scan(tl[:, 2, :], tl[:, 1, :], tl[:, 3, :], 0.0, ALU.add, ALU.add))
                shape = [1, MOE_TILES, NEXP - 1]
                link(dve.tensor_tensor(m_cmp[0:1], tl[:, 2:3, 0:NEXP - 1].to_broadcast(shape),
                                       iota_r[0:1, 0:MOE_TILES].unsqueeze(2).to_broadcast(shape), ALU.is_le))
                link(dve.tensor_tensor(m_mul[0:1], m_cmp[0:1],
                                       tl[:, 1:2, 0:NEXP - 1].to_broadcast(shape), ALU.mult))
                link(dve.memset(tab_e[:, MOE_TILES:], 0.0))
                link(dve.tensor_reduce(tab_e[:, 0:MOE_TILES], m_cmp[0:1], AX.X, ALU.add))
                link(dve.tensor_reduce(tab_f[:, 0, :], m_mul[0:1], AX.X, ALU.add))
                link(dve.tensor_tensor(tab_f[:, 0, :], iota_r[0:1, 0:MOE_TILES], tab_f[:, 0, :], ALU.subtract))
                link(dve.scalar_tensor_tensor(out=tab_f[:, 1, :], in0=tab_e[:, 0:MOE_TILES], scalar=float(NT),
                                              in1=tab_f[:, 0, :], op0=ALU.mult, op1=ALU.add))
                link(dve.tensor_copy(c_tab[:, :], tab_f[:, 1, :]))
                link(dve.tensor_copy(pack_f[:, :], tab_e[:, RING::RING]))
                for j in reversed(range(RING)):
                    link(dve.scalar_tensor_tensor(out=pack_f[:, :], in0=pack_f[:, :], scalar=float(NEXP),
                                                  in1=tab_e[:, j:MOE_TILES:RING], op0=ALU.mult, op1=ALU.add))
                link(dve.tensor_copy(packs[:, :], pack_f[:, :]))
                dve.wait_ge(s_qd, 1)
                size = cum.rearrange("p e t -> p (e t)")
                link(dve.tensor_copy(found, ps[:, TQ, 0:QCOLS]))
                link(dve.tensor_scalar(negative, found, 0.0, float(SIGN), ALU.is_lt, ALU.mult))
                link(dve.tensor_scalar(empty, found, 0.0, NOWHERE, ALU.is_equal, ALU.mult))
                link(dve.scalar_tensor_tensor(out=size, in0=found, scalar=-1.0, in1=found, op0=ALU.mult,
                                              op1=ALU.max))
                link(dve.tensor_tensor(negative, negative, empty, ALU.add))
                link(dve.scalar_tensor_tensor(out=negative, in0=size, scalar=-1.0, in1=negative, op0=ALU.add,
                                              op1=ALU.add))
                link(dve.tensor_copy(q_tok[:, 0:QCOLS], negative))
                link(dve.memset(q_tok[:, QCOLS:], int(NOWHERE)))

            @block.tensor
            def _(pe):
                for s in (s_ntp, s_ny, s_gu):
                    pe.sem_inc(s, CREDIT)

                def turn(n, q):
                    pe.wait_ge(s_ngm, n + 1 + NG)
                    pe.wait_ge(s_nT, n - 1 + CREDIT)
                    for c in range(KD):
                        last = pe.transpose(ps[:, 6 + q, c * P:(c + 1) * P], ngm[:, q, c * P:(c + 1) * P],
                                            ident[:, :])
                    last.then_inc(s_ntp, 1)

                def product(n, q):
                    pe.wait_ge(s_nT, n + 1 + CREDIT)
                    pe.wait_ge(s_x1, n - 1 + CREDIT)
                    for c in range(KD):
                        last = pe.matmul(ps[:, 4 + q, 0:D], xT[:, q, c, :], wnT[:, c, :],
                                         start=(c == 0), stop=(c == KD - 1))
                    last.then_inc(s_ny, 1)
                turn(0, 0)
                with pe.Fori(0, NT // 2) as it:
                    for q in range(2):
                        turn(it * 2 + q + 1, 1 - q)
                        product(it * 2 + q, q)
                product(NT - 1, 0)

                def turn2(n, u):
                    pe.wait_ge(s_x2, n + 1)
                    pe.wait_ge(s_x2T, n + 1)
                    for c in range(KD):
                        last = pe.transpose(ps[:, 4 + u, c * P:(c + 1) * P], x2_ring[:, u, c * P:(c + 1) * P],
                                            ident[:, :])
                    last.then_inc(s_x2p, 1)

                def gate(n, u):
                    pe.wait_ge(s_x2T, n + 1 + NG)
                    for c in range(KD):
                        last = pe.matmul(ps[:, TG, bass.ds(n * NEXP, NEXP)], xT[:, u % 2, c, :], wg_s[:, c, :],
                                         start=(c == 0), stop=(c == KD - 1))
                    last.then_inc(s_gu, 1)
                pe.wait_ge(s_x1, NT + CREDIT)
                turn2(0, 0)
                with pe.Fori(0, NT // NG) as it:
                    for u in range(NG):
                        turn2(it * NG + u + 1, (u + 1) % NG)
                        gate(it * NG + u, u)
                gate(NT - 1, 0)
                pe.wait_ge(s_z, 1)
                pe.matmul(ps[:, TQ, 0:QCOLS], zeros_q[:, 0:P], zeros_q, start=True, stop=False)
                pe.wait_ge(s_mem, 1)
                pe.matmul(ps[:, TR, 0:QCOLS], tri_lt[:, :], flat(member), start=True, stop=True)
                pe.matmul(ps[:, TT, 0:QCOLS], ones[:, :], flat(member), start=True, stop=True).then_inc(s_rk, 1)

                def put(n, turn):
                    for c in range(2):
                        b = turn * 2 + c
                        pe.wait_ge(s_oq, n * 2 + c + 1)
                        if c == 1:
                            pe.wait_ge(s_or, n + 1)
                        last = pe.matmul(ps[:, TQ, 0:QCOLS], oh_row[:, b, :], oh_col[:, b, :],
                                         start=False, stop=False)
                    last.then_inc(s_qm, 1)
                with pe.Fori(0, NT // 2) as it:
                    for q in range(2):
                        put(it * 2 + q, q)
                put(NT - 1, 0)
                pe.wait_ge(s_z, 1)
                pe.matmul(ps[:, TQ, 0:QCOLS], zeros_q[:, 0:P], zeros_q, start=False, stop=True).then_inc(s_qd, 1)

        s_tok = sem("tokens_ready")
        s_xg, s_tok0 = sems("tokens_gathered", RING), sem("token_buffers_cleared")
        s_xp, s_xh, s_xe = sem("tokens_transposed"), sem("tokensT_high"), sem("tokensT_ready")
        s_hp, s_pre, s_gel = sem("hidden_product"), sem("hidden_biased"), sem("hidden_ready")
        s_gp, s_hh, s_hl = sem("hidden_transposed"), sem("hiddenT_high"), sem("hiddenT_ready")
        s_w2 = sem("last_w2_loaded")
        s_yp, s_yb, s_yw = sem("out_product"), sem("out_biased"), sem("out_weighted")
        s_add, s_back = sems("out_added", 2), sem("out_tokens_ready")
        at_xs = [0]
        xs_flat = xs[:, :, :].rearrange("p t d -> p (t d)")

        def over_x(*shape, dt=F32):
            n = 1
            for s in shape:
                n *= s
            v = xs_flat[:, at_xs[0]:at_xs[0] + n]
            at_xs[0] += n
            if dt != F32:
                v = v.bitcast(dt)
            if len(shape) == 2:
                v = v.rearrange("p (a b) -> p a b", b=shape[1])
            elif len(shape) == 3:
                v = v.rearrange("p (a b c) -> p a b c", b=shape[1], c=shape[2])
            return v

        toks = over_x(RING, 2, dt=I32)
        back = over_x(2, 2, dt=I32)
        tg = over_x(RING, XW)
        tgT = over_x(2 * KD * P, dt=F16)\
            .rearrange("p (q a c t) -> p q a c t", q=2, a=2, c=KD)
        pre = over_x(HID)
        hid = over_x(HID)
        hidT = over_x(KH * P, dt=F16).rearrange("p (a c t) -> p a c t", a=2, c=KH)
        yb = over_x(2, D)
        yw = over_x(2, D)
        assert at_xs[0] <= (NT + 1) * XW
        XP, HP, GP, YP = (0, 7), 1, 3, 5
        HALF = KH // 2

        with nc.Block() as block:
            @block.gpsimd
            def _(pool):
                last_tok = pool.to_reg(N - 1)
                pool.memset(tg[:, :, :], 0.0).then_inc(s_tok0, 1)
                pool.wait_ge(s_tok0, 1)

                def gather(it, n, u):
                    c = pool.value_load(c_tab[0:1, bass.ds(n, 1)], min_val=0, max_val=QCOLS + MOE_TILES - 1)
                    pool.tensor_copy(toks[:, u, 0:1], col(q_tok, c)).then_inc(s_tok, 1)
                    pool.wait_ge(s_tok, n + 1)
                    settle(pool)
                    pool.indirect_dma_start(tg[:, u, :], None, x2_dram,
                                            bass.IndirectOffsetOnAxis(toks[:, u, 0:1], 0),
                                            bounds_check=last_tok, oob_is_err=False).then_inc(s_xg[u], 16)

                def add_rows(it, n, u):
                    pool.wait_ge(s_add[1 - u % 2], it * 32 + (u + 1) // 2 * 16)
                    pool.wait_ge(s_xg[u], it * 16 + 16)
                    settle(pool)
                    pool.tensor_copy(back[:, u % 2, 0:1], toks[:, u, 0:1]).then_inc(s_back, 1)
                    pool.wait_ge(s_back, n + 1)
                    pool.wait_ge(s_yw, n + 1 + CREDIT)
                    settle(pool)
                    pool.indirect_dma_start(out, bass.IndirectOffsetOnAxis(back[:, u % 2, 0:1], 0),
                                            yw[:, u % 2, :], None, bounds_check=last_tok, oob_is_err=False,
                                            compute_op=ALU.add).then_inc(s_add[u % 2], 16)
                for u in range(RING):
                    gather(0, u, u)
                for it in turns(pool, TURNS - 1):
                    for u in range(RING):
                        add_rows(it, it * RING + u, u)
                        gather(it + 1, it * RING + u + RING, u)
                for u in range(RING):
                    add_rows(TURNS - 1, MOE_TILES - RING + u, u)
                for q in range(2):
                    pool.wait_ge(s_add[q], MOE_TILES // 2 * 16)

            def pipeline(eng, tokens, turn_round, hidden, output):
                ahead = eng.alloc_register("experts_ahead")
                eng.reg_load(ahead, packs[0:1, 0:1])

                def turn(it, last=False):
                    pack = eng.snap(ahead, min_val=0, max_val=NEXP ** (RING + 1) - 1)
                    e = [(pack >> (3 * j)) & (NEXP - 1) for j in range(RING + 1)]
                    for u in range(RING):
                        n = it * RING + u
                        turn_round(n, e[u])
                        if not last or u + 2 < RING:
                            tokens(it, n + 2, u + 2)
                        if not last or u + 1 < RING:
                            hidden(n + 1, (u + 1) % 2, e[u + 1])
                        if not last and u == RING - 1:
                            eng.reg_load(ahead, packs[0:1, bass.ds(it + 1, 1)])
                        output(it, n, u, e[u])
                for it in turns(eng, TURNS - 1):
                    turn(it)
                turn(TURNS - 1, True)

            def first_expert(eng):
                return eng.value_load(packs[0:1, 0:1], min_val=0, max_val=NEXP ** (RING + 1) - 1) & (NEXP - 1)

            @block.scalar
            def _(act):
                act.activation(pre[:, 0:1], ones[:, 0:1], ACT.Gelu)
                act.wait_ge(s_xg[1], 16)
                act.dma_start(w2_p[:, NEXP - LATE:], w2_split[NEXP - LATE:].rearrange("e p k -> p e k"))\
                   .then_inc(s_w2, 16)
                act.sem_inc(s_yw, CREDIT)

                def high_x(it, n, u):
                    act.wait_ge(s_xp, n + 1 + RING)
                    act.wait_ge(s_hp, 2 * (n - 1 + CREDIT))
                    act.activation(tgT[:, u % 2, 0].rearrange("p c t -> p (c t)"), ps[:, XP[u % 2], 0:D], ACT.Copy,
                                   scale=XSCALE).then_inc(s_xh, 1)

                def gelu(n, q, e):
                    for half in range(2):
                        act.wait_ge(s_pre, 2 * n + half + 1)
                        if half == 0:
                            act.wait_ge(s_gp, 2 * n)
                        act.activation(hid[:, half * 512:(half + 1) * 512], pre[:, half * 512:(half + 1) * 512],
                                       ACT.Gelu).then_inc(s_gel, 1)

                def high_h(n, e):
                    for half in range(2):
                        act.wait_ge(s_gp, 2 * n + half + 1)
                        if half == 0:
                            act.wait_ge(s_yp, n)
                        settle(act)
                        act.activation(hidT[:, 0, half * HALF:half * HALF + HALF, :].rearrange("p c t -> p (c t)"),
                                       ps[:, GP + half, :], ACT.Copy, scale=col(sh, e)).then_inc(s_hh, 1)

                def weigh(it, n, u, e):
                    act.wait_ge(s_yb, n + 1)
                    act.wait_ge(s_add[u % 2], it * 32 + u // 2 * 16)
                    settle(act)
                    act.activation(yw[:, u % 2, :], yb[:, u % 2, :], ACT.Copy,
                                   scale=col(tg[:, u], D + e)).then_inc(s_yw, 1)
                high_x(0, 0, 0)
                high_x(0, 1, 1)
                gelu(0, 0, None)
                pipeline(act, high_x, high_h, gelu, weigh)

            @block.vector
            def _(dve):
                dve.sem_inc(s_xe, CREDIT)

                def low_x(it, n, u):
                    dve.wait_ge(s_xh, n + 1)
                    dve.scalar_tensor_tensor(out=tgT[:, u % 2, 1].rearrange("p c t -> p (c t)"),
                                             in0=ps[:, XP[u % 2], 0:D], scalar=XSCALE,
                                             in1=tgT[:, u % 2, 0].rearrange("p c t -> p (c t)"),
                                             op0=ALU.mult, op1=ALU.subtract).then_inc(s_xe, 1)

                def bias_h(n, q, e):
                    for half in range(2):
                        dve.wait_ge(s_hp, 2 * (n + CREDIT) + half + 1)
                        dve.wait_ge(s_gel, 2 * n)
                        b = b1_s[:, bass.ds(e, 1), half * 512:(half + 1) * 512].rearrange("p a h -> p (a h)")
                        dve.scalar_tensor_tensor(out=pre[:, half * 512:(half + 1) * 512], in0=ps[:, HP + half, :],
                                                 scalar=col(k1, e), in1=b, op0=ALU.mult, op1=ALU.add)\
                           .then_inc(s_pre, 1)

                def low_h(n, e):
                    for half in range(2):
                        dve.wait_ge(s_hh, 2 * n + half + 1)
                        part = [hidT[:, a, half * HALF:half * HALF + HALF, :].rearrange("p c t -> p (c t)")
                                for a in range(2)]
                        dve.scalar_tensor_tensor(out=part[1], in0=ps[:, GP + half, :], scalar=col(sh, e),
                                                 in1=part[0], op0=ALU.mult, op1=ALU.subtract).then_inc(s_hl, 1)

                def bias_y(it, n, u, e):
                    dve.wait_ge(s_yp, n + 1)
                    dve.wait_ge(s_yw, n - 1 + CREDIT)
                    dve.scalar_tensor_tensor(out=yb[:, u % 2, :], in0=ps[:, YP + u % 2, 0:D], scalar=col(k2, e),
                                             in1=b2_s[:, bass.ds(e, 1), :].rearrange("p a d -> p (a d)"),
                                             op0=ALU.mult, op1=ALU.add).then_inc(s_yb, 1)
                low_x(0, 0, 0)
                low_x(0, 1, 1)
                bias_h(0, 0, first_expert(dve))
                pipeline(dve, low_x, low_h, bias_h, bias_y)

            @block.tensor
            def _(pe):
                pe.sem_inc(s_xp, RING)
                pe.sem_inc(s_hp, 2 * CREDIT)

                def turn_x(it, n, u):
                    pe.wait_ge(s_xg[u % RING], (it + u // RING) * 16 + 16)
                    pe.wait_ge(s_xe, n - 1 + CREDIT)
                    for c in range(KD):
                        last = pe.transpose(ps[:, XP[u % 2], c * P:(c + 1) * P],
                                            tg[:, u % RING, c * P:(c + 1) * P], ident[:, :])
                    last.then_inc(s_xp, 1)

                PASSES = ((0, 0), (0, 1), (1, 0))

                def up(n, q, e):
                    pe.wait_ge(s_xe, n + 1 + CREDIT)
                    pe.wait_ge(s_pre, 2 * n)
                    for half in range(2):
                        for c in range(KD):
                            for a, b in PASSES:
                                w = w1_p[:, bass.ds(e, 1), b, c * HID + half * 512:c * HID + (half + 1) * 512]
                                last = pe.matmul(ps[:, HP + half, :], tgT[:, q, a, c, :],
                                                 w.rearrange("p a h -> p (a h)"), start=(c + a + b == 0),
                                                 stop=(c == KD - 1 and (a, b) == PASSES[-1]))
                        last.then_inc(s_hp, 1)

                def turn_h(n, e):
                    for half in range(2):
                        pe.wait_ge(s_gel, 2 * n + half + 1)
                        for c in range(HALF):
                            at = half * HALF + c
                            last = pe.transpose(ps[:, GP + half, c * P:(c + 1) * P], hid[:, at * P:(at + 1) * P],
                                                ident[:, :])
                        last.then_inc(s_gp, 1)

                def down(it, n, u, e):
                    if it is FIRST and u == 0:
                        pe.wait_ge(s_w2, 16)
                    pe.wait_ge(s_yw, n - 1 + CREDIT)
                    for c in range(KH):
                        if c % HALF == 0:
                            pe.wait_ge(s_hl, 2 * n + c // HALF + 1)
                        for a, b in PASSES:
                            w = w2_p[:, bass.ds(e, 1), b * WCH + c * D:b * WCH + (c + 1) * D]
                            last = pe.matmul(ps[:, YP + u % 2, 0:D], hidT[:, a, c, :], w.rearrange("p a d -> p (a d)"),
                                             start=(c + a + b == 0), stop=(c == KH - 1 and (a, b) == PASSES[-1]))
                    last.then_inc(s_yp, 1)
                turn_x(0, 0, 0)
                turn_x(0, 1, 1)
                up(0, 0, first_expert(pe))
                pipeline(pe, turn_x, turn_h, up, down)


_INS = ['x', 'src', 'dst', 'edge_weight1', 'L0_gnn_W_pool', 'L0_gnn_b_pool', 'L0_gnn_W_self', 'L0_gnn_b_self',
        'L0_gnn_W_neigh', 'L0_gnn_b_neigh', 'L0_ffn_Wg', 'L0_ffn_bg', 'L0_ffn_W1', 'L0_ffn_b1', 'L0_ffn_W2',
        'L0_ffn_b2']


def kernel(**inputs):
    import numpy as _np
    import concourse.bacc as _bacc
    from concourse import mybir as _mybir
    from concourse.bass_utils import run_bass_kernel_spmd as _run

    nc = _bacc.Bacc("TRN2", target_bir_lowering=False, num_devices=1)
    arrays, args = {}, []
    for name in _INS:
        a = _np.ascontiguousarray(inputs[name])
        arrays[f"in_{name}_dram"] = a
        args.append(nc.dram_tensor(f"in_{name}_dram", a.shape, _mybir.dt.from_np(a.dtype), kind="ExternalInput").ap())
    args.append(nc.dram_tensor("out_dram", (N, D), F32, kind="ExternalOutput").ap())
    gnn_moe(nc, *args)
    r = _run(nc, [arrays], core_ids=[0])
    return r.results[0]["out_dram"]
```
